# Optimizing a Trainium2 kernel written in Bass

```python
import numpy as np
import jax
import jax.numpy as jnp

def _softmax(x, axis=-1):
    return jax.nn.softmax(x, axis=axis)

def _gelu(x):
    return jax.nn.gelu(x, approximate=True)

def _silu(x):
    return jax.nn.silu(x)

def _sigmoid(x):
    return jax.nn.sigmoid(x)

def _layernorm(x, axis=-1, eps=1e-05):
    m = jnp.mean(x, axis=axis, keepdims=True)
    v = jnp.var(x, axis=axis, keepdims=True)
    return (x - m) / jnp.sqrt(v + eps)

def _scatter_add(tgt, idx, src, axis=0):
    return tgt.at[idx].add(src)

def _segment_sum(src, seg, n):
    return jax.ops.segment_sum(src, seg, n)
kernel_name = 'mk_sandwich_d1_jaxref_r8_d1358e'

def setup_inputs(seed: int=0):
    np.random.seed(seed)
    _w = jnp.asarray

    def _L0_attn_setup():
        import jax, jax.numpy as jnp
        import numpy as np
        from jax.scipy.linalg import solve_triangular
        H = 256
        NK = 16
        NV = 32
        DK = 128
        DV = 128
        KCONV = 4
        CHUNK = 64
        EPS = 1e-06
        KD = NK * DK
        VD = NV * DV
        CONV_DIM = 2 * KD + VD

        def _l2norm(x, eps=1e-06):
            return x * jax.lax.rsqrt(jnp.sum(x * x, axis=-1, keepdims=True) + eps)

        def _chunk_gated_delta_rule(q, k, v, g, beta):
            B, S, Hh, _ = q.shape
            q = _l2norm(q)
            k = _l2norm(k)
            q = q.transpose(0, 2, 1, 3).astype(jnp.float32) * DK ** (-0.5)
            k = k.transpose(0, 2, 1, 3).astype(jnp.float32)
            v = v.transpose(0, 2, 1, 3).astype(jnp.float32)
            g = g.transpose(0, 2, 1).astype(jnp.float32)
            beta = beta.transpose(0, 2, 1).astype(jnp.float32)
            N = S // CHUNK
            ch = lambda x: x.reshape(B, Hh, N, CHUNK, x.shape[-1])
            q, k, v = (ch(q), ch(k), ch(v))
            g = g.reshape(B, Hh, N, CHUNK)
            beta = beta.reshape(B, Hh, N, CHUNK)
            v_beta = v * beta[..., None]
            k_beta = k * beta[..., None]
            g = jnp.cumsum(g, axis=-1)
            dg = g[..., :, None] - g[..., None, :]
            decay = jnp.tril(jnp.exp(jnp.tril(dg)))
            M = -jnp.tril(jnp.einsum('bhnik,bhnjk->bhnij', k_beta, k) * decay, k=-1)
            eye = jnp.eye(CHUNK, dtype=jnp.float32)
            T = solve_triangular(eye - M, jnp.broadcast_to(eye, M.shape), lower=True)
            v_new = jnp.einsum('bhnij,bhnjd->bhnid', T, v_beta)
            k_cumdecay = jnp.einsum('bhnij,bhnjd->bhnid', T, k_beta * jnp.exp(g)[..., None])
            lower_incl = jnp.tril(jnp.ones((CHUNK, CHUNK), bool))

            def step(state, inp):
                q_i, k_i, v_i, kcd_i, g_i, dm_i = inp
                attn = jnp.where(lower_incl, jnp.einsum('bhik,bhjk->bhij', q_i, k_i) * dm_i, 0.0)
                v_prime = jnp.einsum('bhik,bhkv->bhiv', kcd_i, state)
                vn = v_i - v_prime
                inter = jnp.einsum('bhik,bhkv->bhiv', q_i * jnp.exp(g_i)[..., None], state)
                out = inter + jnp.einsum('bhij,bhjv->bhiv', attn, vn)
                g_last = g_i[..., -1]
                state = state * jnp.exp(g_last)[..., None, None] + jnp.einsum('bhck,bhcv->bhkv', k_i * jnp.exp(g_last[..., None] - g_i)[..., None], vn)
                return (state, out)
            xs = tuple((jnp.moveaxis(x, 2, 0) for x in (q, k, v_new, k_cumdecay, g, decay)))
            state0 = jnp.zeros((B, Hh, DK, DV), jnp.float32)
            _, outs = jax.lax.scan(step, state0, xs)
            out = jnp.moveaxis(outs, 0, 2).reshape(B, Hh, S, DV)
            return out.transpose(0, 2, 1, 3)
        key = jax.random.key(seed)
        ks = jax.random.split(key, 8)
        B, S = (2, 256)
        return {'hidden_states': jax.random.normal(ks[0], (B, S, H), jnp.float32), 'W_qkvz': jax.random.normal(ks[1], (H, 2 * KD + 2 * VD), jnp.float32) * 0.02, 'W_ba': jax.random.normal(ks[2], (H, 2 * NV), jnp.float32) * 0.02, 'conv_weight': jax.random.normal(ks[3], (CONV_DIM, KCONV), jnp.float32) * 0.1, 'A_log': jax.random.normal(ks[4], (NV,), jnp.float32) * 0.1, 'dt_bias': jax.random.normal(ks[5], (NV,), jnp.float32) * 0.1, 'norm_weight': jnp.ones((DV,), jnp.float32), 'W_out': jax.random.normal(ks[6], (VD, H), jnp.float32) * 0.02}
    _L0_attn_in = _L0_attn_setup()

    def _L0_ffn_setup():
        import jax, jax.numpy as jnp
        import numpy as np
        B, S, D = (2, 256, 256)
        E, TOP_K, H = (8, 2, 128)
        HS = 256
        key = jax.random.key(seed)
        ks = jax.random.split(key, 8)
        sc_d = 1.0 / np.sqrt(D)
        sc_h = 1.0 / np.sqrt(H)
        sc_hs = 1.0 / np.sqrt(HS)
        return {'hidden_states': jax.random.normal(ks[0], (B, S, D), jnp.float32), 'router_w': jax.random.normal(ks[1], (D, E), jnp.float32) * sc_d, 'w_gate': jax.random.normal(ks[2], (E, D, H), jnp.float32) * sc_d, 'w_up': jax.random.normal(ks[3], (E, D, H), jnp.float32) * sc_d, 'w_down': jax.random.normal(ks[4], (E, H, D), jnp.float32) * sc_h, 'sw_gate': jax.random.normal(ks[5], (D, HS), jnp.float32) * sc_d, 'sw_up': jax.random.normal(ks[6], (D, HS), jnp.float32) * sc_d, 'sw_down': jax.random.normal(ks[7], (HS, D), jnp.float32) * sc_hs}
    _L0_ffn_in = _L0_ffn_setup()
    _d = {'L0_attn_hidden_states': _L0_attn_in['hidden_states'], 'L0_attn_W_qkvz': _L0_attn_in['W_qkvz'], 'L0_attn_W_ba': _L0_attn_in['W_ba'], 'L0_attn_conv_weight': _L0_attn_in['conv_weight'], 'L0_attn_A_log': _L0_attn_in['A_log'], 'L0_attn_dt_bias': _L0_attn_in['dt_bias'], 'L0_attn_norm_weight': _L0_attn_in['norm_weight'], 'L0_attn_W_out': _L0_attn_in['W_out'], 'L0_ffn_router_w': _L0_ffn_in['router_w'], 'L0_ffn_w_gate': _L0_ffn_in['w_gate'], 'L0_ffn_w_up': _L0_ffn_in['w_up'], 'L0_ffn_w_down': _L0_ffn_in['w_down'], 'L0_ffn_sw_gate': _L0_ffn_in['sw_gate'], 'L0_ffn_sw_up': _L0_ffn_in['sw_up'], 'L0_ffn_sw_down': _L0_ffn_in['sw_down']}
    _x0 = _d['L0_attn_hidden_states']
    _d['L0_attn_hidden_states'] = jax.random.normal(jax.random.fold_in(jax.random.key(seed), 1), (2, 512, 256), dtype=_x0.dtype)
    del _x0
    return _d

def reference(L0_attn_hidden_states, L0_attn_W_qkvz, L0_attn_W_ba, L0_attn_conv_weight, L0_attn_A_log, L0_attn_dt_bias, L0_attn_norm_weight, L0_attn_W_out, L0_ffn_router_w, L0_ffn_w_gate, L0_ffn_w_up, L0_ffn_w_down, L0_ffn_sw_gate, L0_ffn_sw_up, L0_ffn_sw_down):

    def _L0_attn_ref(hidden_states, W_qkvz, W_ba, conv_weight, A_log, dt_bias, norm_weight, W_out):
        import jax, jax.numpy as jnp
        import numpy as np
        from jax.scipy.linalg import solve_triangular
        H = 256
        NK = 16
        NV = 32
        DK = 128
        DV = 128
        KCONV = 4
        CHUNK = 64
        EPS = 1e-06
        KD = NK * DK
        VD = NV * DV
        CONV_DIM = 2 * KD + VD

        def _l2norm(x, eps=1e-06):
            return x * jax.lax.rsqrt(jnp.sum(x * x, axis=-1, keepdims=True) + eps)

        def _chunk_gated_delta_rule(q, k, v, g, beta):
            B, S, Hh, _ = q.shape
            q = _l2norm(q)
            k = _l2norm(k)
            q = q.transpose(0, 2, 1, 3).astype(jnp.float32) * DK ** (-0.5)
            k = k.transpose(0, 2, 1, 3).astype(jnp.float32)
            v = v.transpose(0, 2, 1, 3).astype(jnp.float32)
            g = g.transpose(0, 2, 1).astype(jnp.float32)
            beta = beta.transpose(0, 2, 1).astype(jnp.float32)
            N = S // CHUNK
            ch = lambda x: x.reshape(B, Hh, N, CHUNK, x.shape[-1])
            q, k, v = (ch(q), ch(k), ch(v))
            g = g.reshape(B, Hh, N, CHUNK)
            beta = beta.reshape(B, Hh, N, CHUNK)
            v_beta = v * beta[..., None]
            k_beta = k * beta[..., None]
            g = jnp.cumsum(g, axis=-1)
            dg = g[..., :, None] - g[..., None, :]
            decay = jnp.tril(jnp.exp(jnp.tril(dg)))
            M = -jnp.tril(jnp.einsum('bhnik,bhnjk->bhnij', k_beta, k) * decay, k=-1)
            eye = jnp.eye(CHUNK, dtype=jnp.float32)
            T = solve_triangular(eye - M, jnp.broadcast_to(eye, M.shape), lower=True)
            v_new = jnp.einsum('bhnij,bhnjd->bhnid', T, v_beta)
            k_cumdecay = jnp.einsum('bhnij,bhnjd->bhnid', T, k_beta * jnp.exp(g)[..., None])
            lower_incl = jnp.tril(jnp.ones((CHUNK, CHUNK), bool))

            def step(state, inp):
                q_i, k_i, v_i, kcd_i, g_i, dm_i = inp
                attn = jnp.where(lower_incl, jnp.einsum('bhik,bhjk->bhij', q_i, k_i) * dm_i, 0.0)
                v_prime = jnp.einsum('bhik,bhkv->bhiv', kcd_i, state)
                vn = v_i - v_prime
                inter = jnp.einsum('bhik,bhkv->bhiv', q_i * jnp.exp(g_i)[..., None], state)
                out = inter + jnp.einsum('bhij,bhjv->bhiv', attn, vn)
                g_last = g_i[..., -1]
                state = state * jnp.exp(g_last)[..., None, None] + jnp.einsum('bhck,bhcv->bhkv', k_i * jnp.exp(g_last[..., None] - g_i)[..., None], vn)
                return (state, out)
            xs = tuple((jnp.moveaxis(x, 2, 0) for x in (q, k, v_new, k_cumdecay, g, decay)))
            state0 = jnp.zeros((B, Hh, DK, DV), jnp.float32)
            _, outs = jax.lax.scan(step, state0, xs)
            out = jnp.moveaxis(outs, 0, 2).reshape(B, Hh, S, DV)
            return out.transpose(0, 2, 1, 3)
        B, S, _ = hidden_states.shape
        R = NV // NK
        qkvz = (hidden_states @ W_qkvz).reshape(B, S, NK, 2 * DK + 2 * R * DV)
        ba = (hidden_states @ W_ba).reshape(B, S, NK, 2 * R)
        q = qkvz[..., :DK]
        k = qkvz[..., DK:2 * DK]
        v = qkvz[..., 2 * DK:2 * DK + R * DV].reshape(B, S, NV, DV)
        z = qkvz[..., 2 * DK + R * DV:].reshape(B, S, NV, DV)
        b = ba[..., :R].reshape(B, S, NV)
        a = ba[..., R:].reshape(B, S, NV)
        mixed = jnp.concatenate([q.reshape(B, S, -1), k.reshape(B, S, -1), v.reshape(B, S, -1)], -1)
        xp = jnp.pad(mixed, ((0, 0), (KCONV - 1, 0), (0, 0)))
        conv = sum((xp[:, j:j + S, :] * conv_weight[:, j] for j in range(KCONV)))
        mixed = jax.nn.silu(conv)
        q = mixed[..., :KD].reshape(B, S, NK, DK)
        k = mixed[..., KD:2 * KD].reshape(B, S, NK, DK)
        v = mixed[..., 2 * KD:].reshape(B, S, NV, DV)
        beta = jax.nn.sigmoid(b)
        g = -jnp.exp(A_log) * jax.nn.softplus(a + dt_bias)
        q = jnp.repeat(q, R, axis=2)
        k = jnp.repeat(k, R, axis=2)
        core = _chunk_gated_delta_rule(q, k, v, g, beta)
        x = core * jax.nn.silu(z.astype(jnp.float32))
        x = x * jax.lax.rsqrt(jnp.mean(x * x, axis=-1, keepdims=True) + EPS) * norm_weight
        return x.reshape(B, S, VD) @ W_out

    def _L0_ffn_ref(hidden_states, router_w, w_gate, w_up, w_down, sw_gate, sw_up, sw_down):
        import jax, jax.numpy as jnp
        import numpy as np
        B, S, D = (2, 256, 256)
        E, TOP_K, H = (8, 2, 128)
        HS = 256
        b, s, d = hidden_states.shape
        x = hidden_states.reshape(-1, d)
        T = x.shape[0]
        logits = x @ router_w
        probs = jax.nn.softmax(logits, axis=-1)
        topk_w, topk_idx = jax.lax.top_k(probs, TOP_K)
        topk_w = topk_w / jnp.sum(topk_w, axis=-1, keepdims=True)
        g = jnp.einsum('td,edh->teh', x, w_gate)
        u = jnp.einsum('td,edh->teh', x, w_up)
        h = jax.nn.silu(g) * u
        y = jnp.einsum('teh,ehd->ted', h, w_down)
        combine = jnp.zeros((T, E), dtype=x.dtype)
        combine = combine.at[jnp.arange(T)[:, None], topk_idx].add(topk_w)
        routed = jnp.einsum('te,ted->td', combine, y)
        sh = jax.nn.silu(hidden_states @ sw_gate) * (hidden_states @ sw_up)
        shared = sh @ sw_down
        return routed.reshape(b, s, d) + shared
    x = L0_attn_hidden_states
    x = x + _layernorm(_L0_attn_ref(_layernorm(x, axis=-1), L0_attn_W_qkvz, L0_attn_W_ba, L0_attn_conv_weight, L0_attn_A_log, L0_attn_dt_bias, L0_attn_norm_weight, L0_attn_W_out), axis=-1)
    x = x + _layernorm(_L0_ffn_ref(_layernorm(x, axis=-1), L0_ffn_router_w, L0_ffn_w_gate, L0_ffn_w_up, L0_ffn_w_down, L0_ffn_sw_gate, L0_ffn_sw_up, L0_ffn_sw_down), axis=-1)
    return x

_drawn_inputs = setup_inputs


def setup_inputs(seed=0):
    import zlib

    import numpy as np

    out = dict(_drawn_inputs(seed))
    spreads = {'L0_attn_norm_weight': (1.0, 0.2)}
    factors = {}
    for name, (base, spread) in spreads.items():
        noise = np.random.default_rng([zlib.crc32(name.encode()), seed]).standard_normal(out[name].shape)
        drawn = base * np.exp(spread * noise) if base else spread * noise
        out[name] = jnp.asarray(drawn.astype(out[name].dtype))
    for name, factor in factors.items():
        out[name] = (out[name] * factor).astype(out[name].dtype)
    return out
```

```python
from contextlib import ExitStack

import concourse.bass as bass
from concourse import mybir

F32 = mybir.dt.float32
ALU = mybir.AluOpType
ACT = mybir.ActivationFunctionType
AX = mybir.AxisListType

P = 128
NK, R, D = 16, 2, 128
NV = NK * R
B, S, H = 2, 512, 256
UNITS = B * S // P
CH = S // P
KT = H // P
M = UNITS * R
HW = 2 * D + 2 * R * D
TAPS = 4
BLK = 16
NB = P // BLK
E, FH, FS = 8, 128, 256
FW = E * FH + FS
FT = FW // P
LN_EPS, RMS_EPS, L2_EPS = 1e-5, 1e-6, 1e-6

PROJ, ZJ, TR, BACK, GRAM, JOBS_A = 0, 8, 12, 20, 24, 28
MERGE, RECUR, XT, OUTJ, JOBS_B = 0, 32, 60, 64, 68
S_G, S_NEG, S_EG, S_EGL, S_BETA, S_BK, S_NBETA, NSC = 0, 1, 2, 3, 4, 5, 6, 7


FCHUNKS = ((0, 512), (512, 512), (1024, 256))
PRO_NORM, PRO_ABS, PRO_G, PRO_DVE = 5, 13, 17, 22
PRO_POOL, PRO_ACT = 5 + 2 + 6 + E + 5 + 6, 6
DVE_STEPS, POOL_STEPS = 44, 6
EP_NORMS, EP_XN2, EP_EXP, EP_COMB = (5, 12, 45), 13, 19, 40
EP_LOADS = 16 * (8 + 2 + 1)


def recurrence_jobs():
    job, k = {}, RECUR
    for c in range(CH):
        for kind in ("state", "solve", "local", "update"):
            if (kind == "state" and c == 0) or (kind == "update" and c == CH - 1):
                continue
            for b in range(B):
                job[kind, b * CH + c] = k
                k += 1
    assert k == XT
    return job


RJ = recurrence_jobs()


class Steps:

    def __init__(self, eng, sem, base=0):
        self.eng, self.sem, self.base, self.k = eng, sem, base, 0

    def did(self, ins):
        ins.then_inc(self.sem, 1)
        self.k += 1
        return self.k

    def wait(self, k=None):
        self.eng.wait_ge(self.sem, self.base + (self.k if k is None else k))


def build(nc, x_in, w_qkvz, w_ba, conv_w, a_log, dt_bias, norm_w, w_out, router_w, w_gate, w_up, w_down,
          sw_gate, sw_up, sw_down, out, decay_rows, raw_blocks, inv_blocks):
    xf = x_in.rearrange("b (c p) h -> p (b c) h", p=P)
    of = out.rearrange("b (c p) h -> p (b c) h", p=P)

    with ExitStack() as ctx:
        def sb(name, shape):
            return ctx.enter_context(nc.sbuf_tensor(name, shape, F32))

        def sem(name):
            return ctx.enter_context(nc.semaphore(name))

        bank = [ctx.enter_context(nc.psum_tensor(f"bank{i}", [P, 512], F32)) for i in range(8)]
        ring_a, ring_b = bank[:4], bank[4:]

        ident = sb("ident", [P, P])
        upper = sb("upper", [P, P])
        merge16 = sb("merge16", [P, P])
        merge32 = sb("merge32", [P, P])
        ones = sb("ones", [P, P])
        minus_half = sb("minus_half", [P, M])
        l2_consts = sb("l2_consts", [P, 2, M])
        rms_consts = sb("rms_consts", [P, 2, M])
        rank_w = sb("rank_w", [P, E])
        X = sb("X", [P, UNITS, H])
        acc = sb("acc", [P, UNITS, H])
        xnT = sb("xnT", [P, KT, UNITS * P])
        scal = sb("scal", [P, NSC, UNITS, NV])
        convT = sb("convT", [P, TAPS, 64])
        normw = sb("normw", [P, 1])
        W = sb("W", [P, KT, HW])
        Wo = sb("Wo", [P, R, H])
        taps = sb("taps", [P, TAPS, 4])
        sc = sb("sc", [P, NSC, UNITS, R])
        y = sb("y", [P, 8, 512])
        th = sb("th", [P, 2, 512])
        sq = sb("sq", [P, 2, 512])
        ss = sb("ss", [P, M])
        rr = sb("rr", [P, M])
        qhat = sb("qhat", [P, UNITS, D])
        khat = sb("khat", [P, UNITS, D])
        kqT = sb("kqT", [P, UNITS, 2, P])
        v = sb("v", [P, M, D])
        gz = sb("gz", [P, M, D])
        dec = sb("dec", [P, M, P])
        decn = sb("decn", [P, M, P])
        attn = sb("attn", [P, M, P])
        nmat = sb("nmat", [P, M, P])
        n16 = sb("n16", [P, M, P])
        n32 = decn
        nblk = sb("nblk", [P, BLK, BLK])
        ublk = sb("ublk", [P, BLK, BLK])
        tblk = sb("tblk", [P, BLK, BLK])
        prod = sb("prod", [P, BLK * BLK])
        UT0 = sb("UT0", [P, 2, M, P])
        U0, T0 = UT0[:, 0], UT0[:, 1]
        Xm = sb("Xm", [P, M, P])
        U1 = sb("U1", [P, M, P])
        T1 = sb("T1", [P, M, P])
        U2 = U1
        st = sb("st", [P, B, R * D])
        w_ = sb("w_", [P, B, R, D])
        vn = sb("vn", [P, B, R, D])
        vd = sb("vd", [P, B, R, D])
        qs = sb("qs", [P, B, R, D])
        core = Xm
        xT = T1
        lin = gz
        mean = sb("mean", [P, UNITS])
        rstd = sb("rstd", [P, UNITS])

        FG = y[:].rearrange("p a b -> p (a b)")[:, 0:KT * FW].rearrange("p (k c) -> p k c", k=KT)
        FU = UT0[:].rearrange("p a b c -> p (a b c)")[:, 0:KT * FW].rearrange("p (k c) -> p k c", k=KT)
        FD = sb("FD", [P, FT, H])
        router = sb("router", [P, KT, E])
        def lin_x():
            return v[:].rearrange("p a b -> p (a b)").rearrange("p (u h) -> p u h", u=UNITS)

        xt = kqT[:, 0]
        hid = nmat[:].rearrange("p a b -> p (a b)")[:, 0:FW]
        thf = n16[:].rearrange("p a b -> p (a b)")[:, 0:FW]
        hT = attn[:, 0:FT]
        logits = sb("logits", [P, UNITS, E])
        probs = sb("probs", [P, UNITS, E])
        first = sb("first", [P, UNITS, E])
        second = sb("second", [P, UNITS, E])
        best = sb("best", [P, 4, UNITS])
        comb = sb("comb", [P, UNITS, FT])
        comb_u = sb("comb_u", [P, FT])

        s = {n: sem(n) for n in (
            "x_loaded", "params_loaded", "rows_stored", "w_loaded", "rows_loaded", "wo_loaded",
            "raw_stored", "raw_loaded", "inv_stored", "inv_loaded",
            "filled_a", "filled_b", "pro_filled", "pro_dve", "pro_act", "pro_pool", "gates_ready",
            "taps_ready", "tap_done", "tanh_done", "act_done", "sq_done", "ss_done", "rr_done",
            "z_tanh", "dg_done", "exp_done", "dec_done", "decn_done", "n_ready", "base_done",
            "w_done", "vd_done", "x_gated", "sq2_done", "ss2_done", "rr2_done", "x_scaled",
            "dve_step", "pool_step",
            "ep_dve", "ep_act", "ep_pool", "ep_pe", "ep_w_loaded", "ep_drained", "out_stored",
            "f_xt", "f_gu", "f_tanh", "f_h", "f_hs", "f_tr", "f_hT", "f_down", "f_y", "f_gated", "comb_ready", "layer_done")}
        drained_a = [sem(f"drained_a{i}") for i in range(4)]
        drained_b = [sem(f"drained_b{i}") for i in range(4)]
        blk = ctx.enter_context(nc.Block())

        def filled_a(eng, n, j):
            eng.wait_ge(s["filled_a"], n * JOBS_A + j + 2)

        def filled_b(eng, n, j):
            eng.wait_ge(s["filled_b"], n * JOBS_B + j + 2)

        def drained(eng, ring, jobs, n, j):
            eng.wait_ge(ring[j % 4], n * (jobs // 4) + j // 4 + 2)

        def free(eng, ring, jobs, n, j):
            eng.wait_ge(ring[j % 4], n * (jobs // 4) + j // 4 + 1)

        @blk.sync
        def _(sp):
            sp.dma_start(X[:], xf).then_inc(s["x_loaded"], 16)
            sp.dma_start(U1[:, 0, :].rearrange("p (k c) -> p k c", k=KT), w_ba.rearrange("(k p) c -> p k c", p=P)
                         ).then_inc(s["params_loaded"], 16)
            sp.dma_start(U1[:, 1, 0:NV], a_log.rearrange("(a h) -> a h", a=1).to_broadcast([P, NV])
                         ).then_inc(s["params_loaded"], 16)
            sp.dma_start(U1[:, 1, NV:2 * NV], dt_bias.rearrange("(a h) -> a h", a=1).to_broadcast([P, NV])
                         ).then_inc(s["params_loaded"], 16)
            sp.dma_start(T1[0:64, 0:TAPS, :].rearrange("t a p -> t (a p)"),
                         conv_w.rearrange("(t p) a -> t (p a)", p=P)).then_inc(s["params_loaded"], 16)
            sp.dma_start(normw[:], norm_w.rearrange("(p a) -> p a", a=1)).then_inc(s["params_loaded"], 16)
            sp.wait_ge(s["gates_ready"], 1)
            sp.dma_start(decay_rows, Xm[0:NV, 0:UNITS, :].rearrange("h u i -> h (u i)")
                         ).then_inc(s["rows_stored"], 16)
            sp.wait_ge(s["rows_stored"], 16)
            with sp.Fori(0, NK) as n:
                sp.wait_ge(s["filled_a"], n * JOBS_A + 1)
                sp.dma_start(W[:], w_qkvz[:, bass.ds(n * HW, HW)].rearrange("(k p) c -> p k c", p=P)
                             ).then_inc(s["w_loaded"], 16)
                sp.wait_ge(s["n_ready"], n * 8 + 1)
                for r in range(R):
                    sp.dma_start(dec[:].rearrange("p (u r) i -> p u r i", r=R)[:, :, r, :],
                                 decay_rows[bass.ds(n * R + r, 1), :].rearrange("h (u i) -> h u i", u=UNITS)
                                 .to_broadcast([P, UNITS, P])).then_inc(s["rows_loaded"], 16)
                sp.wait_ge(s["filled_b"], n * JOBS_B + 1)
                sp.dma_start(Wo[:], w_out[bass.ds(n * R * D, R * D), :].rearrange("(r p) c -> p r c", p=P)
                             ).then_inc(s["wo_loaded"], 16)
                for g in range(4):
                    drained(sp, drained_a, JOBS_A, n, GRAM + g)
                for k in range(NB):
                    sp.dma_start(raw_blocks[k].rearrange("m j i -> j m i"),
                                 nmat[k * BLK:(k + 1) * BLK, :, k * BLK:(k + 1) * BLK]
                                 ).then_inc(s["raw_stored"], 16)
                sp.wait_ge(s["raw_stored"], (n + 1) * 16 * NB)
                sp.dma_start(nblk[:], raw_blocks.rearrange("k m j i -> (k m) j i")).then_inc(s["raw_loaded"], 16)
                sp.wait_ge(s["base_done"], (n + 1) * 2)
                sp.dma_start(inv_blocks[0].rearrange("k m c i -> (k m) c i"), ublk[:]).then_inc(s["inv_stored"], 16)
                sp.dma_start(inv_blocks[1].rearrange("k m c i -> (k m) c i"), tblk[:]).then_inc(s["inv_stored"], 16)
                sp.wait_ge(s["inv_stored"], (n + 1) * 32)
                for i, dst in enumerate((U0, T0)):
                    for k in range(NB):
                        sp.dma_start(dst[k * BLK:(k + 1) * BLK, :, k * BLK:(k + 1) * BLK],
                                     inv_blocks[i, k].rearrange("m c i -> c m i")).then_inc(s["inv_loaded"], 16)
            sp.wait_ge(s["filled_a"], NK * JOBS_A + 1)
            sp.wait_ge(s["filled_b"], (NK - 1) * JOBS_B + RECUR + 2)
            for t, we, ws in ((FG, w_gate, sw_gate), (FU, w_up, sw_up)):
                for k in range(KT):
                    sp.dma_start(t[:, k, 0:E * FH].rearrange("p (e h) -> p e h", e=E),
                                 we[:, k * P:(k + 1) * P, :].rearrange("e p h -> p e h")
                                 ).then_inc(s["ep_w_loaded"], 16)
                    sp.dma_start(t[:, k, E * FH:FW], ws[k * P:(k + 1) * P, :]).then_inc(s["ep_w_loaded"], 16)
            sp.dma_start(FD[:, 0:E, :], w_down.rearrange("e p d -> p e d")).then_inc(s["ep_w_loaded"], 16)
            sp.dma_start(FD[:, E:FT, :], sw_down.rearrange("(t p) d -> p t d", p=P)).then_inc(s["ep_w_loaded"], 16)
            sp.dma_start(router[:],
                         router_w.rearrange("(k p) e -> p k e", p=P)).then_inc(s["ep_w_loaded"], 16)
            sp.wait_ge(s["layer_done"], 1)
            sp.dma_start(of, X[:]).then_inc(s["out_stored"], 16)
            sp.wait_ge(s["out_stored"], 16)

        def norm(dve, act_sq, steps, src, dst, pool_wait):
            steps.did(dve.tensor_reduce(mean[:], src, AX.X, ALU.add))
            steps.wait()
            steps.did(dve.tensor_scalar(mean[:], mean[:], 1.0 / H, None, ALU.mult))
            steps.wait()
            steps.did(dve.tensor_tensor(dst, src, mean[:].unsqueeze(2).to_broadcast([P, UNITS, H]), ALU.subtract))
            steps.wait()
            flat = lin[:].rearrange("p a b -> p (a b)").rearrange("p (u h) -> p u h", u=UNITS)
            steps.did(dve.tensor_tensor(flat, dst, dst, ALU.mult))
            steps.wait()
            k = steps.did(dve.tensor_reduce(rstd[:], flat, AX.X, ALU.add))
            pool_wait()
            steps.did(dve.tensor_tensor(dst, dst, rstd[:].unsqueeze(2).to_broadcast([P, UNITS, H]), ALU.mult))
            return k


        @blk.gpsimd
        def _(po):
            po.sem_inc(s["n_ready"])
            st_ = Steps(po, s["pro_pool"])
            st_.did(po.memset(ident[:], 0.0))
            st_.did(po.memset(ones[:], 1.0))
            st_.did(po.memset(merge16[:], 0.0))
            st_.did(po.memset(merge32[:], 0.0))
            st_.did(po.memset(minus_half[:], -0.5))
            st_.wait()
            st_.did(po.affine_select(out=ident[:], in_=ident[:], compare_op=ALU.not_equal, fill=1.0, base=0,
                                     pattern=[[-1, P]], channel_multiplier=1))
            st_.did(po.affine_select(out=upper[:], in_=ones[:], compare_op=ALU.is_ge, fill=0.0, base=0,
                                     pattern=[[1, P]], channel_multiplier=-1))
            for m_, size in ((merge16, 16), (merge32, 32)):
                half = m_[:].rearrange("p (b h l) -> p b h l", h=2, l=size)[:, :, 1, :]
                nb = P // (2 * size)
                st_.did(po.memset(half, 1.0))
                st_.wait()
                st_.did(po.affine_select(out=half, in_=half, compare_op=ALU.is_ge, fill=0.0, base=0,
                                         pattern=[[-2 * size, nb], [0, size]], channel_multiplier=1))
                st_.wait()
                st_.did(po.affine_select(out=half, in_=half, compare_op=ALU.is_ge, fill=0.0, base=size - 1,
                                         pattern=[[2 * size, nb], [0, size]], channel_multiplier=-1))
            for e in range(E):
                st_.did(po.memset(rank_w[:, e:e + 1], float(E - e)))
            st_.did(po.memset(U0, 0.0))
            st_.did(po.memset(T0, 0.0))
            st_.did(po.memset(ublk[:], 0.0))
            st_.did(po.memset(acc[:], 0.0))
            for t, value in ((l2_consts[:, 0, 0:UNITS], D), (l2_consts[:, 0, UNITS:M], 1.0),
                             (l2_consts[:, 1, 0:UNITS], 4 * D * L2_EPS), (l2_consts[:, 1, UNITS:M], 4 * L2_EPS),
                             (rms_consts[:, 0], 1.0 / D), (rms_consts[:, 1], 4 * RMS_EPS)):
                st_.did(po.memset(t, float(value)))
            st_.wait()
            st_.did(po.memset(ublk[:].rearrange("p a b -> p (a b)")[:, 0:BLK * BLK:BLK + 1], 1.0))
            assert st_.k == PRO_POOL, st_.k
            po.wait_ge(s["pro_dve"], PRO_NORM)
            st_.did(po.tensor_scalar(rstd[:], rstd[:], 1.0 / H, LN_EPS, ALU.mult, ALU.add))
            st_.wait()
            st_.did(po.tensor_tensor(rstd[:], rstd[:], minus_half[:, 0:UNITS], ALU.pow))
            po.wait_ge(s["pro_dve"], PRO_DVE)
            po.wait_ge(s["pro_act"], PRO_ACT)
            with po.Fori(0, NK) as n:
                ps = Steps(po, s["pool_step"], n * POOL_STEPS)
                po.wait_ge(s["filled_b"], n * JOBS_B + 1)
                for b_ in range(4):
                    po.wait_ge(drained_b[b_], n * (JOBS_B // 4) + 1)
                ps.did(po.tensor_copy(sc[:], scal[:, :, :, bass.ds(n * R, R)]))
                ps.did(po.tensor_copy(taps[:, :, 0:2], convT[:, :, bass.ds(n, 2, NK)]))
                ps.wait()
                po.tensor_copy(taps[:, :, 2:4], convT[:, :, bass.ds(n * R + 2 * NK, 2)]).then_inc(s["taps_ready"], 1)
                po.wait_ge(s["ss_done"], n * 4 + 5)
                ps.did(po.tensor_tensor(rr[:], ss[:], l2_consts[:, 0], ALU.mult))
                ps.wait()
                ps.did(po.tensor_tensor(rr[:], rr[:], l2_consts[:, 1], ALU.add))
                ps.wait()
                po.tensor_tensor(rr[:], rr[:], minus_half[:], ALU.pow).then_inc(s["rr_done"], 1)
                po.wait_ge(s["exp_done"], n + 1)
                po.tensor_tensor(dec[:], dec[:], upper[:].unsqueeze(1).to_broadcast([P, M, P]), ALU.mult
                                 ).then_inc(s["dec_done"], 1)
                po.wait_ge(s["dec_done"], n + 1)
                po.tensor_tensor(decn[:], dec[:],
                                 sc[:, S_NBETA].rearrange("p u r -> p (u r)").unsqueeze(2).to_broadcast([P, M, P]),
                                 ALU.mult).then_inc(s["decn_done"], 1)
                for g in range(4):
                    drained(po, drained_a, JOBS_A, n, GRAM + g)
                for g in range(4):
                    ms = slice(4 * g, 4 * g + 4)
                    po.tensor_tensor(n16[:, ms], nmat[:, ms], merge16[:].unsqueeze(1).to_broadcast([P, 4, P]),
                                     ALU.mult).then_inc(s["n_ready"], 1)
                for g in range(4):
                    ms = slice(4 * g, 4 * g + 4)
                    po.tensor_tensor(n32[:, ms], nmat[:, ms], merge32[:].unsqueeze(1).to_broadcast([P, 4, P]),
                                     ALU.mult).then_inc(s["n_ready"], 1)
                po.wait_ge(s["ss2_done"], n * 4 + 5)
                ps.did(po.tensor_tensor(rr[:], ss[:], rms_consts[:, 0], ALU.mult))
                ps.wait()
                ps.did(po.tensor_tensor(rr[:], rr[:], rms_consts[:, 1], ALU.add))
                ps.wait()
                po.tensor_tensor(rr[:], rr[:], minus_half[:], ALU.pow).then_inc(s["rr2_done"], 1)
                assert ps.k == POOL_STEPS, ps.k
            ep = Steps(po, s["ep_pool"])
            for done in EP_NORMS:
                po.wait_ge(s["ep_dve"], done)
                ep.did(po.tensor_scalar(rstd[:], rstd[:], 1.0 / H, LN_EPS, ALU.mult, ALU.add))
                ep.wait()
                ep.did(po.tensor_tensor(rstd[:], rstd[:], minus_half[:, 0:UNITS], ALU.pow))


        @blk.tensor
        def _(pe):
            for name in ("filled_a", "filled_b", "f_gu", "f_tr", "f_down"):
                pe.sem_inc(s[name])
            pe.wait_ge(s["pro_pool"], PRO_POOL)
            pe.wait_ge(s["pro_dve"], PRO_NORM + 1)
            for q in range(4):
                k, hf = q // 2, q % 2
                for i in range(4):
                    mm = pe.transpose(bank[q][:, i * P:(i + 1) * P], lin_x()[:, hf * 4 + i, k * P:(k + 1) * P],
                                      ident[:])
                mm.then_inc(s["pro_filled"], 1)
            pe.wait_ge(s["params_loaded"], 80)
            for a in range(TAPS):
                mm = pe.transpose(bank[5][:, a * 64:(a + 1) * 64],
                                  T1[0:64, 0:TAPS, :].rearrange("t a p -> t (a p)")[:, a:TAPS * P:TAPS],
                                  ident[0:64, 0:64])
            mm.then_inc(s["pro_filled"], 1)
            pe.wait_ge(s["pro_dve"], PRO_NORM + 5)
            wba = U1[:, 0, :].rearrange("p (k c) -> p k c", k=KT)
            for u in range(UNITS):
                for k in range(KT):
                    mm = pe.matmul(bank[4][:, u * 64:(u + 1) * 64], xnT[:, k, u * P:(u + 1) * P], wba[:, k, :],
                                   start=(k == 0), stop=(k == KT - 1))
            mm.then_inc(s["pro_filled"], 1)
            pe.wait_ge(s["pro_dve"], PRO_G)
            g_ = U1[:, 2:4, :].rearrange("p a b -> p (a b)")
            pe.matmul(bank[6][:, 0:256], upper[:], g_, start=True, stop=True)
            pe.matmul(bank[6][:, 256:512], ones[:], g_, start=True, stop=True).then_inc(s["pro_filled"], 1)
            for u in range(UNITS):
                mm = pe.matmul(bank[u // 4][0:NV, (u % 4) * P:(u % 4 + 1) * P], g_[:, u * NV:(u + 1) * NV], upper[:],
                               start=True, stop=True)
            mm.then_inc(s["pro_filled"], 1)
            pe.wait_ge(s["pro_dve"], PRO_DVE)
            pe.wait_ge(s["pro_act"], PRO_ACT)

            def merge_step(n, step, g):
                j = MERGE + step * 4 + g
                out_ = ring_b[j % 4]
                free(pe, drained_b, JOBS_B, n, j)
                prev = j - 4
                if step:
                    drained(pe, drained_b, JOBS_B, n, prev)
                for i in range(4):
                    m = 4 * g + i
                    o = out_[:, i * P:(i + 1) * P]
                    if step == 0:
                        mm = pe.matmul(o, n16[:, m], T0[:, m], start=True, stop=True)
                    elif step == 1:
                        mm = pe.matmul(o, Xm[:, m], U0[:, m], start=True, stop=True)
                    elif step == 3:
                        mm = pe.matmul(o, n32[:, m], T1[:, m], start=True, stop=True)
                    elif step == 4:
                        mm = pe.matmul(o, Xm[:, m], U1[:, m], start=True, stop=True)
                    elif step in (2, 5):
                        mm = pe.transpose(o, U1[:, m], ident[:])
                    elif step == 6:
                        mm = pe.matmul(out_[:, i * 64:(i + 1) * 64], nmat[0:64, m], T1[0:64, m, 0:64],
                                       start=True, stop=True)
                    else:
                        mm = pe.matmul(out_[:, i * 64:(i + 1) * 64], Xm[64:P, m], U1[64:P, m, 64:P],
                                       start=True, stop=True)
                mm.then_inc(s["filled_b"], 1)

            with pe.Fori(0, NK) as n:
                for j in range(8):
                    ct, b = j // 2, j % 2
                    if j == 0:
                        pe.wait_ge(s["w_loaded"], (n + 1) * 16)
                    free(pe, drained_a, JOBS_A, n, PROJ + j)
                    for k in range(KT):
                        mm = pe.matmul(ring_a[j % 4][:], W[:, k, ct * P:(ct + 1) * P],
                                       xnT[:, k, b * S:(b + 1) * S], start=(k == 0), stop=(k == KT - 1))
                    mm.then_inc(s["filled_a"], 1)
                for g in range(4):
                    free(pe, drained_a, JOBS_A, n, ZJ + g)
                    for i in range(2):
                        u = 2 * g + i
                        for k in range(KT):
                            mm = pe.matmul(ring_a[g][:, i * 256:(i + 1) * 256], xnT[:, k, u * P:(u + 1) * P],
                                           W[:, k, HW - R * D:HW], start=(k == 0), stop=(k == KT - 1))
                    mm.then_inc(s["filled_a"], 1)
                for j in range(8):
                    free(pe, drained_a, JOBS_A, n, TR + j)
                    pe.wait_ge(s["act_done"], n * 8 + j + 2)
                    for i in range(4):
                        mm = pe.transpose(ring_a[j % 4][:, i * P:(i + 1) * P], y[:, j, i * P:(i + 1) * P], ident[:])
                    mm.then_inc(s["filled_a"], 1)
                for g in range(4):
                    for half in (TR + g // 2, TR + 2 + g // 2):
                        if half % 4 != g:
                            drained(pe, drained_a, JOBS_A, n, half)
                    free(pe, drained_a, JOBS_A, n, BACK + g)
                    for i in range(2):
                        for x_, src in enumerate((khat, qhat)):
                            c0 = (2 * i + x_) * P
                            mm = pe.transpose(ring_a[g][:, c0:c0 + P], src[:, 2 * g + i, :], ident[:])
                    mm.then_inc(s["filled_a"], 1)
                for g in range(4):
                    drained(pe, drained_a, JOBS_A, n, BACK + g)
                    for i in range(2):
                        u = 2 * g + i
                        mm = pe.matmul(ring_a[g][:, i * 256:(i + 1) * 256], kqT[:, u, 0, :],
                                       kqT[:, u].rearrange("p x i -> p (x i)"), start=True, stop=True)
                    mm.then_inc(s["filled_a"], 1)
                pe.wait_ge(s["n_ready"], (n + 1) * 8 + 1)
                pe.wait_ge(s["inv_loaded"], (n + 1) * 32 * NB)
                for step in range(8):
                    for g in range(4):
                        merge_step(n, step, g)
                for c in range(CH):
                    for b in range(B):
                        u = b * CH + c
                        if c:
                            j = RJ["state", u]
                            free(pe, drained_b, JOBS_B, n, j)
                            drained(pe, drained_b, JOBS_B, n, RJ["update", u - 1])
                            pe.matmul(ring_b[j % 4][:, 0:256], kqT[:, u, 0, :], st[:, b], start=True, stop=True)
                            pe.matmul(ring_b[j % 4][:, 256:512], kqT[:, u, 1, :], st[:, b], start=True, stop=True
                                      ).then_inc(s["filled_b"], 1)
                    for b in range(B):
                        u = b * CH + c
                        j = RJ["solve", u]
                        free(pe, drained_b, JOBS_B, n, j)
                        if c:
                            pe.wait_ge(s["w_done"], n * (UNITS - B) + (c - 1) * B + b + 1)
                        elif b == 0:
                            for g in range(4):
                                drained(pe, drained_b, JOBS_B, n, MERGE + 28 + g)
                        for r in range(R):
                            rhs = w_[:, b, r] if c else v[:, u * R + r]
                            mm = pe.matmul(ring_b[j % 4][:, r * D:(r + 1) * D], U2[:, u * R + r], rhs,
                                           start=True, stop=True)
                        mm.then_inc(s["filled_b"], 1)
                    for b in range(B):
                        u = b * CH + c
                        j = RJ["local", u]
                        free(pe, drained_b, JOBS_B, n, j)
                        drained(pe, drained_b, JOBS_B, n, RJ["solve", u])
                        for r in range(R):
                            mm = pe.matmul(ring_b[j % 4][:, r * D:(r + 1) * D], attn[:, u * R + r], vn[:, b, r],
                                           start=True, stop=True)
                        mm.then_inc(s["filled_b"], 1)
                    for b in range(B):
                        u = b * CH + c
                        if c < CH - 1:
                            j = RJ["update", u]
                            free(pe, drained_b, JOBS_B, n, j)
                            pe.wait_ge(s["vd_done"], n * (UNITS - B) + c * B + b + 1)
                            pe.matmul(ring_b[j % 4][:, 0:256], khat[:, u], vd[:, b].rearrange("p r d -> p (r d)"),
                                      start=True, stop=True).then_inc(s["filled_b"], 1)
                for g in range(4):
                    free(pe, drained_b, JOBS_B, n, XT + g)
                    pe.wait_ge(s["x_scaled"], n * 4 + g + 1)
                    for i in range(4):
                        mm = pe.transpose(ring_b[g][:, i * P:(i + 1) * P], core[:, 4 * g + i], ident[:])
                    mm.then_inc(s["filled_b"], 1)
                for g in range(4):
                    if g == 0:
                        pe.wait_ge(s["wo_loaded"], (n + 1) * 16)
                    drained(pe, drained_b, JOBS_B, n, XT + g)
                    for i in range(2):
                        for r in range(R):
                            mm = pe.matmul(ring_b[g][:, i * 256:(i + 1) * 256], xT[:, 4 * g + 2 * i + r], Wo[:, r],
                                           start=(r == 0), stop=(r == R - 1))
                    mm.then_inc(s["filled_b"], 1)

            pe.wait_ge(s["ep_dve"], EP_XN2)
            for q in range(4):
                k, hf = q // 2, q % 2
                for i in range(4):
                    mm = pe.transpose(bank[q][:, i * P:(i + 1) * P], lin_x()[:, hf * 4 + i, k * P:(k + 1) * P],
                                      ident[:])
                mm.then_inc(s["ep_pe"], 1)
            pe.wait_ge(s["ep_dve"], EP_XN2 + 4)
            pe.wait_ge(s["ep_w_loaded"], EP_LOADS)
            for u in range(UNITS):
                for k in range(KT):
                    mm = pe.matmul(bank[4][:, u * E:(u + 1) * E], xnT[:, k, u * P:(u + 1) * P],
                                   router[:, k, :], start=(k == 0), stop=(k == KT - 1))
            mm.then_inc(s["ep_pe"], 1)
            pe.wait_ge(s["ep_dve"], EP_COMB)
            with pe.Fori(0, UNITS) as u:
                pe.wait_ge(s["f_xt"], u + 1)
                for q, (c0, cw) in enumerate(FCHUNKS):
                    if q == 2:
                        pe.wait_ge(s["f_h"], u * 3 + 2)
                    elif q == 0:
                        pe.wait_ge(s["f_h"], u * 3 + 1)
                    else:
                        pe.wait_ge(s["f_h"], u * 3 + 1)
                    for x_, wt in enumerate((FG, FU)):
                        for k in range(KT):
                            mm = pe.matmul(bank[2 * (q % 2) + x_][:, 0:cw], xt[:, k, :], wt[:, k, c0:c0 + cw],
                                           start=(k == 0), stop=(k == KT - 1))
                    mm.then_inc(s["f_gu"], 1)
                for q, (c0, cw) in enumerate(FCHUNKS):
                    pe.wait_ge(s["f_hs"], u * 3 + q + 2)
                    pe.wait_ge(s["f_hT"], u * 3 + (1 if q == 2 else 0) + 1)
                    for i in range(cw // P):
                        mm = pe.transpose(bank[4 + q % 2][:, i * P:(i + 1) * P], hid[:, c0 + i * P:c0 + (i + 1) * P],
                                          ident[:])
                    mm.then_inc(s["f_tr"], 1)
                pe.wait_ge(s["f_hT"], u * 3 + 4)
                pe.wait_ge(s["f_y"], u + 1)
                for i in range(FT):
                    mm = pe.matmul(bank[6][:, 0:H], hT[:, i], FD[:, i], start=(i == 0), stop=(i == FT - 1))
                mm.then_inc(s["f_down"], 1)


        @blk.scalar
        def _(a):
            a.sem_inc(s["f_hT"])
            pa = Steps(a, s["pro_act"])
            b3 = bank[4][:].rearrange("p (h x) -> p h x", x=4)
            beta = scal[:, S_BETA].rearrange("p u (k r) -> p (u k) r", r=R)
            a.wait_ge(s["pro_filled"], 6)
            pa.did(a.activation(beta, b3[:, :, 0:2], ACT.Exp, scale=-1.0))
            pa.did(a.activation(U1[:, 1, 0:NV], U1[:, 1, 0:NV], ACT.Exp))
            a.wait_ge(s["pro_dve"], PRO_ABS)
            e_ = T1[:, 8:10, :]
            pa.did(a.activation(e_, e_, ACT.Exp, scale=-1.0))
            pa.wait()
            pa.did(a.activation(e_, e_, ACT.Ln, bias=1.0))
            a.wait_ge(s["pro_filled"], 8)
            a.wait_ge(s["pro_dve"], PRO_G + 2)
            pa.did(a.activation(scal[:, S_EG], scal[:, S_G], ACT.Exp))
            pa.did(a.activation(T1[:, 10:14, :], T1[:, 10:14, :], ACT.Exp))
            assert pa.k == PRO_ACT
            a.wait_ge(s["pro_dve"], PRO_DVE)

            with a.Fori(0, NK) as n:
                def tap(j):
                    if j == 0:
                        a.wait_ge(s["taps_ready"], n + 1)
                    filled_a(a, n, PROJ + j)
                    a.activation(y[:, j], ring_a[j % 4][:], ACT.Copy, scale=taps[:, 3, j // 2:j // 2 + 1]
                                 ).then_inc(s["tap_done"], 1)

                def half_tanh(j):
                    drained(a, drained_a, JOBS_A, n, PROJ + j)
                    a.wait_ge(s["act_done"], n * 8 + (j - 1 if j > 1 else 0) + 1)
                    a.activation(th[:, j % 2], y[:, j], ACT.Tanh, scale=0.5).then_inc(s["tanh_done"], 1)

                tap(0)
                for j in range(1, 8):
                    tap(j)
                    half_tanh(j - 1)
                half_tanh(7)
                for g in range(4):
                    filled_a(a, n, ZJ + g)
                    if g >= 2:
                        drained(a, drained_a, JOBS_A, n, ZJ + g - 2)
                    else:
                        a.wait_ge(s["act_done"], n * 8 + 9)
                    a.activation(th[:, g % 2], ring_a[g][:], ACT.Tanh, scale=0.5).then_inc(s["z_tanh"], 1)
                for i in range(4):
                    filled_a(a, n, TR + i)
                    a.wait_ge(s["ss_done"], n * 4 + (i - 1 if i > 1 else 0) + 1)
                    a.activation(sq[:, i % 2], ring_a[i][:], ACT.Square).then_inc(s["sq_done"], 1)
                for i in range(4):
                    r, b = i // 2, i % 2
                    filled_a(a, n, TR + 4 + i)
                    a.wait_ge(s["filled_b"], n * JOBS_B + 1)
                    a.activation(v[:].rearrange("p (u r) d -> p u r d", r=R)[:, b * CH:(b + 1) * CH, r, :],
                                 ring_a[i][:].rearrange("p (u d) -> p u d", d=D), ACT.Copy, scale=0.5
                                 ).then_inc(drained_a[i], 1)
                a.wait_ge(s["dg_done"], n + 1)
                a.activation(dec[:], dec[:], ACT.Exp).then_inc(s["exp_done"], 1)
                for g in range(4):
                    filled_a(a, n, BACK + g)
                    a.activation(kqT[:, 2 * g:2 * g + 2].rearrange("p u x i -> p (u x i)"), ring_a[g][:], ACT.Copy
                                 ).then_inc(drained_a[g], 1)
                for step in range(8):
                    for g in range(4):
                        ms = slice(4 * g, 4 * g + 4)
                        j = MERGE + 4 * step + g
                        if step in (1, 4):
                            continue
                        filled_b(a, n, j)
                        if step in (0, 3):
                            dst, src = Xm[:, ms], ring_b[g][:].rearrange("p (m i) -> p m i", m=4)
                        elif step == 2:
                            dst, src = T1[:, ms], ring_b[g][:].rearrange("p (m i) -> p m i", m=4)
                        elif step == 5:
                            dst = T1[0:64, ms, 0:64]
                            src = ring_b[g][0:64, :].rearrange("p (m i) -> p m i", m=4)[:, :, 0:64]
                        elif step == 6:
                            dst = Xm[64:P, ms, 0:64]
                            src = ring_b[g][64:P, 0:256].rearrange("p (m i) -> p m i", m=4)
                        else:
                            dst = U2[0:64, ms, 64:P]
                            src = ring_b[g][0:64, 0:256].rearrange("p (m i) -> p m i", m=4)
                        a.activation(dst, src, ACT.Copy).then_inc(drained_b[g], 1)
                for c in range(CH):
                    for b in range(B):
                        u = b * CH + c
                        if c:
                            j = RJ["state", u]
                            a.wait_ge(s["w_done"], n * (UNITS - B) + (c - 1) * B + b + 1)
                            if c > 1:
                                drained(a, drained_b, JOBS_B, n, RJ["local", u - 1])
                            for r in range(R):
                                t = a.activation(qs[:, b, r], ring_b[j % 4][:, 256 + r * D:256 + (r + 1) * D],
                                                 ACT.Copy, scale=sc[:, S_EG, u, r:r + 1])
                            t.then_inc(drained_b[j % 4], 1)
                    for b in range(B):
                        u = b * CH + c
                        j = RJ["solve", u]
                        if c < CH - 1:
                            a.wait_ge(s["vd_done"], n * (UNITS - B) + c * B + b + 1)
                        else:
                            filled_b(a, n, j)
                        if 0 < c < CH - 1:
                            filled_b(a, n, RJ["local", u - 1])
                        for r in range(R):
                            t = a.activation(vn[:, b, r], ring_b[j % 4][:, r * D:(r + 1) * D], ACT.Copy,
                                             scale=sc[:, S_BETA, u, r:r + 1])
                        t.then_inc(drained_b[j % 4], 1)
                for g in range(4):
                    a.wait_ge(s["x_gated"], n * 4 + g + 1)
                    a.wait_ge(s["ss2_done"], n * 4 + (g - 1 if g > 1 else 0) + 1)
                    if g == 0:
                        a.wait_ge(s["ss_done"], n * 4 + 5)
                    a.activation(sq[:, g % 2], core[:, 4 * g:4 * g + 4].rearrange("p m d -> p (m d)"), ACT.Square
                                 ).then_inc(s["sq2_done"], 1)
                for g in range(4):
                    filled_b(a, n, XT + g)
                    a.activation(xT[:, 4 * g:4 * g + 4].rearrange("p m d -> p (m d)"), ring_b[g][:], ACT.Copy,
                                 scale=normw[:, 0:1]).then_inc(drained_b[g], 1)
            ea = Steps(a, s["ep_act"])
            a.wait_ge(s["ep_dve"], EP_EXP)
            ea.did(a.activation(probs[:], logits[:], ACT.Exp))
            with a.Fori(0, UNITS) as u:
                for q, (c0, cw) in enumerate(FCHUNKS):
                    a.wait_ge(s["f_gu"], u * 3 + q + 2)
                    a.wait_ge(s["f_h"], u * 3 + 1)
                    a.activation(thf[:, c0:c0 + cw], bank[2 * (q % 2)][:, 0:cw], ACT.Tanh, scale=0.5
                                 ).then_inc(s["f_tanh"], 1)
                for q, (c0, cw) in enumerate(FCHUNKS):
                    a.wait_ge(s["f_tr"], u * 3 + q + 2)
                    a.wait_ge(s["f_down"], u + 1)
                    a.activation(hT[:, c0 // P:(c0 + cw) // P].rearrange("p a b -> p (a b)"), bank[4 + q % 2][:, 0:cw],
                                 ACT.Copy).then_inc(s["f_hT"], 1)

        @blk.vector
        def _(d):
            for name in ("act_done", "ss_done", "ss2_done", "f_h", "f_hs", "f_y"):
                d.sem_inc(s[name])
            for q in (*drained_a, *drained_b):
                d.sem_inc(q)
            pr = Steps(d, s["pro_dve"])
            flat8 = lin_x()

            def pool_first():
                d.wait_ge(s["pro_pool"], PRO_POOL + 2)
            d.wait_ge(s["x_loaded"], 16)
            norm(d, None, pr, X[:], flat8, pool_first)
            for q in range(4):
                d.wait_ge(s["pro_filled"], q + 1)
                pr.did(d.tensor_copy(xnT[:, q // 2, (q % 2) * 512:(q % 2 + 1) * 512], bank[q][:]))
            d.wait_ge(s["pro_filled"], 5)
            pr.did(d.tensor_copy(convT[:].rearrange("p a t -> p (a t)"), bank[5][:, 0:256]))
            d.wait_ge(s["pro_filled"], 6)
            d.wait_ge(s["pro_act"], 2)
            za = T1[:, 6:8, :]
            za4 = za.rearrange("p a b -> p (a b)").rearrange("p (u k r) -> p u k r", u=UNITS, r=R)
            ain = bank[4][:].rearrange("p (u k x) -> p u k x", u=UNITS, x=4)[:, :, :, 2:4]
            dtb = U1[:, 1, NV:2 * NV].rearrange("p (k r) -> p k r", r=R).unsqueeze(1).to_broadcast([P, UNITS, NK, R])
            pr.did(d.tensor_tensor(za4, ain, dtb, ALU.add))
            pr.wait()
            e_ = T1[:, 8:10, :]
            pr.did(d.scalar_tensor_tensor(e_, za, -1.0, za, ALU.mult, ALU.max))
            d.wait_ge(s["pro_act"], 4)
            pr.did(d.scalar_tensor_tensor(za, za, 0.0, e_, ALU.max, ALU.add))
            beta = scal[:, S_BETA]
            pr.did(d.tensor_scalar(beta, beta, 1.0, None, ALU.add))
            pr.wait()
            pr.did(d.reciprocal(beta, beta))
            g_ = U1[:, 2:4, :].rearrange("p a b -> p (a b)").rearrange("p (u h) -> p u h", u=UNITS)
            pr.did(d.scalar_tensor_tensor(g_, za.rearrange("p a b -> p (a b)").rearrange("p (u h) -> p u h", u=UNITS),
                                          -1.0, U1[:, 1, 0:NV].unsqueeze(1).to_broadcast([P, UNITS, NV]),
                                          ALU.mult, ALU.mult))
            assert pr.k == PRO_G
            d.wait_ge(s["pro_filled"], 8)
            G = scal[:, S_G].rearrange("p u h -> p (u h)")
            pr.did(d.tensor_copy(G, bank[6][:, 0:256]))
            pr.wait()
            gl = T1[:, 10:14, :].rearrange("p a b -> p (a b)")
            d.tensor_copy(gl[:, 0:256], bank[6][:, 256:512])
            pr.did(d.tensor_tensor(gl[:, 256:512], bank[6][:, 256:512], G, ALU.subtract))
            d.tensor_copy(Xm[0:NV, 0:4, :].rearrange("h u i -> h (u i)"), bank[0][0:NV, :])
            d.tensor_copy(Xm[0:NV, 4:8, :].rearrange("h u i -> h (u i)"), bank[1][0:NV, :]
                          ).then_inc(s["gates_ready"], 1)
            d.wait_ge(s["pro_act"], 6)
            pr.did(d.tensor_copy(scal[:, S_EGL].rearrange("p u h -> p (u h)"), gl[:, 0:256]))
            d.tensor_scalar(scal[:, S_NEG], scal[:, S_EG], -1.0, None, ALU.mult)
            pr.did(d.tensor_scalar(scal[:, S_NBETA], beta, -1.0, None, ALU.mult))
            pr.did(d.tensor_tensor(scal[:, S_BK].rearrange("p u h -> p (u h)"), gl[:, 256:512],
                                   scal[:, S_BETA].rearrange("p u h -> p (u h)"), ALU.mult))
            assert pr.k == PRO_DVE

            with d.Fori(0, NK) as n:
                ds = Steps(d, s["dve_step"], n * DVE_STEPS)

                def silu(j):
                    d.wait_ge(s["tanh_done"], n * 8 + j + 1)
                    d.scalar_tensor_tensor(y[:, j], th[:, j % 2], 1.0, y[:, j], ALU.add, ALU.mult
                                           ).then_inc(s["act_done"], 1)

                for j in range(8):
                    d.wait_ge(s["tap_done"], n * 8 + j + 1)
                    for back in range(1, TAPS):
                        if back > 1:
                            ds.wait()
                        t = d.scalar_tensor_tensor(y[:, j, back:], ring_a[j % 4][:, 0:S - back],
                                                   taps[:, TAPS - 1 - back, j // 2:j // 2 + 1], y[:, j, back:],
                                                   ALU.mult, ALU.add)
                        if back < TAPS - 1:
                            ds.did(t)
                        else:
                            t.then_inc(drained_a[j % 4], 1)
                    if j:
                        silu(j - 1)
                silu(7)
                for g in range(4):
                    d.wait_ge(s["z_tanh"], n * 4 + g + 1)
                    d.scalar_tensor_tensor(gz[:, 4 * g:4 * g + 4].rearrange("p m d -> p (m d)"), th[:, g % 2], 1.0,
                                           ring_a[g][:], ALU.add, ALU.mult).then_inc(drained_a[g], 1)
                d.wait_ge(s["rows_loaded"], (n + 1) * 16 * R)
                d.wait_ge(s["taps_ready"], n + 1)
                for m in range(M):
                    t = d.tensor_scalar(dec[:, m], dec[:, m], sc[:, S_G, m // R, m % R:m % R + 1], 0.0,
                                        ALU.subtract, ALU.min)
                t.then_inc(s["dg_done"], 1)
                for i in range(4):
                    d.wait_ge(s["sq_done"], n * 4 + i + 1)
                    d.tensor_reduce(ss[:, 4 * i:4 * i + 4], sq[:, i % 2].rearrange("p (u d) -> p u d", d=D), AX.X,
                                    ALU.add).then_inc(s["ss_done"], 1)
                d.wait_ge(s["rr_done"], n + 1)
                d.wait_ge(s["filled_b"], n * JOBS_B + 1)
                for i in range(4):
                    dst = (qhat, khat)[i // 2]
                    d.tensor_tensor(dst[:, (i % 2) * CH:(i % 2 + 1) * CH], ring_a[i][:].rearrange("p (u d) -> p u d", d=D),
                                    rr[:, 4 * i:4 * i + 4].unsqueeze(2).to_broadcast([P, 4, D]), ALU.mult
                                    ).then_inc(drained_a[i], 1)
                d.wait_ge(s["dec_done"], n + 1)
                d.wait_ge(s["decn_done"], n + 1)
                for g in range(4):
                    filled_a(d, n, GRAM + g)
                    kk = ring_a[g][:].rearrange("p (u x i) -> p u x i", x=2, i=P)
                    for x_, (dst, by) in enumerate(((nmat, decn), (attn, dec))):
                        for i in range(2):
                            ms = slice(4 * g + 2 * i, 4 * g + 2 * i + 2)
                            t = d.tensor_tensor(dst[:, ms], kk[:, i, x_, :].unsqueeze(1).to_broadcast([P, R, P]),
                                                by[:, ms], ALU.mult)
                    t.then_inc(drained_a[g], 1)
                d.wait_ge(s["raw_loaded"], (n + 1) * 16)
                for i in range(1, BLK):
                    if i == 1:
                        ds.did(d.tensor_copy(ublk[:, 0:1, 1], nblk[:, 0:1, 1]))
                        ds.wait()
                        continue
                    pv = prod[:, 0:i * i].rearrange("p (c j) -> p c j", c=i)
                    ds.did(d.tensor_tensor(pv, ublk[:, 0:i, 0:i],
                                           nblk[:, 0:i, i].unsqueeze(1).to_broadcast([P, i, i]), ALU.mult))
                    ds.wait()
                    t = d.tensor_reduce(ublk[:, 0:i, i], pv, AX.X, ALU.add)
                    if i < BLK - 1:
                        ds.did(t)
                        ds.wait()
                    else:
                        t.then_inc(s["base_done"], 1)
                d.wait_ge(s["base_done"], n * 2 + 1)
                d.tensor_copy(tblk[:].rearrange("p i c -> p c i"), ublk[:]).then_inc(s["base_done"], 1)
                for step in (1, 4):
                    for g in range(4):
                        ms = slice(4 * g, 4 * g + 4)
                        filled_b(d, n, MERGE + 4 * step + g)
                        d.tensor_tensor(U1[:, ms], ring_b[g][:].rearrange("p (m i) -> p m i", m=4),
                                        (U0 if step == 1 else U1)[:, ms], ALU.add).then_inc(drained_b[g], 1)
                for c in range(CH):
                    for b in range(B):
                        u = b * CH + c
                        if c:
                            j = RJ["state", u]
                            filled_b(d, n, j)
                            for r in range(R):
                                t = d.scalar_tensor_tensor(w_[:, b, r], ring_b[j % 4][:, r * D:(r + 1) * D],
                                                           sc[:, S_NEG, u, r:r + 1], v[:, u * R + r],
                                                           ALU.mult, ALU.add)
                            t.then_inc(s["w_done"], 1)
                    if c < CH - 1:
                        for b in range(B):
                            u = b * CH + c
                            j = RJ["solve", u]
                            filled_b(d, n, j)
                            d.tensor_tensor(vd[:, b], ring_b[j % 4][:, 0:256].rearrange("p (r d) -> p r d", r=R),
                                            sc[:, S_BK, u].unsqueeze(2).to_broadcast([P, R, D]), ALU.mult
                                            ).then_inc(s["vd_done"], 1)
                    for b in range(B):
                        u = b * CH + c
                        j = RJ["local", u]
                        filled_b(d, n, j)
                        cu = core[:, u * R:(u + 1) * R].rearrange("p r d -> p (r d)")
                        if c:
                            drained(d, drained_b, JOBS_B, n, RJ["state", u])
                            t = d.tensor_tensor(cu, ring_b[j % 4][:, 0:256], qs[:, b].rearrange("p r d -> p (r d)"),
                                                ALU.add)
                        else:
                            t = d.tensor_copy(cu, ring_b[j % 4][:, 0:256])
                        t.then_inc(drained_b[j % 4], 1)
                    if c < CH - 1:
                        for b in range(B):
                            u = b * CH + c
                            j = RJ["update", u]
                            filled_b(d, n, j)
                            if c:
                                drained(d, drained_b, JOBS_B, n, RJ["update", u - 1])
                                for r in range(R):
                                    t = d.scalar_tensor_tensor(st[:, b, r * D:(r + 1) * D],
                                                               st[:, b, r * D:(r + 1) * D],
                                                               sc[:, S_EGL, u, r:r + 1],
                                                               ring_b[j % 4][:, r * D:(r + 1) * D],
                                                               ALU.mult, ALU.add)
                            else:
                                t = d.tensor_copy(st[:, b], ring_b[j % 4][:, 0:256])
                            t.then_inc(drained_b[j % 4], 1)
                for b in range(B):
                    drained(d, drained_b, JOBS_B, n, RJ["local", b * CH + CH - 1])
                for g in range(4):
                    d.tensor_tensor(core[:, 4 * g:4 * g + 4], core[:, 4 * g:4 * g + 4], gz[:, 4 * g:4 * g + 4],
                                    ALU.mult).then_inc(s["x_gated"], 1)
                for g in range(4):
                    d.wait_ge(s["sq2_done"], n * 4 + g + 1)
                    d.tensor_reduce(ss[:, 4 * g:4 * g + 4], sq[:, g % 2].rearrange("p (u d) -> p u d", d=D), AX.X,
                                    ALU.add).then_inc(s["ss2_done"], 1)
                d.wait_ge(s["rr2_done"], n + 1)
                for g in range(4):
                    d.tensor_tensor(core[:, 4 * g:4 * g + 4], core[:, 4 * g:4 * g + 4],
                                    rr[:, 4 * g:4 * g + 4].unsqueeze(2).to_broadcast([P, 4, D]), ALU.mult
                                    ).then_inc(s["x_scaled"], 1)
                for g in range(4):
                    filled_b(d, n, OUTJ + g)
                    au = acc[:, 2 * g:2 * g + 2].rearrange("p u h -> p (u h)")
                    d.tensor_tensor(au, au, ring_b[g][:], ALU.add).then_inc(drained_b[g], 1)
                assert ds.k == DVE_STEPS, ds.k

            ep = Steps(d, s["ep_dve"])
            for g in range(4):
                d.wait_ge(drained_b[g], NK * (JOBS_B // 4) + 1)
            t = d.tensor_copy(comb[:, :, E:FT], ones[:, 0:UNITS * 2].rearrange("p (u e) -> p u e", e=2))
            t.then_inc(s["ep_drained"], 1)
            d.wait_ge(s["ep_drained"], 1)

            def pool_turn(k):
                def wait():
                    d.wait_ge(s["ep_pool"], 2 * k)
                return wait
            norms = []
            norms.append(norm(d, None, ep, acc[:], acc[:], pool_turn(1)))
            ep.wait()
            ep.did(d.tensor_tensor(X[:], X[:], acc[:], ALU.add))
            ep.wait()
            norms.append(norm(d, None, ep, X[:], lin_x(), pool_turn(2)))
            assert ep.k == EP_XN2, ep.k
            for q in range(4):
                d.wait_ge(s["ep_pe"], q + 1)
                ep.did(d.tensor_copy(xnT[:, q // 2, (q % 2) * 512:(q % 2 + 1) * 512], bank[q][:]))
            d.wait_ge(s["ep_pe"], 5)
            lg = bank[4][:, 0:UNITS * E].rearrange("p (u e) -> p u e", e=E)

            def row(i):
                return best[:, i].unsqueeze(2).to_broadcast([P, UNITS, E])
            ep.did(d.tensor_reduce(best[:, 0], lg, AX.X, ALU.max))
            ep.wait()
            ep.did(d.tensor_tensor(logits[:], lg, row(0), ALU.subtract))
            assert ep.k == EP_EXP, ep.k
            d.wait_ge(s["ep_act"], 1)
            ep.did(d.tensor_reduce(best[:, 1], probs[:], AX.X, ALU.add))
            ep.wait()
            ep.did(d.reciprocal(best[:, 1], best[:, 1]))
            ep.wait()
            ep.did(d.tensor_tensor(probs[:], probs[:], row(1), ALU.mult))
            ep.wait()
            src = probs
            for i, pick in enumerate((first, second)):
                ep.did(d.tensor_reduce(best[:, i], src[:], AX.X, ALU.max))
                ep.wait()
                ep.did(d.tensor_tensor(pick[:], src[:], row(i), ALU.is_equal))
                ep.wait()
                ep.did(d.tensor_tensor(pick[:], pick[:], rank_w[:].unsqueeze(1).to_broadcast([P, UNITS, E]), ALU.mult))
                ep.wait()
                ep.did(d.tensor_reduce(best[:, 2], pick[:], AX.X, ALU.max))
                ep.wait()
                ep.did(d.tensor_tensor(pick[:], pick[:], row(2), ALU.is_equal))
                ep.wait()
                if i == 0:
                    src = logits
                    ep.did(d.scalar_tensor_tensor(logits[:], first[:], -2.0, probs[:], ALU.mult, ALU.add))
                    ep.wait()
            ep.did(d.tensor_tensor(best[:, 3], best[:, 0], best[:, 1], ALU.add))
            ep.wait()
            ep.did(d.reciprocal(best[:, 3], best[:, 3]))
            ep.did(d.tensor_tensor(first[:], first[:], row(0), ALU.mult))
            ep.did(d.tensor_tensor(second[:], second[:], row(1), ALU.mult))
            ep.wait()
            ep.did(d.tensor_tensor(first[:], first[:], second[:], ALU.add))
            ep.wait()
            ep.did(d.tensor_tensor(comb[:, :, 0:E], first[:], row(3), ALU.mult))
            ep.wait()
            ep.did(d.tensor_scalar(comb[:], comb[:], 0.5, None, ALU.mult))
            ep.wait()
            assert ep.k == EP_COMB, ep.k
            with d.Fori(0, UNITS) as u:
                d.wait_ge(s["f_gu"], u * 3 + 1)
                d.wait_ge(s["f_hs"], u * 3 + 1)
                d.tensor_copy(comb_u[:], comb[:, bass.ds(u, 1), :].rearrange("p a e -> p (a e)")).then_inc(s["comb_ready"], 1)
                d.tensor_copy(xt, xnT[:, :, bass.ds(u * P, P)]).then_inc(s["f_xt"], 1)
                for q, (c0, cw) in enumerate(FCHUNKS):
                    d.wait_ge(s["f_tanh"], u * 3 + q + 1)
                    d.wait_ge(s["f_tr"], u * 3 + 1)
                    hq = hid[:, c0:c0 + cw]
                    d.scalar_tensor_tensor(hq, thf[:, c0:c0 + cw], 1.0, bank[2 * (q % 2)][:, 0:cw], ALU.add, ALU.mult
                                           ).then_inc(s["f_gated"], 1)
                    d.wait_ge(s["f_gated"], u * 3 + q + 1)
                    d.tensor_tensor(hq, hq, bank[2 * (q % 2) + 1][:, 0:cw], ALU.mult).then_inc(s["f_h"], 1)
                    d.wait_ge(s["f_h"], u * 3 + q + 2)
                    if q == 0:
                        d.wait_ge(s["comb_ready"], u + 1)
                    h3 = hq.rearrange("p (e h) -> p e h", h=P)
                    d.tensor_tensor(h3, h3, comb_u[:, c0 // P:(c0 + cw) // P].unsqueeze(2).to_broadcast([P, cw // P, P]),
                                    ALU.mult).then_inc(s["f_hs"], 1)
                d.wait_ge(s["f_down"], u + 2)
                d.tensor_copy(acc[:, bass.ds(u, 1), :].rearrange("p a h -> p (a h)"), bank[6][:, 0:H]
                              ).then_inc(s["f_y"], 1)
            d.wait_ge(s["f_y"], UNITS + 1)
            norms.append(norm(d, None, ep, acc[:], acc[:], pool_turn(3)))
            ep.wait()
            d.tensor_tensor(X[:], X[:], acc[:], ALU.add).then_inc(s["layer_done"], 1)
            assert tuple(norms) == EP_NORMS, norms


_INS = ["L0_attn_hidden_states", "L0_attn_W_qkvz", "L0_attn_W_ba", "L0_attn_conv_weight", "L0_attn_A_log",
        "L0_attn_dt_bias", "L0_attn_norm_weight", "L0_attn_W_out", "L0_ffn_router_w", "L0_ffn_w_gate",
        "L0_ffn_w_up", "L0_ffn_w_down", "L0_ffn_sw_gate", "L0_ffn_sw_up", "L0_ffn_sw_down"]


def kernel(**inputs):
    import numpy as np
    import concourse.bacc as bacc
    from concourse.bass_utils import run_bass_kernel_spmd

    nc = bacc.Bacc("TRN2", target_bir_lowering=False, num_devices=1)
    arrays, args = {}, []
    for name in _INS:
        a = np.ascontiguousarray(inputs[name])
        arrays[name + "_dram"] = a
        args.append(nc.dram_tensor(name + "_dram", a.shape, mybir.dt.from_np(a.dtype), kind="ExternalInput").ap())
    args.append(nc.dram_tensor("out_dram", (B, S, H), F32, kind="ExternalOutput").ap())
    args.append(nc.dram_tensor("decay_rows", (NV, UNITS * P), F32, kind="Internal").ap())
    args.append(nc.dram_tensor("raw_blocks", (NB, M, BLK, BLK), F32, kind="Internal").ap())
    args.append(nc.dram_tensor("inv_blocks", (2, NB, M, BLK, BLK), F32, kind="Internal").ap())
    build(nc, *args)
    r = run_bass_kernel_spmd(nc, [arrays], core_ids=[0])
    return r.results[0]["out_dram"]
```

```python
from contextlib import ExitStack

import concourse.bass as bass
from concourse import mybir

F32 = mybir.dt.float32
ALU = mybir.AluOpType
ACT = mybir.ActivationFunctionType
AX = mybir.AxisListType

P = 128
NK, R, D = 16, 2, 128
NV = NK * R
B, S, H = 2, 512, 256
UNITS = B * S // P
CH = S // P
KT = H // P
M = UNITS * R
HW = 2 * D + 2 * R * D
TAPS = 4
BLK = 16
NB = P // BLK
E, FH, FS = 8, 128, 256
FW = E * FH + FS
FT = FW // P
LN_EPS, RMS_EPS, L2_EPS = 1e-5, 1e-6, 1e-6

PROJ, TR_QK, BACK, TR_V, GRAM, ZJ, JOBS_A = 0, 8, 12, 16, 20, 24, 28
MERGE, RECUR, XT, OUTJ, JOBS_B = 0, 32, 60, 64, 68
S_G, S_NEG, S_EG, S_EGL, S_BETA, S_BK, S_NBETA, NSC = 0, 1, 2, 3, 4, 5, 6, 7


FCHUNKS = ((0, 512), (512, 512), (1024, 256))
PRO_NORM, PRO_ABS, PRO_G, PRO_DVE = 5, 13, 17, 22
PRO_POOL, PRO_ACT = 5 + 2 + 6 + E + 5 + 6, 6
CONV_STEPS, BASE_STEPS, RR_STEPS = 2 * 8, 2 * BLK - 4, 2
EP_NORMS, EP_XN2, EP_EXP, EP_COMB = (5, 12, 45), 13, 19, 40
EP_LOADS = 16 * (8 + 2 + 1)


def recurrence_jobs():
    job, k = {}, RECUR
    for c in range(CH):
        for kind in ("state", "solve", "local", "update"):
            if (kind == "state" and c == 0) or (kind == "update" and c == CH - 1):
                continue
            for b in range(B):
                job[kind, b * CH + c] = k
                k += 1
    assert k == XT
    return job


RJ = recurrence_jobs()


class Steps:

    def __init__(self, eng, sem, base=0):
        self.eng, self.sem, self.base, self.k = eng, sem, base, 0

    def did(self, ins):
        ins.then_inc(self.sem, 1)
        self.k += 1
        return self.k

    def wait(self, k=None):
        self.eng.wait_ge(self.sem, self.base + (self.k if k is None else k))


def build(nc, x_in, w_qkvz, w_ba, conv_w, a_log, dt_bias, norm_w, w_out, router_w, w_gate, w_up, w_down,
          sw_gate, sw_up, sw_down, out, decay_rows, raw_blocks, inv_blocks):
    xf = x_in.rearrange("b (c p) h -> p (b c) h", p=P)
    of = out.rearrange("b (c p) h -> p (b c) h", p=P)

    with ExitStack() as ctx:
        def sb(name, shape):
            return ctx.enter_context(nc.sbuf_tensor(name, shape, F32))

        def sem(name):
            return ctx.enter_context(nc.semaphore(name))

        bank = [ctx.enter_context(nc.psum_tensor(f"bank{i}", [P, 512], F32)) for i in range(8)]
        ring_a, ring_b = bank[:4], bank[4:]

        ident = sb("ident", [P, P])
        upper = sb("upper", [P, P])
        merge16 = sb("merge16", [P, P])
        merge32 = sb("merge32", [P, P])
        ones = sb("ones", [P, P])
        minus_half = sb("minus_half", [P, M])
        l2_consts = sb("l2_consts", [P, 2, M])
        rms_consts = sb("rms_consts", [P, 2, M])
        rank_w = sb("rank_w", [P, E])
        X = sb("X", [P, UNITS, H])
        acc = sb("acc", [P, UNITS, H])
        xnT = sb("xnT", [P, KT, UNITS * P])
        scal = sb("scal", [P, NSC, UNITS, NV])
        convT = sb("convT", [P, TAPS, 64])
        normw = sb("normw", [P, 1])
        Wqk = sb("Wqk", [P, KT, 2 * D])
        Wv = sb("Wv", [P, KT, R * D])
        Wz = sb("Wz", [P, KT, R * D])
        Wo = sb("Wo", [P, R, H])
        taps_qk = sb("taps_qk", [P, TAPS, 2])
        taps_v = sb("taps_v", [P, TAPS, R])
        sc_a = sb("sc_a", [P, NSC, UNITS, R])
        sc_b = sb("sc_b", [P, NSC, UNITS, R])
        y = sb("y", [P, 8, 512])
        th = sb("th", [P, 2, 512])
        sq = sb("sq", [P, 2, 512])
        ss = sb("ss", [P, M])
        rr = sb("rr", [P, M])
        ss_out = sb("ss_out", [P, M])
        rr_out = sb("rr_out", [P, M])
        qhat = sb("qhat", [P, UNITS, D])
        khat = sb("khat", [P, UNITS, D])
        kqT = sb("kqT", [P, UNITS, 2, P])
        v = sb("v", [P, M, D])
        gz = sb("gz", [P, M, D])
        dec = sb("dec", [P, M, P])
        decn = sb("decn", [P, M, P])
        attn = sb("attn", [P, M, P])
        nmat = sb("nmat", [P, M, P])
        n16 = sb("n16", [P, M, P])
        n32 = decn
        nblk = sb("nblk", [P, BLK, BLK])
        ublk = sb("ublk", [P, BLK, BLK])
        tblk = sb("tblk", [P, BLK, BLK])
        prod = sb("prod", [P, BLK * BLK])
        UT0 = sb("UT0", [P, 2, M, P])
        U0, T0 = UT0[:, 0], UT0[:, 1]
        Xm = sb("Xm", [P, M, P])
        U1 = sb("U1", [P, M, P])
        T1 = sb("T1", [P, M, P])
        U2 = U1
        st = sb("st", [P, B, R * D])
        w_ = sb("w_", [P, B, R, D])
        vn = sb("vn", [P, B, R, D])
        vd = sb("vd", [P, B, R, D])
        qs = sb("qs", [P, B, R, D])
        core = Xm
        xT = T1
        sq_out = (w_, vd)
        lin = gz
        mean = sb("mean", [P, UNITS])
        rstd = sb("rstd", [P, UNITS])

        FG = y[:].rearrange("p a b -> p (a b)")[:, 0:KT * FW].rearrange("p (k c) -> p k c", k=KT)
        FU = UT0[:].rearrange("p a b c -> p (a b c)")[:, 0:KT * FW].rearrange("p (k c) -> p k c", k=KT)
        FD = sb("FD", [P, FT, H])
        router = sb("router", [P, KT, E])
        def lin_x():
            return v[:].rearrange("p a b -> p (a b)").rearrange("p (u h) -> p u h", u=UNITS)

        xt = kqT[:, 0]
        hid = nmat[:].rearrange("p a b -> p (a b)")[:, 0:FW]
        thf = n16[:].rearrange("p a b -> p (a b)")[:, 0:FW]
        hT = attn[:, 0:FT]
        logits = sb("logits", [P, UNITS, E])
        probs = sb("probs", [P, UNITS, E])
        first = sb("first", [P, UNITS, E])
        second = sb("second", [P, UNITS, E])
        best = sb("best", [P, 4, UNITS])
        comb = sb("comb", [P, UNITS, FT])
        comb_u = sb("comb_u", [P, FT])

        s = {n: sem(n) for n in (
            "x_loaded", "params_loaded", "rows_stored", "wqk_loaded", "wv_loaded", "wz_loaded", "rows_loaded", "wo_loaded",
            "raw_stored", "raw_loaded", "inv_stored", "t0_loaded", "u0_loaded",
            "filled_a", "filled_b", "pro_filled", "pro_dve", "pro_act", "pro_pool", "gates_ready",
            "taps_qk_ready", "taps_v_ready", "sc_a_ready", "sc_b_ready", "tap_done", "tanh_done", "act_done", "sq_done", "ss_done", "rr_done",
            "z_tanh", "dg_done", "exp_done", "dec_done", "decn_done", "n_ready", "base_done",
            "w_done", "vd_done", "x_gated", "sq2_done", "ss2_done", "rr2_done", "x_scaled",
            "conv_step", "base_step", "rr_step", "rr_out_step",
            "ep_dve", "ep_act", "ep_pool", "ep_pe", "ep_w_loaded", "ep_drained", "out_stored",
            "f_xt", "f_gu", "f_tanh", "f_h", "f_hs", "f_tr", "f_hT", "f_down", "f_y", "f_gated", "comb_ready", "layer_done")}
        drained_a = [sem(f"drained_a{i}") for i in range(4)]
        drained_b = [sem(f"drained_b{i}") for i in range(4)]
        blk = ctx.enter_context(nc.Block())

        def filled_a(eng, n, j):
            eng.wait_ge(s["filled_a"], n * JOBS_A + j + 2)

        def filled_b(eng, n, j):
            eng.wait_ge(s["filled_b"], n * JOBS_B + j + 2)

        def drained(eng, ring, jobs, n, j):
            eng.wait_ge(ring[j % 4], n * (jobs // 4) + j // 4 + 2)

        def free(eng, ring, jobs, n, j):
            eng.wait_ge(ring[j % 4], n * (jobs // 4) + j // 4 + 1)

        def tap_of(t, j):
            return (taps_qk if j < 4 else taps_v)[:, t, (j // 2) % 2:(j // 2) % 2 + 1]

        @blk.sync
        def _(sp):
            sp.dma_start(X[:], xf).then_inc(s["x_loaded"], 16)
            sp.dma_start(U1[:, 0, :].rearrange("p (k c) -> p k c", k=KT), w_ba.rearrange("(k p) c -> p k c", p=P)
                         ).then_inc(s["params_loaded"], 16)
            sp.dma_start(U1[:, 1, 0:NV], a_log.rearrange("(a h) -> a h", a=1).to_broadcast([P, NV])
                         ).then_inc(s["params_loaded"], 16)
            sp.dma_start(U1[:, 1, NV:2 * NV], dt_bias.rearrange("(a h) -> a h", a=1).to_broadcast([P, NV])
                         ).then_inc(s["params_loaded"], 16)
            sp.dma_start(T1[0:64, 0:TAPS, :].rearrange("t a p -> t (a p)"),
                         conv_w.rearrange("(t p) a -> t (p a)", p=P)).then_inc(s["params_loaded"], 16)
            sp.dma_start(normw[:], norm_w.rearrange("(p a) -> p a", a=1)).then_inc(s["params_loaded"], 16)
            sp.wait_ge(s["gates_ready"], 1)
            sp.dma_start(decay_rows, Xm[0:NV, 0:UNITS, :].rearrange("h u i -> h (u i)")
                         ).then_inc(s["rows_stored"], 16)
            sp.wait_ge(s["rows_stored"], 16)

            def columns(h, at, width):
                return w_qkvz[:, bass.ds(h * HW + at, width)].rearrange("(k p) c -> p k c", p=P)

            def load_qk(h, first=False):
                if not first:
                    sp.wait_ge(s["filled_a"], h * JOBS_A - JOBS_A + PROJ + 5)
                sp.dma_start(Wqk[:], columns(h, 0, 2 * D)).then_inc(s["wqk_loaded"], 16)

            def load_v(h, first=False):
                if not first:
                    sp.wait_ge(s["filled_a"], h * JOBS_A - JOBS_A + PROJ + 9)
                sp.dma_start(Wv[:], columns(h, 2 * D, R * D)).then_inc(s["wv_loaded"], 16)

            def load_z(h, first=False):
                if not first:
                    sp.wait_ge(s["filled_a"], h * JOBS_A + 1)
                sp.dma_start(Wz[:], columns(h, 2 * D + R * D, R * D)).then_inc(s["wz_loaded"], 16)

            def load_rows(h, first=False):
                if not first:
                    sp.wait_ge(s["n_ready"], h * 8 + 1)
                for r in range(R):
                    sp.dma_start(dec[:].rearrange("p (u r) i -> p u r i", r=R)[:, :, r, :],
                                 decay_rows[bass.ds(h * R + r, 1), :].rearrange("h (u i) -> h u i", u=UNITS)
                                 .to_broadcast([P, UNITS, P])).then_inc(s["rows_loaded"], 16)

            def load_wo(h, first=False):
                if not first:
                    sp.wait_ge(s["filled_b"], h * JOBS_B + 1)
                sp.dma_start(Wo[:], w_out[bass.ds(h * R * D, R * D), :].rearrange("(r p) c -> p r c", p=P)
                             ).then_inc(s["wo_loaded"], 16)

            def blocks(h):
                for g in range(4):
                    drained(sp, drained_a, JOBS_A, h, GRAM + g)
                for k in range(NB):
                    sp.dma_start(raw_blocks[k].rearrange("m j i -> j m i"),
                                 nmat[k * BLK:(k + 1) * BLK, :, k * BLK:(k + 1) * BLK]
                                 ).then_inc(s["raw_stored"], 16)
                sp.wait_ge(s["raw_stored"], (h + 1) * 16 * NB)
                sp.dma_start(nblk[:], raw_blocks.rearrange("k m j i -> (k m) j i")).then_inc(s["raw_loaded"], 16)
                sp.wait_ge(s["base_done"], (h + 1) * 2)
                sp.dma_start(inv_blocks[1].rearrange("k m c i -> (k m) c i"), tblk[:]).then_inc(s["inv_stored"], 16)
                sp.dma_start(inv_blocks[0].rearrange("k m c i -> (k m) c i"), ublk[:]).then_inc(s["inv_stored"], 16)
                sp.wait_ge(s["inv_stored"], (h + 1) * 32)
                for i, dst, said in ((1, T0, "t0_loaded"), (0, U0, "u0_loaded")):
                    for k in range(NB):
                        sp.dma_start(dst[k * BLK:(k + 1) * BLK, :, k * BLK:(k + 1) * BLK],
                                     inv_blocks[i, k].rearrange("m c i -> c m i")).then_inc(s[said], 16)

            def body(n, more, most):
                if more:
                    load_v(n + 1)
                    load_rows(n + 1)
                if most:
                    load_qk(n + 2)
                if more:
                    load_z(n + 1)
                    blocks(n + 1)
                    load_wo(n + 1)

            load_qk(0, True)
            load_rows(0, True)
            load_v(0, True)
            load_z(0, True)
            load_wo(0, True)
            load_qk(1)
            blocks(0)
            with sp.Fori(0, NK - 2) as n:
                body(n, True, True)
            body(NK - 2, True, False)
            sp.wait_ge(s["filled_a"], NK * JOBS_A + 1)
            sp.wait_ge(s["filled_b"], (NK - 1) * JOBS_B + RECUR + 2)
            for t, we, ws in ((FG, w_gate, sw_gate), (FU, w_up, sw_up)):
                for k in range(KT):
                    sp.dma_start(t[:, k, 0:E * FH].rearrange("p (e h) -> p e h", e=E),
                                 we[:, k * P:(k + 1) * P, :].rearrange("e p h -> p e h")
                                 ).then_inc(s["ep_w_loaded"], 16)
                    sp.dma_start(t[:, k, E * FH:FW], ws[k * P:(k + 1) * P, :]).then_inc(s["ep_w_loaded"], 16)
            sp.dma_start(FD[:, 0:E, :], w_down.rearrange("e p d -> p e d")).then_inc(s["ep_w_loaded"], 16)
            sp.dma_start(FD[:, E:FT, :], sw_down.rearrange("(t p) d -> p t d", p=P)).then_inc(s["ep_w_loaded"], 16)
            sp.dma_start(router[:],
                         router_w.rearrange("(k p) e -> p k e", p=P)).then_inc(s["ep_w_loaded"], 16)
            sp.wait_ge(s["layer_done"], 1)
            sp.dma_start(of, X[:]).then_inc(s["out_stored"], 16)
            sp.wait_ge(s["out_stored"], 16)

        def norm(dve, act_sq, steps, src, dst, pool_wait):
            steps.did(dve.tensor_reduce(mean[:], src, AX.X, ALU.add))
            steps.wait()
            steps.did(dve.tensor_scalar(mean[:], mean[:], 1.0 / H, None, ALU.mult))
            steps.wait()
            steps.did(dve.tensor_tensor(dst, src, mean[:].unsqueeze(2).to_broadcast([P, UNITS, H]), ALU.subtract))
            steps.wait()
            flat = lin[:].rearrange("p a b -> p (a b)").rearrange("p (u h) -> p u h", u=UNITS)
            steps.did(dve.tensor_tensor(flat, dst, dst, ALU.mult))
            steps.wait()
            k = steps.did(dve.tensor_reduce(rstd[:], flat, AX.X, ALU.add))
            pool_wait()
            steps.did(dve.tensor_tensor(dst, dst, rstd[:].unsqueeze(2).to_broadcast([P, UNITS, H]), ALU.mult))
            return k


        @blk.gpsimd
        def _(po):
            po.sem_inc(s["n_ready"])
            st_ = Steps(po, s["pro_pool"])
            st_.did(po.memset(ident[:], 0.0))
            st_.did(po.memset(ones[:], 1.0))
            st_.did(po.memset(merge16[:], 0.0))
            st_.did(po.memset(merge32[:], 0.0))
            st_.did(po.memset(minus_half[:], -0.5))
            st_.wait()
            st_.did(po.affine_select(out=ident[:], in_=ident[:], compare_op=ALU.not_equal, fill=1.0, base=0,
                                     pattern=[[-1, P]], channel_multiplier=1))
            st_.did(po.affine_select(out=upper[:], in_=ones[:], compare_op=ALU.is_ge, fill=0.0, base=0,
                                     pattern=[[1, P]], channel_multiplier=-1))
            for m_, size in ((merge16, 16), (merge32, 32)):
                half = m_[:].rearrange("p (b h l) -> p b h l", h=2, l=size)[:, :, 1, :]
                nb = P // (2 * size)
                st_.did(po.memset(half, 1.0))
                st_.wait()
                st_.did(po.affine_select(out=half, in_=half, compare_op=ALU.is_ge, fill=0.0, base=0,
                                         pattern=[[-2 * size, nb], [0, size]], channel_multiplier=1))
                st_.wait()
                st_.did(po.affine_select(out=half, in_=half, compare_op=ALU.is_ge, fill=0.0, base=size - 1,
                                         pattern=[[2 * size, nb], [0, size]], channel_multiplier=-1))
            for e in range(E):
                st_.did(po.memset(rank_w[:, e:e + 1], float(E - e)))
            st_.did(po.memset(U0, 0.0))
            st_.did(po.memset(T0, 0.0))
            st_.did(po.memset(ublk[:], 0.0))
            st_.did(po.memset(acc[:], 0.0))
            for t, value in ((l2_consts[:, 0, 0:UNITS], D), (l2_consts[:, 0, UNITS:M], 1.0),
                             (l2_consts[:, 1, 0:UNITS], 4 * D * L2_EPS), (l2_consts[:, 1, UNITS:M], 4 * L2_EPS),
                             (rms_consts[:, 0], 1.0 / D), (rms_consts[:, 1], 4 * RMS_EPS)):
                st_.did(po.memset(t, float(value)))
            st_.wait()
            st_.did(po.memset(ublk[:].rearrange("p a b -> p (a b)")[:, 0:BLK * BLK:BLK + 1], 1.0))
            assert st_.k == PRO_POOL, st_.k
            po.wait_ge(s["pro_dve"], PRO_NORM)
            st_.did(po.tensor_scalar(rstd[:], rstd[:], 1.0 / H, LN_EPS, ALU.mult, ALU.add))
            st_.wait()
            st_.did(po.tensor_tensor(rstd[:], rstd[:], minus_half[:, 0:UNITS], ALU.pow))
            po.wait_ge(s["pro_dve"], PRO_DVE)
            po.wait_ge(s["pro_act"], PRO_ACT)

            def head_scalars(h, dst, said):
                po.tensor_copy(dst[:], scal[:, :, :, bass.ds(h * R, R)]).then_inc(s[said], 1)

            def head_taps_qk(h):
                po.tensor_copy(taps_qk[:, :, 0], convT[:, :, bass.ds(h, 1)].rearrange("p t a -> p (t a)"))
                po.tensor_copy(taps_qk[:, :, 1], convT[:, :, bass.ds(h + NK, 1)].rearrange("p t a -> p (t a)")
                               ).then_inc(s["taps_qk_ready"], 1)

            def head_taps_v(h):
                po.tensor_copy(taps_v[:], convT[:, :, bass.ds(h * R + 2 * NK, R)]).then_inc(s["taps_v_ready"], 1)

            def decays(h, n=None):
                po.wait_ge(s["exp_done"], h + 1)
                po.tensor_tensor(dec[:], dec[:], upper[:].unsqueeze(1).to_broadcast([P, M, P]), ALU.mult
                                 ).then_inc(s["dec_done"], 1)
                po.wait_ge(s["dec_done"], h + 1)
                if n is not None:
                    filled_b(po, n, MERGE + 15)
                po.wait_ge(s["sc_a_ready"], h + 1)
                po.tensor_tensor(decn[:], dec[:],
                                 sc_a[:, S_NBETA].rearrange("p u r -> p (u r)").unsqueeze(2).to_broadcast([P, M, P]),
                                 ALU.mult).then_inc(s["decn_done"], 1)

            def rsqrt(h, sums, done, said, dst, consts, stepped):
                ps = Steps(po, s[stepped], h * RR_STEPS)
                po.wait_ge(s[done], h * 4 + 5)
                ps.did(po.tensor_tensor(dst[:], sums[:], consts[:, 0], ALU.mult))
                ps.wait()
                ps.did(po.tensor_tensor(dst[:], dst[:], consts[:, 1], ALU.add))
                ps.wait()
                po.tensor_tensor(dst[:], dst[:], minus_half[:], ALU.pow).then_inc(s[said], 1)

            def qk_rsqrt(h):
                rsqrt(h, ss, "ss_done", "rr_done", rr, l2_consts, "rr_step")

            def out_rsqrt(h):
                rsqrt(h, ss_out, "ss2_done", "rr2_done", rr_out, rms_consts, "rr_out_step")

            def n_parts(h, dst, mask):
                for g in range(4):
                    ms = slice(4 * g, 4 * g + 4)
                    po.tensor_tensor(dst[:, ms], nmat[:, ms], mask[:].unsqueeze(1).to_broadcast([P, 4, P]),
                                     ALU.mult).then_inc(s["n_ready"], 1)

            def gate(n):
                for b_ in range(B):
                    drained(po, drained_b, JOBS_B, n, RJ["local", b_ * CH + CH - 1])
                for g in range(4):
                    drained(po, drained_a, JOBS_A, n, ZJ + g)
                    ms = slice(4 * g, 4 * g + 4)
                    po.tensor_tensor(core[:, ms], core[:, ms], gz[:, ms], ALU.mult).then_inc(s["x_gated"], 1)

            def scale_out(n):
                po.wait_ge(s["rr2_done"], n + 1)
                for g in range(4):
                    ms = slice(4 * g, 4 * g + 4)
                    po.tensor_tensor(core[:, ms], core[:, ms], rr_out[:, ms].unsqueeze(2).to_broadcast([P, 4, D]),
                                     ALU.mult).then_inc(s["x_scaled"], 1)

            def body(n, more, most):
                if more:
                    head_scalars(n + 1, sc_a, "sc_a_ready")
                    head_taps_v(n + 1)
                if most:
                    for j in range(4):
                        drained(po, drained_a, JOBS_A, n + 1, PROJ + j)
                    head_taps_qk(n + 2)
                if more:
                    decays(n + 1, n)
                    qk_rsqrt(n + 1)
                gate(n)
                if more:
                    head_scalars(n + 1, sc_b, "sc_b_ready")
                    for g in range(4):
                        drained(po, drained_a, JOBS_A, n + 1, GRAM + g)
                    n_parts(n + 1, n16, merge16)
                out_rsqrt(n)
                scale_out(n)
                if more:
                    n_parts(n + 1, n32, merge32)

            head_taps_qk(0)
            head_taps_v(0)
            head_scalars(0, sc_a, "sc_a_ready")
            head_scalars(0, sc_b, "sc_b_ready")
            for j in range(4):
                drained(po, drained_a, JOBS_A, 0, PROJ + j)
            head_taps_qk(1)
            decays(0)
            qk_rsqrt(0)
            for g in range(4):
                drained(po, drained_a, JOBS_A, 0, GRAM + g)
            n_parts(0, n16, merge16)
            n_parts(0, n32, merge32)
            with po.Fori(0, NK - 2) as n:
                body(n, True, True)
            body(NK - 2, True, False)
            body(NK - 1, False, False)
            ep = Steps(po, s["ep_pool"])
            for done in EP_NORMS:
                po.wait_ge(s["ep_dve"], done)
                ep.did(po.tensor_scalar(rstd[:], rstd[:], 1.0 / H, LN_EPS, ALU.mult, ALU.add))
                ep.wait()
                ep.did(po.tensor_tensor(rstd[:], rstd[:], minus_half[:, 0:UNITS], ALU.pow))


        @blk.tensor
        def _(pe):
            for name in ("filled_a", "filled_b", "f_gu", "f_tr", "f_down"):
                pe.sem_inc(s[name])
            pe.wait_ge(s["pro_pool"], PRO_POOL)
            pe.wait_ge(s["pro_dve"], PRO_NORM + 1)
            for q in range(4):
                k, hf = q // 2, q % 2
                for i in range(4):
                    mm = pe.transpose(bank[q][:, i * P:(i + 1) * P], lin_x()[:, hf * 4 + i, k * P:(k + 1) * P],
                                      ident[:])
                mm.then_inc(s["pro_filled"], 1)
            pe.wait_ge(s["params_loaded"], 80)
            for a in range(TAPS):
                mm = pe.transpose(bank[5][:, a * 64:(a + 1) * 64],
                                  T1[0:64, 0:TAPS, :].rearrange("t a p -> t (a p)")[:, a:TAPS * P:TAPS],
                                  ident[0:64, 0:64])
            mm.then_inc(s["pro_filled"], 1)
            pe.wait_ge(s["pro_dve"], PRO_NORM + 5)
            wba = U1[:, 0, :].rearrange("p (k c) -> p k c", k=KT)
            for u in range(UNITS):
                for k in range(KT):
                    mm = pe.matmul(bank[4][:, u * 64:(u + 1) * 64], xnT[:, k, u * P:(u + 1) * P], wba[:, k, :],
                                   start=(k == 0), stop=(k == KT - 1))
            mm.then_inc(s["pro_filled"], 1)
            pe.wait_ge(s["pro_dve"], PRO_G)
            g_ = U1[:, 2:4, :].rearrange("p a b -> p (a b)")
            pe.matmul(bank[6][:, 0:256], upper[:], g_, start=True, stop=True)
            pe.matmul(bank[6][:, 256:512], ones[:], g_, start=True, stop=True).then_inc(s["pro_filled"], 1)
            for u in range(UNITS):
                mm = pe.matmul(bank[u // 4][0:NV, (u % 4) * P:(u % 4 + 1) * P], g_[:, u * NV:(u + 1) * NV], upper[:],
                               start=True, stop=True)
            mm.then_inc(s["pro_filled"], 1)
            pe.wait_ge(s["pro_dve"], PRO_DVE)
            pe.wait_ge(s["pro_act"], PRO_ACT)

            def merge_step(n, step, g):
                j = MERGE + step * 4 + g
                out_ = ring_b[j % 4]
                free(pe, drained_b, JOBS_B, n, j)
                prev = j - 4
                if step:
                    drained(pe, drained_b, JOBS_B, n, prev)
                for i in range(4):
                    m = 4 * g + i
                    o = out_[:, i * P:(i + 1) * P]
                    if step == 0:
                        mm = pe.matmul(o, n16[:, m], T0[:, m], start=True, stop=True)
                    elif step == 1:
                        mm = pe.matmul(o, Xm[:, m], U0[:, m], start=True, stop=True)
                    elif step == 3:
                        mm = pe.matmul(o, n32[:, m], T1[:, m], start=True, stop=True)
                    elif step == 4:
                        mm = pe.matmul(o, Xm[:, m], U1[:, m], start=True, stop=True)
                    elif step in (2, 5):
                        mm = pe.transpose(o, U1[:, m], ident[:])
                    elif step == 6:
                        mm = pe.matmul(out_[:, i * 64:(i + 1) * 64], nmat[0:64, m], T1[0:64, m, 0:64],
                                       start=True, stop=True)
                    else:
                        mm = pe.matmul(out_[:, i * 64:(i + 1) * 64], Xm[64:P, m], U1[64:P, m, 64:P],
                                       start=True, stop=True)
                mm.then_inc(s["filled_b"], 1)


            def proj(h, j):
                ct, b = j // 2, j % 2
                if j == 0:
                    pe.wait_ge(s["wqk_loaded"], (h + 1) * 16)
                if j == 4:
                    pe.wait_ge(s["wv_loaded"], (h + 1) * 16)
                w = (Wqk if j < 4 else Wv)[:, :, (ct % 2) * P:(ct % 2 + 1) * P]
                free(pe, drained_a, JOBS_A, h, PROJ + j)
                for k in range(KT):
                    mm = pe.matmul(ring_a[j % 4][:], w[:, k], xnT[:, k, b * S:(b + 1) * S],
                                   start=(k == 0), stop=(k == KT - 1))
                mm.then_inc(s["filled_a"], 1)

            def z_by_token(h):
                pe.wait_ge(s["wz_loaded"], (h + 1) * 16)
                for g in range(4):
                    free(pe, drained_a, JOBS_A, h, ZJ + g)
                    for i in range(2):
                        u = 2 * g + i
                        for k in range(KT):
                            mm = pe.matmul(ring_a[g][:, i * 256:(i + 1) * 256], xnT[:, k, u * P:(u + 1) * P],
                                           Wz[:, k], start=(k == 0), stop=(k == KT - 1))
                    mm.then_inc(s["filled_a"], 1)

            def by_token(h, job, first):
                for i in range(4):
                    free(pe, drained_a, JOBS_A, h, job + i)
                    pe.wait_ge(s["act_done"], h * 8 + first + i + 2)
                    for t in range(4):
                        mm = pe.transpose(ring_a[i][:, t * P:(t + 1) * P], y[:, first + i, t * P:(t + 1) * P],
                                          ident[:])
                    mm.then_inc(s["filled_a"], 1)

            def back(h):
                for g in range(4):
                    for half in (TR_QK + g // 2, TR_QK + 2 + g // 2):
                        drained(pe, drained_a, JOBS_A, h, half)
                    if g not in (g // 2, 2 + g // 2):
                        free(pe, drained_a, JOBS_A, h, BACK + g)
                    for i in range(2):
                        for x_, src in enumerate((khat, qhat)):
                            c0 = (2 * i + x_) * P
                            mm = pe.transpose(ring_a[g][:, c0:c0 + P], src[:, 2 * g + i, :], ident[:])
                    mm.then_inc(s["filled_a"], 1)

            def gram(h):
                for g in range(4):
                    free(pe, drained_a, JOBS_A, h, GRAM + g)
                    for i in range(2):
                        u = 2 * g + i
                        mm = pe.matmul(ring_a[g][:, i * 256:(i + 1) * 256], kqT[:, u, 0, :],
                                       kqT[:, u].rearrange("p x i -> p (x i)"), start=True, stop=True)
                    mm.then_inc(s["filled_a"], 1)

            def recur(n, c):
                for b in range(B):
                    u = b * CH + c
                    if c:
                        j = RJ["state", u]
                        free(pe, drained_b, JOBS_B, n, j)
                        drained(pe, drained_b, JOBS_B, n, RJ["update", u - 1])
                        pe.matmul(ring_b[j % 4][:, 0:256], kqT[:, u, 0, :], st[:, b], start=True, stop=True)
                        pe.matmul(ring_b[j % 4][:, 256:512], kqT[:, u, 1, :], st[:, b], start=True, stop=True
                                  ).then_inc(s["filled_b"], 1)
                for b in range(B):
                    u = b * CH + c
                    j = RJ["solve", u]
                    free(pe, drained_b, JOBS_B, n, j)
                    if c:
                        pe.wait_ge(s["w_done"], n * (UNITS - B) + (c - 1) * B + b + 1)
                    elif b == 0:
                        for g in range(4):
                            drained(pe, drained_b, JOBS_B, n, MERGE + 28 + g)
                    for r in range(R):
                        rhs = w_[:, b, r] if c else v[:, u * R + r]
                        mm = pe.matmul(ring_b[j % 4][:, r * D:(r + 1) * D], U2[:, u * R + r], rhs,
                                       start=True, stop=True)
                    mm.then_inc(s["filled_b"], 1)
                for b in range(B):
                    u = b * CH + c
                    j = RJ["local", u]
                    free(pe, drained_b, JOBS_B, n, j)
                    drained(pe, drained_b, JOBS_B, n, RJ["solve", u])
                    for r in range(R):
                        mm = pe.matmul(ring_b[j % 4][:, r * D:(r + 1) * D], attn[:, u * R + r], vn[:, b, r],
                                       start=True, stop=True)
                    mm.then_inc(s["filled_b"], 1)
                for b in range(B):
                    u = b * CH + c
                    if c < CH - 1:
                        j = RJ["update", u]
                        free(pe, drained_b, JOBS_B, n, j)
                        pe.wait_ge(s["vd_done"], n * (UNITS - B) + c * B + b + 1)
                        pe.matmul(ring_b[j % 4][:, 0:256], khat[:, u], vd[:, b].rearrange("p r d -> p (r d)"),
                                  start=True, stop=True).then_inc(s["filled_b"], 1)

            def output(n):
                for g in range(4):
                    free(pe, drained_b, JOBS_B, n, XT + g)
                    pe.wait_ge(s["x_scaled"], n * 4 + g + 1)
                    for i in range(4):
                        mm = pe.transpose(ring_b[g][:, i * P:(i + 1) * P], core[:, 4 * g + i], ident[:])
                    mm.then_inc(s["filled_b"], 1)
                pe.wait_ge(s["wo_loaded"], (n + 1) * 16)
                for g in range(4):
                    drained(pe, drained_b, JOBS_B, n, XT + g)
                    for i in range(2):
                        for r in range(R):
                            mm = pe.matmul(ring_b[g][:, i * 256:(i + 1) * 256], xT[:, 4 * g + 2 * i + r], Wo[:, r],
                                           start=(r == 0), stop=(r == R - 1))
                    mm.then_inc(s["filled_b"], 1)

            def body(n, more, most):
                pe.wait_ge(s["n_ready"], (n + 1) * 8 + 1)
                pe.wait_ge(s["t0_loaded"], (n + 1) * 16 * NB)
                for step in range(8):
                    if step == 1:
                        pe.wait_ge(s["u0_loaded"], (n + 1) * 16 * NB)
                    for g in range(4):
                        merge_step(n, step, g)
                    if more and step in (0, 2, 4, 6):
                        proj(n + 1, 4 + step // 2)
                recur(n, 0)
                recur(n, 1)
                if more:
                    by_token(n + 1, TR_QK, 0)
                recur(n, 2)
                recur(n, 3)
                if more:
                    back(n + 1)
                    by_token(n + 1, TR_V, 4)
                    gram(n + 1)
                    z_by_token(n + 1)
                if most:
                    for j in range(4):
                        proj(n + 2, j)
                output(n)

            for j in range(8):
                proj(0, j)
            by_token(0, TR_QK, 0)
            back(0)
            by_token(0, TR_V, 4)
            gram(0)
            z_by_token(0)
            for j in range(4):
                proj(1, j)
            with pe.Fori(0, NK - 2) as n:
                body(n, True, True)
            body(NK - 2, True, False)
            body(NK - 1, False, False)

            pe.wait_ge(s["ep_dve"], EP_XN2)
            for q in range(4):
                k, hf = q // 2, q % 2
                for i in range(4):
                    mm = pe.transpose(bank[q][:, i * P:(i + 1) * P], lin_x()[:, hf * 4 + i, k * P:(k + 1) * P],
                                      ident[:])
                mm.then_inc(s["ep_pe"], 1)
            pe.wait_ge(s["ep_dve"], EP_XN2 + 4)
            pe.wait_ge(s["ep_w_loaded"], EP_LOADS)
            for u in range(UNITS):
                for k in range(KT):
                    mm = pe.matmul(bank[4][:, u * E:(u + 1) * E], xnT[:, k, u * P:(u + 1) * P],
                                   router[:, k, :], start=(k == 0), stop=(k == KT - 1))
            mm.then_inc(s["ep_pe"], 1)
            pe.wait_ge(s["ep_dve"], EP_COMB)
            with pe.Fori(0, UNITS) as u:
                pe.wait_ge(s["f_xt"], u + 1)
                for q, (c0, cw) in enumerate(FCHUNKS):
                    if q == 2:
                        pe.wait_ge(s["f_h"], u * 3 + 2)
                    elif q == 0:
                        pe.wait_ge(s["f_h"], u * 3 + 1)
                    else:
                        pe.wait_ge(s["f_h"], u * 3 + 1)
                    for x_, wt in enumerate((FG, FU)):
                        for k in range(KT):
                            mm = pe.matmul(bank[2 * (q % 2) + x_][:, 0:cw], xt[:, k, :], wt[:, k, c0:c0 + cw],
                                           start=(k == 0), stop=(k == KT - 1))
                    mm.then_inc(s["f_gu"], 1)
                for q, (c0, cw) in enumerate(FCHUNKS):
                    pe.wait_ge(s["f_hs"], u * 3 + q + 2)
                    pe.wait_ge(s["f_hT"], u * 3 + (1 if q == 2 else 0) + 1)
                    for i in range(cw // P):
                        mm = pe.transpose(bank[4 + q % 2][:, i * P:(i + 1) * P], hid[:, c0 + i * P:c0 + (i + 1) * P],
                                          ident[:])
                    mm.then_inc(s["f_tr"], 1)
                pe.wait_ge(s["f_hT"], u * 3 + 4)
                pe.wait_ge(s["f_y"], u + 1)
                for i in range(FT):
                    mm = pe.matmul(bank[6][:, 0:H], hT[:, i], FD[:, i], start=(i == 0), stop=(i == FT - 1))
                mm.then_inc(s["f_down"], 1)


        @blk.scalar
        def _(a):
            a.sem_inc(s["f_hT"])
            pa = Steps(a, s["pro_act"])
            b3 = bank[4][:].rearrange("p (h x) -> p h x", x=4)
            beta = scal[:, S_BETA].rearrange("p u (k r) -> p (u k) r", r=R)
            a.wait_ge(s["pro_filled"], 6)
            pa.did(a.activation(beta, b3[:, :, 0:2], ACT.Exp, scale=-1.0))
            pa.did(a.activation(U1[:, 1, 0:NV], U1[:, 1, 0:NV], ACT.Exp))
            a.wait_ge(s["pro_dve"], PRO_ABS)
            e_ = T1[:, 8:10, :]
            pa.did(a.activation(e_, e_, ACT.Exp, scale=-1.0))
            pa.wait()
            pa.did(a.activation(e_, e_, ACT.Ln, bias=1.0))
            a.wait_ge(s["pro_filled"], 8)
            a.wait_ge(s["pro_dve"], PRO_G + 2)
            pa.did(a.activation(scal[:, S_EG], scal[:, S_G], ACT.Exp))
            pa.did(a.activation(T1[:, 10:14, :], T1[:, 10:14, :], ACT.Exp))
            assert pa.k == PRO_ACT
            a.wait_ge(s["pro_dve"], PRO_DVE)


            def tap(h, j):
                if j == 0:
                    a.wait_ge(s["taps_qk_ready"], h + 1)
                if j == 4:
                    a.wait_ge(s["taps_v_ready"], h + 1)
                filled_a(a, h, PROJ + j)
                a.activation(y[:, j], ring_a[j % 4][:], ACT.Copy, scale=tap_of(TAPS - 1, j)
                             ).then_inc(s["tap_done"], 1)

            def half_tanh(h, j):
                drained(a, drained_a, JOBS_A, h, PROJ + j)
                a.wait_ge(s["act_done"], h * 8 + (j - 1 if j > 1 else 0) + 1)
                a.activation(th[:, j % 2], y[:, j], ACT.Tanh, scale=0.5).then_inc(s["tanh_done"], 1)

            def z_tanh(h, g):
                filled_a(a, h, ZJ + g)
                if g >= 2:
                    drained(a, drained_a, JOBS_A, h, ZJ + g - 2)
                else:
                    a.wait_ge(s["act_done"], h * 8 + 9)
                a.activation(th[:, g % 2], ring_a[g][:], ACT.Tanh, scale=0.5).then_inc(s["z_tanh"], 1)

            def squares(h):
                for i in range(4):
                    filled_a(a, h, TR_QK + i)
                    a.wait_ge(s["ss_done"], h * 4 + (i - 1 if i > 1 else 0) + 1)
                    a.activation(sq[:, i % 2], ring_a[i][:], ACT.Square).then_inc(s["sq_done"], 1)

            def kq_by_channel(h):
                for g in range(4):
                    filled_a(a, h, BACK + g)
                    a.activation(kqT[:, 2 * g:2 * g + 2].rearrange("p u x i -> p (u x i)"), ring_a[g][:], ACT.Copy
                                 ).then_inc(drained_a[g], 1)

            def v_by_token(h):
                for i in range(4):
                    r, b = i // 2, i % 2
                    filled_a(a, h, TR_V + i)
                    a.activation(v[:].rearrange("p (u r) d -> p u r d", r=R)[:, b * CH:(b + 1) * CH, r, :],
                                 ring_a[i][:].rearrange("p (u d) -> p u d", d=D), ACT.Copy, scale=0.5
                                 ).then_inc(drained_a[i], 1)

            def decays(h):
                a.wait_ge(s["dg_done"], h + 1)
                a.activation(dec[:], dec[:], ACT.Exp).then_inc(s["exp_done"], 1)

            def merge(n, step):
                for g in range(4):
                    ms = slice(4 * g, 4 * g + 4)
                    filled_b(a, n, MERGE + 4 * step + g)
                    whole = ring_b[g][:].rearrange("p (m i) -> p m i", m=4)
                    left = ring_b[g][:, 0:256].rearrange("p (m i) -> p m i", m=4)
                    dst, src = {0: (Xm[:, ms], whole), 3: (Xm[:, ms], whole), 2: (T1[:, ms], whole),
                                5: (T1[0:64, ms, 0:64], whole[0:64, :, 0:64]),
                                6: (Xm[64:P, ms, 0:64], left[64:P]),
                                7: (U2[0:64, ms, 64:P], left[0:64])}[step]
                    a.activation(dst, src, ACT.Copy).then_inc(drained_b[g], 1)

            def recur(n, c):
                for b in range(B):
                    u = b * CH + c
                    if c:
                        j = RJ["state", u]
                        a.wait_ge(s["w_done"], n * (UNITS - B) + (c - 1) * B + b + 1)
                        if c > 1:
                            drained(a, drained_b, JOBS_B, n, RJ["local", u - 1])
                        for r in range(R):
                            t = a.activation(qs[:, b, r], ring_b[j % 4][:, 256 + r * D:256 + (r + 1) * D],
                                             ACT.Copy, scale=sc_b[:, S_EG, u, r:r + 1])
                        t.then_inc(drained_b[j % 4], 1)
                for b in range(B):
                    u = b * CH + c
                    j = RJ["solve", u]
                    if c == 0 and b == 0:
                        a.wait_ge(s["sc_b_ready"], n + 1)
                    if c < CH - 1:
                        a.wait_ge(s["vd_done"], n * (UNITS - B) + c * B + b + 1)
                    else:
                        filled_b(a, n, j)
                    if 0 < c < CH - 1:
                        filled_b(a, n, RJ["local", u - 1])
                    for r in range(R):
                        t = a.activation(vn[:, b, r], ring_b[j % 4][:, r * D:(r + 1) * D], ACT.Copy,
                                         scale=sc_b[:, S_BETA, u, r:r + 1])
                    t.then_inc(drained_b[j % 4], 1)

            def out_squares(n, g):
                a.wait_ge(s["x_gated"], n * 4 + g + 1)
                a.wait_ge(s["ss2_done"], n * 4 + (g - 1 if g > 1 else 0) + 1)
                a.activation(sq_out[g % 2][:].rearrange("p b r d -> p (b r d)"),
                             core[:, 4 * g:4 * g + 4].rearrange("p m d -> p (m d)"), ACT.Square
                             ).then_inc(s["sq2_done"], 1)

            def out_by_channel(n):
                for g in range(4):
                    filled_b(a, n, XT + g)
                    a.activation(xT[:, 4 * g:4 * g + 4].rearrange("p m d -> p (m d)"), ring_b[g][:], ACT.Copy,
                                 scale=normw[:, 0:1]).then_inc(drained_b[g], 1)

            def body(n, more, most):
                merge(n, 0)
                if more:
                    tap(n + 1, 4)
                merge(n, 2)
                if more:
                    half_tanh(n + 1, 4)
                    tap(n + 1, 5)
                merge(n, 3)
                if more:
                    half_tanh(n + 1, 5)
                    tap(n + 1, 6)
                merge(n, 5)
                if more:
                    half_tanh(n + 1, 6)
                merge(n, 6)
                if more:
                    tap(n + 1, 7)
                merge(n, 7)
                if more:
                    half_tanh(n + 1, 7)
                recur(n, 0)
                if more:
                    decays(n + 1)
                recur(n, 1)
                if more:
                    squares(n + 1)
                recur(n, 2)
                recur(n, 3)
                if more:
                    kq_by_channel(n + 1)
                    v_by_token(n + 1)
                for g in range(4):
                    if more:
                        z_tanh(n + 1, g)
                    out_squares(n, g)
                if most:
                    for j in (0, 2):
                        tap(n + 2, j)
                        tap(n + 2, j + 1)
                        half_tanh(n + 2, j)
                        half_tanh(n + 2, j + 1)
                out_by_channel(n)

            tap(0, 0)
            for j in range(1, 8):
                tap(0, j)
                half_tanh(0, j - 1)
            half_tanh(0, 7)
            decays(0)
            squares(0)
            kq_by_channel(0)
            v_by_token(0)
            for g in range(4):
                z_tanh(0, g)
            for j in (0, 2):
                tap(1, j)
                tap(1, j + 1)
                half_tanh(1, j)
                half_tanh(1, j + 1)
            with a.Fori(0, NK - 2) as n:
                body(n, True, True)
            body(NK - 2, True, False)
            body(NK - 1, False, False)

            ea = Steps(a, s["ep_act"])
            a.wait_ge(s["ep_dve"], EP_EXP)
            ea.did(a.activation(probs[:], logits[:], ACT.Exp))
            with a.Fori(0, UNITS) as u:
                for q, (c0, cw) in enumerate(FCHUNKS):
                    a.wait_ge(s["f_gu"], u * 3 + q + 2)
                    a.wait_ge(s["f_h"], u * 3 + 1)
                    a.activation(thf[:, c0:c0 + cw], bank[2 * (q % 2)][:, 0:cw], ACT.Tanh, scale=0.5
                                 ).then_inc(s["f_tanh"], 1)
                for q, (c0, cw) in enumerate(FCHUNKS):
                    a.wait_ge(s["f_tr"], u * 3 + q + 2)
                    a.wait_ge(s["f_down"], u + 1)
                    a.activation(hT[:, c0 // P:(c0 + cw) // P].rearrange("p a b -> p (a b)"), bank[4 + q % 2][:, 0:cw],
                                 ACT.Copy).then_inc(s["f_hT"], 1)

        @blk.vector
        def _(d):
            for name in ("act_done", "ss_done", "ss2_done", "f_h", "f_hs", "f_y"):
                d.sem_inc(s[name])
            for q in (*drained_a, *drained_b):
                d.sem_inc(q)
            pr = Steps(d, s["pro_dve"])
            flat8 = lin_x()

            def pool_first():
                d.wait_ge(s["pro_pool"], PRO_POOL + 2)
            d.wait_ge(s["x_loaded"], 16)
            norm(d, None, pr, X[:], flat8, pool_first)
            for q in range(4):
                d.wait_ge(s["pro_filled"], q + 1)
                pr.did(d.tensor_copy(xnT[:, q // 2, (q % 2) * 512:(q % 2 + 1) * 512], bank[q][:]))
            d.wait_ge(s["pro_filled"], 5)
            pr.did(d.tensor_copy(convT[:].rearrange("p a t -> p (a t)"), bank[5][:, 0:256]))
            d.wait_ge(s["pro_filled"], 6)
            d.wait_ge(s["pro_act"], 2)
            za = T1[:, 6:8, :]
            za4 = za.rearrange("p a b -> p (a b)").rearrange("p (u k r) -> p u k r", u=UNITS, r=R)
            ain = bank[4][:].rearrange("p (u k x) -> p u k x", u=UNITS, x=4)[:, :, :, 2:4]
            dtb = U1[:, 1, NV:2 * NV].rearrange("p (k r) -> p k r", r=R).unsqueeze(1).to_broadcast([P, UNITS, NK, R])
            pr.did(d.tensor_tensor(za4, ain, dtb, ALU.add))
            pr.wait()
            e_ = T1[:, 8:10, :]
            pr.did(d.scalar_tensor_tensor(e_, za, -1.0, za, ALU.mult, ALU.max))
            d.wait_ge(s["pro_act"], 4)
            pr.did(d.scalar_tensor_tensor(za, za, 0.0, e_, ALU.max, ALU.add))
            beta = scal[:, S_BETA]
            pr.did(d.tensor_scalar(beta, beta, 1.0, None, ALU.add))
            pr.wait()
            pr.did(d.reciprocal(beta, beta))
            g_ = U1[:, 2:4, :].rearrange("p a b -> p (a b)").rearrange("p (u h) -> p u h", u=UNITS)
            pr.did(d.scalar_tensor_tensor(g_, za.rearrange("p a b -> p (a b)").rearrange("p (u h) -> p u h", u=UNITS),
                                          -1.0, U1[:, 1, 0:NV].unsqueeze(1).to_broadcast([P, UNITS, NV]),
                                          ALU.mult, ALU.mult))
            assert pr.k == PRO_G
            d.wait_ge(s["pro_filled"], 8)
            G = scal[:, S_G].rearrange("p u h -> p (u h)")
            pr.did(d.tensor_copy(G, bank[6][:, 0:256]))
            pr.wait()
            gl = T1[:, 10:14, :].rearrange("p a b -> p (a b)")
            d.tensor_copy(gl[:, 0:256], bank[6][:, 256:512])
            pr.did(d.tensor_tensor(gl[:, 256:512], bank[6][:, 256:512], G, ALU.subtract))
            d.tensor_copy(Xm[0:NV, 0:4, :].rearrange("h u i -> h (u i)"), bank[0][0:NV, :])
            d.tensor_copy(Xm[0:NV, 4:8, :].rearrange("h u i -> h (u i)"), bank[1][0:NV, :]
                          ).then_inc(s["gates_ready"], 1)
            d.wait_ge(s["pro_act"], 6)
            pr.did(d.tensor_copy(scal[:, S_EGL].rearrange("p u h -> p (u h)"), gl[:, 0:256]))
            d.tensor_scalar(scal[:, S_NEG], scal[:, S_EG], -1.0, None, ALU.mult)
            pr.did(d.tensor_scalar(scal[:, S_NBETA], beta, -1.0, None, ALU.mult))
            pr.did(d.tensor_tensor(scal[:, S_BK].rearrange("p u h -> p (u h)"), gl[:, 256:512],
                                   scal[:, S_BETA].rearrange("p u h -> p (u h)"), ALU.mult))
            assert pr.k == PRO_DVE


            def conv(h, j):
                d.wait_ge(s["tap_done"], h * 8 + j + 1)
                ds = Steps(d, s["conv_step"], h * CONV_STEPS + 2 * j)
                for back in range(1, TAPS):
                    if back > 1:
                        ds.wait()
                    t = d.scalar_tensor_tensor(y[:, j, back:], ring_a[j % 4][:, 0:S - back],
                                               tap_of(TAPS - 1 - back, j), y[:, j, back:], ALU.mult, ALU.add)
                    if back < TAPS - 1:
                        ds.did(t)
                    else:
                        t.then_inc(drained_a[j % 4], 1)

            def silu(h, j):
                d.wait_ge(s["tanh_done"], h * 8 + j + 1)
                d.scalar_tensor_tensor(y[:, j], th[:, j % 2], 1.0, y[:, j], ALU.add, ALU.mult
                                       ).then_inc(s["act_done"], 1)

            def z_gate(h, g):
                d.wait_ge(s["z_tanh"], h * 4 + g + 1)
                if not isinstance(h, int) or h:
                    d.wait_ge(s["x_gated"], h * 4 + g - 3)
                d.scalar_tensor_tensor(gz[:, 4 * g:4 * g + 4].rearrange("p m d -> p (m d)"), th[:, g % 2], 1.0,
                                       ring_a[g][:], ALU.add, ALU.mult).then_inc(drained_a[g], 1)

            def differences(h):
                d.wait_ge(s["rows_loaded"], (h + 1) * 16 * R)
                d.wait_ge(s["sc_a_ready"], h + 1)
                for m in range(M):
                    t = d.tensor_scalar(dec[:, m], dec[:, m], sc_a[:, S_G, m // R, m % R:m % R + 1], 0.0,
                                        ALU.subtract, ALU.min)
                t.then_inc(s["dg_done"], 1)

            def square_sums(h):
                for i in range(4):
                    d.wait_ge(s["sq_done"], h * 4 + i + 1)
                    d.tensor_reduce(ss[:, 4 * i:4 * i + 4], sq[:, i % 2].rearrange("p (u d) -> p u d", d=D), AX.X,
                                    ALU.add).then_inc(s["ss_done"], 1)

            def normalise(h):
                d.wait_ge(s["rr_done"], h + 1)
                for i in range(4):
                    dst = (qhat, khat)[i // 2]
                    d.tensor_tensor(dst[:, (i % 2) * CH:(i % 2 + 1) * CH],
                                    ring_a[i][:].rearrange("p (u d) -> p u d", d=D),
                                    rr[:, 4 * i:4 * i + 4].unsqueeze(2).to_broadcast([P, 4, D]), ALU.mult
                                    ).then_inc(drained_a[i], 1)

            def n_and_a(h):
                d.wait_ge(s["decn_done"], h + 1)
                for g in range(4):
                    filled_a(d, h, GRAM + g)
                    kk = ring_a[g][:].rearrange("p (u x i) -> p u x i", x=2, i=P)
                    for x_, (dst, by) in enumerate(((nmat, decn), (attn, dec))):
                        for i in range(2):
                            ms = slice(4 * g + 2 * i, 4 * g + 2 * i + 2)
                            t = d.tensor_tensor(dst[:, ms], kk[:, i, x_, :].unsqueeze(1).to_broadcast([P, R, P]),
                                                by[:, ms], ALU.mult)
                    t.then_inc(drained_a[g], 1)

            def invert_blocks(h):
                ds = Steps(d, s["base_step"], h * BASE_STEPS)
                d.wait_ge(s["raw_loaded"], (h + 1) * 16)
                for i in range(1, BLK):
                    if i == 1:
                        ds.did(d.tensor_copy(ublk[:, 0:1, 1], nblk[:, 0:1, 1]))
                        ds.wait()
                        continue
                    pv = prod[:, 0:i * i].rearrange("p (c j) -> p c j", c=i)
                    ds.did(d.tensor_tensor(pv, ublk[:, 0:i, 0:i],
                                           nblk[:, 0:i, i].unsqueeze(1).to_broadcast([P, i, i]), ALU.mult))
                    ds.wait()
                    t = d.tensor_reduce(ublk[:, 0:i, i], pv, AX.X, ALU.add)
                    if i < BLK - 1:
                        ds.did(t)
                        ds.wait()
                    else:
                        t.then_inc(s["base_done"], 1)
                assert ds.k == BASE_STEPS, ds.k
                d.wait_ge(s["base_done"], h * 2 + 1)
                d.tensor_copy(tblk[:].rearrange("p i c -> p c i"), ublk[:]).then_inc(s["base_done"], 1)

            def merge(n, step):
                for g in range(4):
                    ms = slice(4 * g, 4 * g + 4)
                    filled_b(d, n, MERGE + 4 * step + g)
                    d.tensor_tensor(U1[:, ms], ring_b[g][:].rearrange("p (m i) -> p m i", m=4),
                                    (U0 if step == 1 else U1)[:, ms], ALU.add).then_inc(drained_b[g], 1)

            def recur(n, c):
                for b in range(B):
                    u = b * CH + c
                    if c:
                        j = RJ["state", u]
                        filled_b(d, n, j)
                        for r in range(R):
                            t = d.scalar_tensor_tensor(w_[:, b, r], ring_b[j % 4][:, r * D:(r + 1) * D],
                                                       sc_b[:, S_NEG, u, r:r + 1], v[:, u * R + r],
                                                       ALU.mult, ALU.add)
                        t.then_inc(s["w_done"], 1)
                if c < CH - 1:
                    for b in range(B):
                        u = b * CH + c
                        j = RJ["solve", u]
                        if c == 0 and b == 0:
                            d.wait_ge(s["sc_b_ready"], n + 1)
                        filled_b(d, n, j)
                        d.tensor_tensor(vd[:, b], ring_b[j % 4][:, 0:256].rearrange("p (r d) -> p r d", r=R),
                                        sc_b[:, S_BK, u].unsqueeze(2).to_broadcast([P, R, D]), ALU.mult
                                        ).then_inc(s["vd_done"], 1)
                for b in range(B):
                    u = b * CH + c
                    j = RJ["local", u]
                    filled_b(d, n, j)
                    cu = core[:, u * R:(u + 1) * R].rearrange("p r d -> p (r d)")
                    if c:
                        drained(d, drained_b, JOBS_B, n, RJ["state", u])
                        t = d.tensor_tensor(cu, ring_b[j % 4][:, 0:256], qs[:, b].rearrange("p r d -> p (r d)"),
                                            ALU.add)
                    else:
                        t = d.tensor_copy(cu, ring_b[j % 4][:, 0:256])
                    t.then_inc(drained_b[j % 4], 1)
                if c < CH - 1:
                    for b in range(B):
                        u = b * CH + c
                        j = RJ["update", u]
                        filled_b(d, n, j)
                        if c:
                            drained(d, drained_b, JOBS_B, n, RJ["update", u - 1])
                            for r in range(R):
                                t = d.scalar_tensor_tensor(st[:, b, r * D:(r + 1) * D],
                                                           st[:, b, r * D:(r + 1) * D],
                                                           sc_b[:, S_EGL, u, r:r + 1],
                                                           ring_b[j % 4][:, r * D:(r + 1) * D],
                                                           ALU.mult, ALU.add)
                        else:
                            t = d.tensor_copy(st[:, b], ring_b[j % 4][:, 0:256])
                        t.then_inc(drained_b[j % 4], 1)

            def out_sums(n, g):
                d.wait_ge(s["sq2_done"], n * 4 + g + 1)
                d.tensor_reduce(ss_out[:, 4 * g:4 * g + 4],
                                sq_out[g % 2][:].rearrange("p b r d -> p (b r) d"), AX.X,
                                ALU.add).then_inc(s["ss2_done"], 1)

            def accumulate(n):
                for g in range(4):
                    filled_b(d, n, OUTJ + g)
                    au = acc[:, 2 * g:2 * g + 2].rearrange("p u h -> p (u h)")
                    d.tensor_tensor(au, au, ring_b[g][:], ALU.add).then_inc(drained_b[g], 1)

            def body(n, more, most):
                if more:
                    conv(n + 1, 4)
                merge(n, 1)
                if more:
                    silu(n + 1, 4)
                    conv(n + 1, 5)
                merge(n, 4)
                if more:
                    silu(n + 1, 5)
                    conv(n + 1, 6)
                    silu(n + 1, 6)
                    differences(n + 1)
                    conv(n + 1, 7)
                    silu(n + 1, 7)
                recur(n, 0)
                recur(n, 1)
                if more:
                    square_sums(n + 1)
                recur(n, 2)
                recur(n, 3)
                if more:
                    normalise(n + 1)
                    n_and_a(n + 1)
                for g in range(4):
                    if more:
                        z_gate(n + 1, g)
                    out_sums(n, g)
                if most:
                    conv(n + 2, 0)
                    conv(n + 2, 1)
                    silu(n + 2, 0)
                    silu(n + 2, 1)
                if more:
                    invert_blocks(n + 1)
                if most:
                    conv(n + 2, 2)
                    conv(n + 2, 3)
                    silu(n + 2, 2)
                    silu(n + 2, 3)
                accumulate(n)

            for j in range(8):
                conv(0, j)
                if j:
                    silu(0, j - 1)
            silu(0, 7)
            differences(0)
            square_sums(0)
            normalise(0)
            n_and_a(0)
            for g in range(4):
                z_gate(0, g)
            conv(1, 0)
            conv(1, 1)
            silu(1, 0)
            silu(1, 1)
            invert_blocks(0)
            conv(1, 2)
            conv(1, 3)
            silu(1, 2)
            silu(1, 3)
            with d.Fori(0, NK - 2) as n:
                body(n, True, True)
            body(NK - 2, True, False)
            body(NK - 1, False, False)

            ep = Steps(d, s["ep_dve"])
            for g in range(4):
                d.wait_ge(drained_b[g], NK * (JOBS_B // 4) + 1)
            t = d.tensor_copy(comb[:, :, E:FT], ones[:, 0:UNITS * 2].rearrange("p (u e) -> p u e", e=2))
            t.then_inc(s["ep_drained"], 1)
            d.wait_ge(s["ep_drained"], 1)

            def pool_turn(k):
                def wait():
                    d.wait_ge(s["ep_pool"], 2 * k)
                return wait
            norms = []
            norms.append(norm(d, None, ep, acc[:], acc[:], pool_turn(1)))
            ep.wait()
            ep.did(d.tensor_tensor(X[:], X[:], acc[:], ALU.add))
            ep.wait()
            norms.append(norm(d, None, ep, X[:], lin_x(), pool_turn(2)))
            assert ep.k == EP_XN2, ep.k
            for q in range(4):
                d.wait_ge(s["ep_pe"], q + 1)
                ep.did(d.tensor_copy(xnT[:, q // 2, (q % 2) * 512:(q % 2 + 1) * 512], bank[q][:]))
            d.wait_ge(s["ep_pe"], 5)
            lg = bank[4][:, 0:UNITS * E].rearrange("p (u e) -> p u e", e=E)

            def row(i):
                return best[:, i].unsqueeze(2).to_broadcast([P, UNITS, E])
            ep.did(d.tensor_reduce(best[:, 0], lg, AX.X, ALU.max))
            ep.wait()
            ep.did(d.tensor_tensor(logits[:], lg, row(0), ALU.subtract))
            assert ep.k == EP_EXP, ep.k
            d.wait_ge(s["ep_act"], 1)
            ep.did(d.tensor_reduce(best[:, 1], probs[:], AX.X, ALU.add))
            ep.wait()
            ep.did(d.reciprocal(best[:, 1], best[:, 1]))
            ep.wait()
            ep.did(d.tensor_tensor(probs[:], probs[:], row(1), ALU.mult))
            ep.wait()
            src = probs
            for i, pick in enumerate((first, second)):
                ep.did(d.tensor_reduce(best[:, i], src[:], AX.X, ALU.max))
                ep.wait()
                ep.did(d.tensor_tensor(pick[:], src[:], row(i), ALU.is_equal))
                ep.wait()
                ep.did(d.tensor_tensor(pick[:], pick[:], rank_w[:].unsqueeze(1).to_broadcast([P, UNITS, E]), ALU.mult))
                ep.wait()
                ep.did(d.tensor_reduce(best[:, 2], pick[:], AX.X, ALU.max))
                ep.wait()
                ep.did(d.tensor_tensor(pick[:], pick[:], row(2), ALU.is_equal))
                ep.wait()
                if i == 0:
                    src = logits
                    ep.did(d.scalar_tensor_tensor(logits[:], first[:], -2.0, probs[:], ALU.mult, ALU.add))
                    ep.wait()
            ep.did(d.tensor_tensor(best[:, 3], best[:, 0], best[:, 1], ALU.add))
            ep.wait()
            ep.did(d.reciprocal(best[:, 3], best[:, 3]))
            ep.did(d.tensor_tensor(first[:], first[:], row(0), ALU.mult))
            ep.did(d.tensor_tensor(second[:], second[:], row(1), ALU.mult))
            ep.wait()
            ep.did(d.tensor_tensor(first[:], first[:], second[:], ALU.add))
            ep.wait()
            ep.did(d.tensor_tensor(comb[:, :, 0:E], first[:], row(3), ALU.mult))
            ep.wait()
            ep.did(d.tensor_scalar(comb[:], comb[:], 0.5, None, ALU.mult))
            ep.wait()
            assert ep.k == EP_COMB, ep.k
            with d.Fori(0, UNITS) as u:
                d.wait_ge(s["f_gu"], u * 3 + 1)
                d.wait_ge(s["f_hs"], u * 3 + 1)
                d.tensor_copy(comb_u[:], comb[:, bass.ds(u, 1), :].rearrange("p a e -> p (a e)")).then_inc(s["comb_ready"], 1)
                d.tensor_copy(xt, xnT[:, :, bass.ds(u * P, P)]).then_inc(s["f_xt"], 1)
                for q, (c0, cw) in enumerate(FCHUNKS):
                    d.wait_ge(s["f_tanh"], u * 3 + q + 1)
                    d.wait_ge(s["f_tr"], u * 3 + 1)
                    hq = hid[:, c0:c0 + cw]
                    d.scalar_tensor_tensor(hq, thf[:, c0:c0 + cw], 1.0, bank[2 * (q % 2)][:, 0:cw], ALU.add, ALU.mult
                                           ).then_inc(s["f_gated"], 1)
                    d.wait_ge(s["f_gated"], u * 3 + q + 1)
                    d.tensor_tensor(hq, hq, bank[2 * (q % 2) + 1][:, 0:cw], ALU.mult).then_inc(s["f_h"], 1)
                    d.wait_ge(s["f_h"], u * 3 + q + 2)
                    if q == 0:
                        d.wait_ge(s["comb_ready"], u + 1)
                    h3 = hq.rearrange("p (e h) -> p e h", h=P)
                    d.tensor_tensor(h3, h3, comb_u[:, c0 // P:(c0 + cw) // P].unsqueeze(2).to_broadcast([P, cw // P, P]),
                                    ALU.mult).then_inc(s["f_hs"], 1)
                d.wait_ge(s["f_down"], u + 2)
                d.tensor_copy(acc[:, bass.ds(u, 1), :].rearrange("p a h -> p (a h)"), bank[6][:, 0:H]
                              ).then_inc(s["f_y"], 1)
            d.wait_ge(s["f_y"], UNITS + 1)
            norms.append(norm(d, None, ep, acc[:], acc[:], pool_turn(3)))
            ep.wait()
            d.tensor_tensor(X[:], X[:], acc[:], ALU.add).then_inc(s["layer_done"], 1)
            assert tuple(norms) == EP_NORMS, norms


_INS = ["L0_attn_hidden_states", "L0_attn_W_qkvz", "L0_attn_W_ba", "L0_attn_conv_weight", "L0_attn_A_log",
        "L0_attn_dt_bias", "L0_attn_norm_weight", "L0_attn_W_out", "L0_ffn_router_w", "L0_ffn_w_gate",
        "L0_ffn_w_up", "L0_ffn_w_down", "L0_ffn_sw_gate", "L0_ffn_sw_up", "L0_ffn_sw_down"]


def kernel(**inputs):
    import numpy as np
    import concourse.bacc as bacc
    from concourse.bass_utils import run_bass_kernel_spmd

    nc = bacc.Bacc("TRN2", target_bir_lowering=False, num_devices=1)
    arrays, args = {}, []
    for name in _INS:
        a = np.ascontiguousarray(inputs[name])
        arrays[name + "_dram"] = a
        args.append(nc.dram_tensor(name + "_dram", a.shape, mybir.dt.from_np(a.dtype), kind="ExternalInput").ap())
    args.append(nc.dram_tensor("out_dram", (B, S, H), F32, kind="ExternalOutput").ap())
    args.append(nc.dram_tensor("decay_rows", (NV, UNITS * P), F32, kind="Internal").ap())
    args.append(nc.dram_tensor("raw_blocks", (NB, M, BLK, BLK), F32, kind="Internal").ap())
    args.append(nc.dram_tensor("inv_blocks", (2, NB, M, BLK, BLK), F32, kind="Internal").ap())
    build(nc, *args)
    r = run_bass_kernel_spmd(nc, [arrays], core_ids=[0])
    return r.results[0]["out_dram"]
```

```python
from contextlib import ExitStack

import concourse.bass as bass
from concourse import mybir

F32 = mybir.dt.float32
ALU = mybir.AluOpType
ACT = mybir.ActivationFunctionType
AX = mybir.AxisListType

P = 128
NK, R, D = 16, 2, 128
NV = NK * R
B, S, H = 2, 512, 256
UNITS = B * S // P
CH = S // P
KT = H // P
M = UNITS * R
HW = 2 * D + 2 * R * D
TAPS = 4
BLK = 16
NB = P // BLK
E, FH, FS = 8, 128, 256
FT = E + FS // P
LN_EPS, RMS_EPS, L2_EPS = 1e-5, 1e-6, 1e-6

QKJ, VJ, TR_QK, BACK, GRAM, TR_V, ZJ, JOBS_A = 0, 8, 12, 16, 20, 32, 52, 28
MERGE, RECUR, OUTPUT, JOBS_B = 0, 32, 60, 68
S_G, S_NEG, S_EG, S_EGL, S_BETA, S_BK, S_NBETA, NSC = 0, 1, 2, 3, 4, 5, 6, 7


PRO_NORM, PRO_ABS, PRO_G, PRO_DVE = 2, 10, 14, 19
PRO_POOL, PRO_ACT = 5 + 3 + 6 + E + 5 + 6, 6
CONV_STEPS, BASE_STEPS, RR_STEPS = 2 * 8, 2 * BLK - 4, 2
GROUPS = (0, 2, 1, 3)
MASKED = -1e30
EP_NORMS, EP_XN2, EP_EXP, EP_COMB = (2, 6, 36), 7, 13, 34


def recurrence_jobs():
    job, k = {}, RECUR
    for c in range(CH):
        for kind in ("state", "solve", "local", "update"):
            if (kind == "state" and c == 0) or (kind == "update" and c == CH - 1):
                continue
            for b in range(B):
                job[kind, b * CH + c] = k
                k += 1
    assert k == OUTPUT
    return job


RJ = recurrence_jobs()
XTJ = [OUTPUT + 4 * (k // 2) + k % 2 for k in range(4)]
OUTJ = [j + 2 for j in XTJ]


def job_a(h, kind, i):
    j = kind + i
    if isinstance(h, int):
        if h == 0:
            j += {QKJ: 8, VJ: 4, TR_QK: 4, BACK: 4, GRAM: 4}.get(kind, 0)
        if h == NK - 1:
            j -= {TR_V: 4, ZJ: 20}.get(kind, 0)
    return j


class Steps:

    def __init__(self, eng, sem, base=0):
        self.eng, self.sem, self.base, self.k = eng, sem, base, 0

    def did(self, ins):
        ins.then_inc(self.sem, 1)
        self.k += 1
        return self.k

    def wait(self, k=None):
        self.eng.wait_ge(self.sem, self.base + (self.k if k is None else k))


def build(nc, x_in, w_qkvz, w_ba, conv_w, a_log, dt_bias, norm_w, w_out, router_w, w_gate, w_up, w_down,
          sw_gate, sw_up, sw_down, out, decay_rows, raw_blocks, inv_blocks):
    xf = x_in.rearrange("b (c p) h -> p (b c) h", p=P)
    of = out.rearrange("b (c p) h -> p (b c) h", p=P)

    with ExitStack() as ctx:
        def sb(name, shape):
            return ctx.enter_context(nc.sbuf_tensor(name, shape, F32))

        def sem(name):
            return ctx.enter_context(nc.semaphore(name))

        bank = [ctx.enter_context(nc.psum_tensor(f"bank{i}", [P, 512], F32)) for i in range(8)]
        ring_a, ring_b = bank[:4], bank[4:]

        ident = sb("ident", [P, P])
        upper = sb("upper", [P, P])
        below = sb("below", [P, P])
        merge16 = sb("merge16", [P, P])
        merge32 = sb("merge32", [P, P])
        ones = sb("ones", [P, P])
        minus_half = sb("minus_half", [P, M])
        l2_consts = sb("l2_consts", [P, 2, M])
        rms_consts = sb("rms_consts", [P, 2, M])
        rank_w = sb("rank_w", [P, E])
        acc = sb("acc", [P, UNITS, H])
        xnT = sb("xnT", [P, KT, UNITS * P])
        scal = sb("scal", [P, NSC, UNITS, NV])
        convT = sb("convT", [P, TAPS, 64])
        normw = sb("normw", [P, 1])
        Wqk = sb("Wqk", [P, KT, 2 * D])
        Wv = sb("Wv", [P, KT, R * D])
        Wz = sb("Wz", [P, KT, R * D])
        Wo = sb("Wo", [P, R, H])
        taps_qk = sb("taps_qk", [P, TAPS, 2])
        taps_v = sb("taps_v", [P, TAPS, R])
        sc_a = sb("sc_a", [P, NSC, UNITS, R])
        sc_b = sb("sc_b", [P, NSC, UNITS, R])
        y = sb("y", [P, 8, 512])
        th = sb("th", [P, 2, 512])
        sq = sb("sq", [P, 2, 512])
        ss = sb("ss", [P, M])
        rr = sb("rr", [P, M])
        ss_out = sb("ss_out", [P, M])
        rr_out = sb("rr_out", [P, M])
        qhat = sb("qhat", [P, UNITS, D])
        khat2 = sb("khat2", [P, 2, UNITS, D])
        kqT2 = sb("kqT2", [P, 2, UNITS, 2, P])
        attn2 = sb("attn2", [P, 2, M, P])
        khat, kqT, attn = ([t[:, i] for i in range(2)] for t in (khat2, kqT2, attn2))
        v = sb("v", [P, M, D])
        gz = sb("gz", [P, M, D])
        dec2 = sb("dec2", [P, 2, M, P])
        dec, decn = dec2[:, 0], dec2[:, 1]
        nmat = sb("nmat", [P, M, P])
        n16 = sb("n16", [P, M, P])
        n32 = decn
        nblk = sb("nblk", [P, BLK, BLK])
        ublk = sb("ublk", [P, BLK, BLK])
        tblk = sb("tblk", [P, BLK, BLK])
        prod = sb("prod", [P, BLK * BLK])
        UT0 = sb("UT0", [P, 2, M, P])
        U0, T0 = UT0[:, 0], UT0[:, 1]
        Xm = sb("Xm", [P, M, P])
        U1 = sb("U1", [P, M, P])
        T1 = sb("T1", [P, M, P])
        U2 = U1
        st = sb("st", [P, B, R * D])
        w_ = sb("w_", [P, B, R, D])
        vn = sb("vn", [P, B, R, D])
        vd = sb("vd", [P, B, R, D])
        qs = sb("qs", [P, B, R, D])
        core = Xm
        xT = T1
        stats = sb("stats", [P, UNITS, 6])
        moments = sb("moments", [P, UNITS, 2])
        rstd = sb("rstd", [P, UNITS])

        fw = [y[:].rearrange("p a b -> p (a b)")[:, i * 3 * H:(i + 1) * 3 * H] for i in range(4)]
        w_gate_of, w_up_of = ([t[:, i * H:(i + 1) * H].rearrange("p (k c) -> p k c", k=KT) for t in fw]
                              for i in range(2))
        w_down_of = [t[:, 2 * H:3 * H] for t in fw]
        hT = [UT0[:, i].rearrange("p m i -> p (m i)")[:, 0:UNITS * P] for i in range(2)]
        thf = n16[:].rearrange("p a b -> p (a b)")[:, 0:2 * S].rearrange("p (b i) -> p b i", b=B)
        X = attn2[:, 1].rearrange("p m i -> p (m i)").rearrange("p (u h) -> p u h", u=UNITS)
        router = sb("router", [P, KT, E])
        def lin_x():
            return v[:].rearrange("p a b -> p (a b)").rearrange("p (u h) -> p u h", u=UNITS)

        rest = y[:].rearrange("p a b -> p (a b)")[:, 12 * H:]
        logits, probs, first, second = (rest[:, i * UNITS * E:(i + 1) * UNITS * E]
                                        .rearrange("p (u e) -> p u e", u=UNITS) for i in range(4))
        comb = rest[:, 4 * UNITS * E:4 * UNITS * E + UNITS * FT].rearrange("p (u e) -> p u e", u=UNITS)
        comb_e = sb("comb_e", [P, UNITS])
        best = sb("best", [P, 4, UNITS])

        s = {n: sem(n) for n in (
            "x_loaded", "params_loaded", "rows_stored", "wqk_loaded", "wv_loaded", "wz_loaded", "rows_loaded", "wo_loaded",
            "raw_stored", "raw_loaded", "inv_stored", "t0_loaded", "u0_loaded",
            "filled_a", "filled_b", "pro_filled", "pro_dve", "pro_act", "pro_pool", "gates_ready",
            "taps_qk_ready", "taps_v_ready", "sc_a_ready", "sc_b_ready", "tap_done", "tanh_done", "act_done", "sq_done", "ss_done", "rr_done",
            "z_tanh", "masked", "exp_done", "decn_done", "nmat_done", "n_ready", "base_done",
            "w_done", "vd_done", "x_gated", "sq2_done", "ss2_done", "rr2_done", "x_scaled",
            "conv_step", "base_step", "rr_step", "rr_out_step",
            "ep_dve", "ep_act", "ep_pool", "ep_pe", "router_loaded", "ep_drained", "out_stored",
            "f_w_loaded0", "f_w_loaded1", "f_w_loaded2", "f_w_loaded3", "f_gu", "f_tanh", "f_gated", "f_h", "f_down", "f_y", "comb_ready", "acc_cleared", "layer_done")}
        drained_a = [sem(f"drained_a{i}") for i in range(4)]
        drained_b = [sem(f"drained_b{i}") for i in range(4)]
        blk = ctx.enter_context(nc.Block())

        def filled_a(eng, h, kind, i):
            eng.wait_ge(s["filled_a"], h * JOBS_A + job_a(h, kind, i) + 2)

        def drained_from_a(eng, h, kind, i):
            eng.wait_ge(drained_a[i], h * (JOBS_A // 4) + job_a(h, kind, i) // 4 + 2)

        def free_a(eng, h, kind, i):
            eng.wait_ge(drained_a[i], h * (JOBS_A // 4) + job_a(h, kind, i) // 4 + 1)

        def filled_b(eng, n, j):
            eng.wait_ge(s["filled_b"], n * JOBS_B + j + 2)

        def drained_from_b(eng, n, j):
            eng.wait_ge(drained_b[j % 4], n * (JOBS_B // 4) + j // 4 + 2)

        def free_b(eng, n, j):
            eng.wait_ge(drained_b[j % 4], n * (JOBS_B // 4) + j // 4 + 1)

        def tap_of(t, j):
            return (taps_qk if j < 4 else taps_v)[:, t, (j // 2) % 2:(j // 2) % 2 + 1]

        @blk.sync
        def _(sp):
            sp.dma_start(X, xf).then_inc(s["x_loaded"], 16)
            sp.dma_start(U1[:, 0, :].rearrange("p (k c) -> p k c", k=KT), w_ba.rearrange("(k p) c -> p k c", p=P)
                         ).then_inc(s["params_loaded"], 16)
            sp.dma_start(U1[:, 1, 0:NV], a_log.rearrange("(a h) -> a h", a=1).to_broadcast([P, NV])
                         ).then_inc(s["params_loaded"], 16)
            sp.dma_start(U1[:, 1, NV:2 * NV], dt_bias.rearrange("(a h) -> a h", a=1).to_broadcast([P, NV])
                         ).then_inc(s["params_loaded"], 16)
            sp.dma_start(T1[0:64, 0:TAPS, :].rearrange("t a p -> t (a p)"),
                         conv_w.rearrange("(t p) a -> t (p a)", p=P)).then_inc(s["params_loaded"], 16)
            sp.dma_start(normw[:], norm_w.rearrange("(p a) -> p a", a=1)).then_inc(s["params_loaded"], 16)
            sp.wait_ge(s["gates_ready"], 1)
            sp.dma_start(decay_rows, Xm[0:NV, 0:UNITS, :].rearrange("h u i -> h (u i)")
                         ).then_inc(s["rows_stored"], 16)
            sp.wait_ge(s["rows_stored"], 16)

            def columns(h, at, width):
                return w_qkvz[:, bass.ds(h * HW + at, width)].rearrange("(k p) c -> p k c", p=P)

            def load_qk(h, first=False):
                if not first:
                    filled_a(sp, h - 1, QKJ, 3)
                sp.dma_start(Wqk[:], columns(h, 0, 2 * D)).then_inc(s["wqk_loaded"], 16)

            def load_v(h, first=False):
                if not first:
                    filled_a(sp, h - 1, VJ, 3)
                sp.dma_start(Wv[:], columns(h, 2 * D, R * D)).then_inc(s["wv_loaded"], 16)

            def load_z(h):
                filled_b(sp, h - 1, OUTJ[3])
                sp.dma_start(Wz[:], columns(h, 2 * D + R * D, R * D)).then_inc(s["wz_loaded"], 16)
                sp.dma_start(Wo[:], w_out[bass.ds(h * R * D, R * D), :].rearrange("(r p) c -> p r c", p=P)
                             ).then_inc(s["wo_loaded"], 16)

            def load_rows(h, first=False):
                if not first:
                    for g in range(4):
                        drained_from_a(sp, h - 1, GRAM, g)
                for r in range(R):
                    sp.dma_start(dec.rearrange("p (u r) i -> p u r i", r=R)[:, :, r, :],
                                 decay_rows[bass.ds(h * R + r, 1), :].rearrange("h (u i) -> h u i", u=UNITS)
                                 .to_broadcast([P, UNITS, P])).then_inc(s["rows_loaded"], 16)

            def blocks_out(h):
                sp.wait_ge(s["nmat_done"], (h + 1) * 4)
                for k in range(NB):
                    sp.dma_start(raw_blocks[k].rearrange("m j i -> j m i"),
                                 nmat[k * BLK:(k + 1) * BLK, :, k * BLK:(k + 1) * BLK]
                                 ).then_inc(s["raw_stored"], 16)
                sp.wait_ge(s["raw_stored"], (h + 1) * 16 * NB)
                sp.dma_start(nblk[:], raw_blocks.rearrange("k m j i -> (k m) j i")).then_inc(s["raw_loaded"], 16)

            def blocks_back(h):
                sp.wait_ge(s["base_done"], (h + 1) * 2)
                sp.dma_start(inv_blocks[1].rearrange("k m c i -> (k m) c i"), tblk[:]).then_inc(s["inv_stored"], 16)
                sp.dma_start(inv_blocks[0].rearrange("k m c i -> (k m) c i"), ublk[:]).then_inc(s["inv_stored"], 16)
                sp.wait_ge(s["inv_stored"], (h + 1) * 32)
                for i, dst, said in ((1, T0, "t0_loaded"), (0, U0, "u0_loaded")):
                    for k in range(NB):
                        sp.dma_start(dst[k * BLK:(k + 1) * BLK, :, k * BLK:(k + 1) * BLK],
                                     inv_blocks[i, k].rearrange("m c i -> c m i")).then_inc(s[said], 16)

            def body(n, more, most):
                if more:
                    load_v(n + 1)
                if most:
                    load_qk(n + 2)
                load_z(n)
                if more:
                    blocks_out(n + 1)
                if most:
                    load_rows(n + 2)
                if more:
                    blocks_back(n + 1)

            load_qk(0, True)
            load_rows(0, True)
            load_v(0, True)
            load_qk(1)
            blocks_out(0)
            load_rows(1)
            blocks_back(0)
            with sp.Fori(0, (NK - 2) // 2) as pair:
                for parity in range(2):
                    body(pair * 2 + parity, True, True)
            body(NK - 2, True, False)
            body(NK - 1, False, False)
            filled_b(sp, NK - 1, RJ["local", UNITS - 1])
            sp.dma_start(X, xf).then_inc(s["x_loaded"], 16)
            sp.dma_start(router[:],
                         router_w.rearrange("(k p) e -> p k e", p=P)).then_inc(s["router_loaded"], 16)

            def load_tile(i, gate, up, down):
                for dst, src in ((w_gate_of[i], gate), (w_up_of[i], up), (w_down_of[i], down)):
                    sp.dma_start(dst, src).then_inc(s[f"f_w_loaded{i}"], 16)

            for e in range(FT):
                if e >= 4:
                    sp.wait_ge(s["f_down"], 4 * (e - 3))
                if e < E:
                    load_tile(e % 4, w_gate[e].rearrange("(k p) h -> p k h", p=P),
                              w_up[e].rearrange("(k p) h -> p k h", p=P), w_down[e])
                else:
                    cs = slice((e - E) * P, (e - E + 1) * P)
                    load_tile(e % 4, sw_gate[:, cs].rearrange("(k p) h -> p k h", p=P),
                              sw_up[:, cs].rearrange("(k p) h -> p k h", p=P), sw_down[cs, :])
            sp.wait_ge(s["layer_done"], 1)
            sp.dma_start(of, X).then_inc(s["out_stored"], 16)
            sp.wait_ge(s["out_stored"], 16)

        def norm(dve, steps, src, dst, pool_wait):
            for u in range(UNITS):
                t = dve.bn_stats(stats[:, u], src[:, u])
            steps.did(t)
            steps.wait()
            for u in range(UNITS):
                t = dve.bn_aggr(moments[:, u], stats[:, u])
            k = steps.did(t)
            pool_wait()
            for u in range(UNITS):
                t = dve.tensor_scalar(dst[:, u], src[:, u], moments[:, u, 0:1], rstd[:, u:u + 1],
                                      ALU.subtract, ALU.mult)
            steps.did(t)
            return k

        def rstd_of(po, steps):
            steps.did(po.tensor_scalar(rstd[:], moments[:, :, 1], 1.0, LN_EPS, ALU.mult, ALU.add))
            steps.wait()
            steps.did(po.tensor_tensor(rstd[:], rstd[:], minus_half[:, 0:UNITS], ALU.pow))

        @blk.gpsimd
        def _(po):
            po.sem_inc(s["n_ready"])
            st_ = Steps(po, s["pro_pool"])
            st_.did(po.memset(ident[:], 0.0))
            st_.did(po.memset(ones[:], 1.0))
            st_.did(po.memset(merge16[:], 0.0))
            st_.did(po.memset(merge32[:], 0.0))
            st_.did(po.memset(minus_half[:], -0.5))
            st_.wait()
            st_.did(po.affine_select(out=ident[:], in_=ident[:], compare_op=ALU.not_equal, fill=1.0, base=0,
                                     pattern=[[-1, P]], channel_multiplier=1))
            st_.did(po.affine_select(out=upper[:], in_=ones[:], compare_op=ALU.is_ge, fill=0.0, base=0,
                                     pattern=[[1, P]], channel_multiplier=-1))
            st_.wait()
            st_.did(po.tensor_scalar(below[:], upper[:], -MASKED, MASKED, ALU.mult, ALU.add))
            for m_, size in ((merge16, 16), (merge32, 32)):
                half = m_[:].rearrange("p (b h l) -> p b h l", h=2, l=size)[:, :, 1, :]
                nb = P // (2 * size)
                st_.did(po.memset(half, 1.0))
                st_.wait()
                st_.did(po.affine_select(out=half, in_=half, compare_op=ALU.is_ge, fill=0.0, base=0,
                                         pattern=[[-2 * size, nb], [0, size]], channel_multiplier=1))
                st_.wait()
                st_.did(po.affine_select(out=half, in_=half, compare_op=ALU.is_ge, fill=0.0, base=size - 1,
                                         pattern=[[2 * size, nb], [0, size]], channel_multiplier=-1))
            for e in range(E):
                st_.did(po.memset(rank_w[:, e:e + 1], float(E - e)))
            st_.did(po.memset(U0, 0.0))
            st_.did(po.memset(T0, 0.0))
            st_.did(po.memset(ublk[:], 0.0))
            st_.did(po.memset(acc[:], 0.0))
            for t, value in ((l2_consts[:, 0, 0:UNITS], D), (l2_consts[:, 0, UNITS:M], 1.0),
                             (l2_consts[:, 1, 0:UNITS], 4 * D * L2_EPS), (l2_consts[:, 1, UNITS:M], 4 * L2_EPS),
                             (rms_consts[:, 0], 1.0 / D), (rms_consts[:, 1], 4 * RMS_EPS)):
                st_.did(po.memset(t, float(value)))
            st_.wait()
            st_.did(po.memset(ublk[:].rearrange("p a b -> p (a b)")[:, 0:BLK * BLK:BLK + 1], 1.0))
            assert st_.k == PRO_POOL, st_.k
            po.wait_ge(s["pro_dve"], PRO_NORM)
            rstd_of(po, st_)
            po.wait_ge(s["pro_dve"], PRO_DVE)
            po.wait_ge(s["pro_act"], PRO_ACT)

            def head_scalars(h, dst, said):
                po.tensor_copy(dst[:], scal[:, :, :, bass.ds(h * R, R)]).then_inc(s[said], 1)

            def head_taps_qk(h):
                po.tensor_copy(taps_qk[:, :, 0], convT[:, :, bass.ds(h, 1)].rearrange("p t a -> p (t a)"))
                po.tensor_copy(taps_qk[:, :, 1], convT[:, :, bass.ds(h + NK, 1)].rearrange("p t a -> p (t a)")
                               ).then_inc(s["taps_qk_ready"], 1)

            def head_taps_v(h):
                po.tensor_copy(taps_v[:], convT[:, :, bass.ds(h * R + 2 * NK, R)]).then_inc(s["taps_v_ready"], 1)

            def mask_rows(h):
                po.wait_ge(s["rows_loaded"], (h + 1) * 16 * R)
                po.tensor_tensor(dec, dec, below[:].unsqueeze(1).to_broadcast([P, M, P]), ALU.add
                                 ).then_inc(s["masked"], 1)

            def decays_n(h, n=None):
                po.wait_ge(s["exp_done"], h + 1)
                if n is not None:
                    filled_b(po, n, MERGE + 15)
                po.wait_ge(s["sc_a_ready"], h + 1)
                po.tensor_tensor(decn, dec,
                                 sc_a[:, S_NBETA].rearrange("p u r -> p (u r)").unsqueeze(2).to_broadcast([P, M, P]),
                                 ALU.mult).then_inc(s["decn_done"], 1)

            def qk_rsqrt(h):
                ps = Steps(po, s["rr_step"], h * RR_STEPS)
                po.wait_ge(s["ss_done"], h * 4 + 5)
                ps.did(po.tensor_tensor(rr[:], ss[:], l2_consts[:, 0], ALU.mult))
                ps.wait()
                ps.did(po.tensor_tensor(rr[:], rr[:], l2_consts[:, 1], ALU.add))
                ps.wait()
                po.tensor_tensor(rr[:], rr[:], minus_half[:], ALU.pow).then_inc(s["rr_done"], 1)

            def half_of(t, half):
                return t.rearrange("p (b c x) -> p b c x", b=2, c=2)[:, :, half, :]

            def out_rsqrt(n, half):
                ps = Steps(po, s["rr_out_step"], n * 2 * RR_STEPS + half * RR_STEPS)
                dst = half_of(rr_out[:], half)
                po.wait_ge(s["ss2_done"], n * 4 + 2 * half + 3)
                ps.did(po.tensor_tensor(dst, half_of(ss_out[:], half), half_of(rms_consts[:, 0], half), ALU.mult))
                ps.wait()
                ps.did(po.tensor_tensor(dst, dst, half_of(rms_consts[:, 1], half), ALU.add))
                ps.wait()
                po.tensor_tensor(dst, dst, half_of(minus_half[:], half), ALU.pow).then_inc(s["rr2_done"], 1)

            def n_parts(h, dst, mask):
                for g in range(4):
                    ms = slice(4 * g, 4 * g + 4)
                    po.tensor_tensor(dst[:, ms], nmat[:, ms], mask[:].unsqueeze(1).to_broadcast([P, 4, P]),
                                     ALU.mult).then_inc(s["n_ready"], 1)

            def gate(n, half):
                for b_ in range(B):
                    drained_from_b(po, n, RJ["local", b_ * CH + 2 * half + 1])
                for k in (2 * half, 2 * half + 1):
                    g = GROUPS[k]
                    drained_from_a(po, n, ZJ, g)
                    ms = slice(4 * g, 4 * g + 4)
                    po.tensor_tensor(core[:, ms], core[:, ms], gz[:, ms], ALU.mult).then_inc(s["x_gated"], 1)

            def scale_out(n, half):
                po.wait_ge(s["rr2_done"], n * 2 + half + 1)
                for k in (2 * half, 2 * half + 1):
                    ms = slice(4 * GROUPS[k], 4 * GROUPS[k] + 4)
                    po.tensor_tensor(core[:, ms], core[:, ms], rr_out[:, ms].unsqueeze(2).to_broadcast([P, 4, D]),
                                     ALU.mult).then_inc(s["x_scaled"], 1)

            def body(n, more, most):
                if most:
                    for i in range(4):
                        drained_from_a(po, n + 1, QKJ, i)
                    head_taps_qk(n + 2)
                if more:
                    qk_rsqrt(n + 1)
                    decays_n(n + 1, n)
                    po.wait_ge(s["nmat_done"], (n + 2) * 4)
                    n_parts(n + 1, n16, merge16)
                gate(n, 0)
                if more:
                    n_parts(n + 1, n32, merge32)
                out_rsqrt(n, 0)
                scale_out(n, 0)
                gate(n, 1)
                out_rsqrt(n, 1)
                scale_out(n, 1)
                if more:
                    head_scalars(n + 1, sc_b, "sc_b_ready")
                if most:
                    for i in range(4):
                        drained_from_a(po, n + 1, VJ, i)
                    head_taps_v(n + 2)
                    head_scalars(n + 2, sc_a, "sc_a_ready")
                    mask_rows(n + 2)

            head_taps_qk(0)
            head_taps_v(0)
            head_scalars(0, sc_a, "sc_a_ready")
            head_scalars(0, sc_b, "sc_b_ready")
            mask_rows(0)
            for i in range(4):
                drained_from_a(po, 0, QKJ, i)
            head_taps_qk(1)
            decays_n(0)
            qk_rsqrt(0)
            for i in range(4):
                drained_from_a(po, 0, VJ, i)
            head_taps_v(1)
            po.wait_ge(s["nmat_done"], 4)
            n_parts(0, n16, merge16)
            n_parts(0, n32, merge32)
            head_scalars(1, sc_a, "sc_a_ready")
            mask_rows(1)
            with po.Fori(0, (NK - 2) // 2) as pair:
                for parity in range(2):
                    body(pair * 2 + parity, True, True)
            body(NK - 2, True, False)
            body(NK - 1, False, False)
            ep = Steps(po, s["ep_pool"])
            for done in EP_NORMS:
                po.wait_ge(s["ep_dve"], done)
                rstd_of(po, ep)


        @blk.tensor
        def _(pe):
            pe.sem_inc(s["filled_b"])
            pe.sem_inc(s["filled_a"], 1 + job_a(0, QKJ, 0))
            pe.wait_ge(s["pro_pool"], PRO_POOL)
            pe.wait_ge(s["pro_dve"], PRO_NORM + 1)
            for q in range(4):
                k, hf = q // 2, q % 2
                for i in range(4):
                    mm = pe.transpose(bank[q][:, i * P:(i + 1) * P], lin_x()[:, hf * 4 + i, k * P:(k + 1) * P],
                                      ident[:])
                mm.then_inc(s["pro_filled"], 1)
            pe.wait_ge(s["params_loaded"], 80)
            for a in range(TAPS):
                mm = pe.transpose(bank[5][:, a * 64:(a + 1) * 64],
                                  T1[0:64, 0:TAPS, :].rearrange("t a p -> t (a p)")[:, a:TAPS * P:TAPS],
                                  ident[0:64, 0:64])
            mm.then_inc(s["pro_filled"], 1)
            pe.wait_ge(s["pro_dve"], PRO_NORM + 5)
            wba = U1[:, 0, :].rearrange("p (k c) -> p k c", k=KT)
            for u in range(UNITS):
                for k in range(KT):
                    mm = pe.matmul(bank[4][:, u * 64:(u + 1) * 64], xnT[:, k, u * P:(u + 1) * P], wba[:, k, :],
                                   start=(k == 0), stop=(k == KT - 1))
            mm.then_inc(s["pro_filled"], 1)
            pe.wait_ge(s["pro_dve"], PRO_G)
            g_ = U1[:, 2:4, :].rearrange("p a b -> p (a b)")
            pe.matmul(bank[6][:, 0:256], upper[:], g_, start=True, stop=True)
            pe.matmul(bank[6][:, 256:512], ones[:], g_, start=True, stop=True).then_inc(s["pro_filled"], 1)
            for u in range(UNITS):
                mm = pe.matmul(bank[u // 4][0:NV, (u % 4) * P:(u % 4 + 1) * P], g_[:, u * NV:(u + 1) * NV], upper[:],
                               start=True, stop=True)
            mm.then_inc(s["pro_filled"], 1)
            pe.wait_ge(s["pro_dve"], PRO_DVE)
            pe.wait_ge(s["pro_act"], PRO_ACT)

            def merge_step(n, step, g):
                j = MERGE + step * 4 + g
                out_ = ring_b[j % 4]
                free_b(pe, n, j)
                prev = j - 4
                if step:
                    drained_from_b(pe, n, prev)
                for i in range(4):
                    m = 4 * g + i
                    o = out_[:, i * P:(i + 1) * P]
                    if step == 0:
                        mm = pe.matmul(o, n16[:, m], T0[:, m], start=True, stop=True)
                    elif step == 1:
                        mm = pe.matmul(o, Xm[:, m], U0[:, m], start=True, stop=True)
                    elif step == 3:
                        mm = pe.matmul(o, n32[:, m], T1[:, m], start=True, stop=True)
                    elif step == 4:
                        mm = pe.matmul(o, Xm[:, m], U1[:, m], start=True, stop=True)
                    elif step in (2, 5):
                        mm = pe.transpose(o, U1[:, m], ident[:])
                    elif step == 6:
                        mm = pe.matmul(out_[:, i * 64:(i + 1) * 64], nmat[0:64, m], T1[0:64, m, 0:64],
                                       start=True, stop=True)
                    else:
                        mm = pe.matmul(out_[:, i * 64:(i + 1) * 64], Xm[64:P, m], U1[64:P, m, 64:P],
                                       start=True, stop=True)
                mm.then_inc(s["filled_b"], 1)


            def proj(h, j):
                ct, b = j // 2, j % 2
                if j == 0:
                    pe.wait_ge(s["wqk_loaded"], (h + 1) * 16)
                if j == 4:
                    pe.wait_ge(s["wv_loaded"], (h + 1) * 16)
                w = (Wqk if j < 4 else Wv)[:, :, (ct % 2) * P:(ct % 2 + 1) * P]
                free_a(pe, h, QKJ if j < 4 else VJ, j % 4)
                for k in range(KT):
                    mm = pe.matmul(ring_a[j % 4][:], w[:, k], xnT[:, k, b * S:(b + 1) * S],
                                   start=(k == 0), stop=(k == KT - 1))
                mm.then_inc(s["filled_a"], 1)

            def z_by_token(h, g):
                if g == 0:
                    pe.wait_ge(s["wz_loaded"], (h + 1) * 16)
                free_a(pe, h, ZJ, g)
                for i in range(2):
                    u = 2 * g + i
                    for k in range(KT):
                        mm = pe.matmul(ring_a[g][:, i * 256:(i + 1) * 256], xnT[:, k, u * P:(u + 1) * P],
                                       Wz[:, k], start=(k == 0), stop=(k == KT - 1))
                mm.then_inc(s["filled_a"], 1)

            def by_token(h, job, first):
                for i in range(4):
                    free_a(pe, h, job, i)
                    pe.wait_ge(s["act_done"], h * 8 + first + i + 2)
                    for t in range(4):
                        mm = pe.transpose(ring_a[i][:, t * P:(t + 1) * P], y[:, first + i, t * P:(t + 1) * P],
                                          ident[:])
                    mm.then_inc(s["filled_a"], 1)

            def back(h, parity):
                for g in range(4):
                    for half in (g // 2, 2 + g // 2):
                        drained_from_a(pe, h, TR_QK, half)
                    if g not in (g // 2, 2 + g // 2):
                        free_a(pe, h, BACK, g)
                    for i in range(2):
                        for x_, src in enumerate((khat[parity], qhat)):
                            c0 = (2 * i + x_) * P
                            mm = pe.transpose(ring_a[g][:, c0:c0 + P], src[:, 2 * g + i, :], ident[:])
                    mm.then_inc(s["filled_a"], 1)

            def gram(h, parity):
                for g in range(4):
                    free_a(pe, h, GRAM, g)
                    for i in range(2):
                        u = 2 * g + i
                        mm = pe.matmul(ring_a[g][:, i * 256:(i + 1) * 256], kqT[parity][:, u, 0, :],
                                       kqT[parity][:, u].rearrange("p x i -> p (x i)"), start=True, stop=True)
                    mm.then_inc(s["filled_a"], 1)

            def recur(n, c, parity, between):
                for b in range(B):
                    u = b * CH + c
                    if c:
                        j = RJ["state", u]
                        free_b(pe, n, j)
                        drained_from_b(pe, n, RJ["update", u - 1])
                        pe.matmul(ring_b[j % 4][:, 0:256], kqT[parity][:, u, 0, :], st[:, b], start=True, stop=True)
                        pe.matmul(ring_b[j % 4][:, 256:512], kqT[parity][:, u, 1, :], st[:, b], start=True, stop=True
                                  ).then_inc(s["filled_b"], 1)
                for b in range(B):
                    u = b * CH + c
                    j = RJ["solve", u]
                    free_b(pe, n, j)
                    if c:
                        pe.wait_ge(s["w_done"], n * (UNITS - B) + (c - 1) * B + b + 1)
                    elif b == 0:
                        for g in range(4):
                            drained_from_b(pe, n, MERGE + 28 + g)
                    for r in range(R):
                        rhs = w_[:, b, r] if c else v[:, u * R + r]
                        mm = pe.matmul(ring_b[j % 4][:, r * D:(r + 1) * D], U2[:, u * R + r], rhs,
                                       start=True, stop=True)
                    mm.then_inc(s["filled_b"], 1)
                if between:
                    between[0]()
                for b in range(B):
                    u = b * CH + c
                    j = RJ["local", u]
                    free_b(pe, n, j)
                    drained_from_b(pe, n, RJ["solve", u])
                    for r in range(R):
                        mm = pe.matmul(ring_b[j % 4][:, r * D:(r + 1) * D], attn[parity][:, u * R + r], vn[:, b, r],
                                       start=True, stop=True)
                    mm.then_inc(s["filled_b"], 1)
                for b in range(B):
                    u = b * CH + c
                    if c < CH - 1:
                        j = RJ["update", u]
                        free_b(pe, n, j)
                        pe.wait_ge(s["vd_done"], n * (UNITS - B) + c * B + b + 1)
                        pe.matmul(ring_b[j % 4][:, 0:256], khat[parity][:, u], vd[:, b].rearrange("p r d -> p (r d)"),
                                  start=True, stop=True).then_inc(s["filled_b"], 1)
                if len(between) > 1:
                    between[1]()

            def output(n):
                for half in range(2):
                    for k in (2 * half, 2 * half + 1):
                        free_b(pe, n, XTJ[k])
                        pe.wait_ge(s["x_scaled"], n * 4 + k + 1)
                        for i in range(4):
                            mm = pe.transpose(ring_b[XTJ[k] % 4][:, i * P:(i + 1) * P], core[:, 4 * GROUPS[k] + i],
                                              ident[:])
                        mm.then_inc(s["filled_b"], 1)
                    if half == 0:
                        pe.wait_ge(s["wo_loaded"], (n + 1) * 16)
                    for k in (2 * half, 2 * half + 1):
                        g = GROUPS[k]
                        free_b(pe, n, OUTJ[k])
                        drained_from_b(pe, n, XTJ[k])
                        for i in range(2):
                            for r in range(R):
                                mm = pe.matmul(ring_b[OUTJ[k] % 4][:, i * 256:(i + 1) * 256],
                                               xT[:, 4 * g + 2 * i + r], Wo[:, r], start=(r == 0), stop=(r == R - 1))
                        mm.then_inc(s["filled_b"], 1)

            def body(n, parity, more, most):
                pe.wait_ge(s["n_ready"], (n + 1) * 8 + 1)
                pe.wait_ge(s["t0_loaded"], (n + 1) * 16 * NB)
                for step in range(8):
                    if step == 1:
                        pe.wait_ge(s["u0_loaded"], (n + 1) * 16 * NB)
                    for g in range(4):
                        merge_step(n, step, g)
                    if more:
                        for j in {0: (4, 5), 1: (6,), 2: (7,)}.get(step, ()):
                            proj(n + 1, j)
                        if step == 2:
                            by_token(n + 1, TR_QK, 0)
                        if step == 5:
                            back(n + 1, 1 - parity)
                        if step == 6:
                            gram(n + 1, 1 - parity)
                z = [lambda g=g: z_by_token(n, g) for g in range(4)]
                qk = [lambda j=j: proj(n + 2, j) for j in range(4)] if most else []
                recur(n, 0, parity, z[0:2])
                recur(n, 1, parity, z[2:4])
                recur(n, 2, parity, qk[0:1])
                recur(n, 3, parity, qk[1:2])
                for do in qk[2:4]:
                    do()
                output(n)
                if more:
                    by_token(n + 1, TR_V, 4)

            for j in range(8):
                proj(0, j)
            by_token(0, TR_QK, 0)
            back(0, 0)
            gram(0, 0)
            for j in range(4):
                proj(1, j)
            by_token(0, TR_V, 4)
            with pe.Fori(0, (NK - 2) // 2) as pair:
                for parity in range(2):
                    body(pair * 2 + parity, parity, True, True)
            body(NK - 2, 0, True, False)
            body(NK - 1, 1, False, False)

            pe.wait_ge(s["ep_dve"], EP_XN2)
            for q in range(4):
                k, hf = q // 2, q % 2
                for i in range(4):
                    mm = pe.transpose(bank[q][:, i * P:(i + 1) * P], lin_x()[:, hf * 4 + i, k * P:(k + 1) * P],
                                      ident[:])
                mm.then_inc(s["ep_pe"], 1)
            pe.wait_ge(s["ep_dve"], EP_XN2 + 4)
            pe.wait_ge(s["router_loaded"], 16)
            for u in range(UNITS):
                for k in range(KT):
                    mm = pe.matmul(bank[4][:, u * E:(u + 1) * E], xnT[:, k, u * P:(u + 1) * P],
                                   router[:, k, :], start=(k == 0), stop=(k == KT - 1))
            mm.then_inc(s["ep_pe"], 1)

            def gate_up(e, i):
                pe.wait_ge(s[f"f_w_loaded{i}"], (e - i) * 12 + 48)
                for b in range(B):
                    pe.wait_ge(s["f_h"], e * 2 + b + 1)
                    for x_, w in enumerate((w_gate_of[i], w_up_of[i])):
                        for k in range(KT):
                            mm = pe.matmul(bank[2 * b + x_][:], w[:, k], xnT[:, k, b * S:(b + 1) * S],
                                           start=(k == 0), stop=(k == KT - 1))
                    mm.then_inc(s["f_gu"], 1)

            def down(e, i):
                for g in range(4):
                    pe.wait_ge(s["f_h"], e * 2 + g // 2 + 3)
                    pe.wait_ge(s["f_y"], e * 4 + g + 1)
                    for x_ in range(2):
                        u = 2 * g + x_
                        mm = pe.matmul(bank[4 + g][:, x_ * H:(x_ + 1) * H], hT[i % 2][:, u * P:(u + 1) * P],
                                       w_down_of[i], start=True, stop=True)
                    mm.then_inc(s["f_down"], 1)

            gate_up(0, 0)
            with pe.Fori(0, (FT - 2) // 4) as four:
                for i in range(1, 5):
                    gate_up(four * 4 + i, i % 4)
                    down(four * 4 + (i - 1), i - 1)
            gate_up(FT - 1, 1)
            down(FT - 2, 0)
            down(FT - 1, 1)

        @blk.scalar
        def _(a):
            pa = Steps(a, s["pro_act"])
            b3 = bank[4][:].rearrange("p (h x) -> p h x", x=4)
            beta = scal[:, S_BETA].rearrange("p u (k r) -> p (u k) r", r=R)
            a.wait_ge(s["pro_filled"], 6)
            pa.did(a.activation(beta, b3[:, :, 0:2], ACT.Exp, scale=-1.0))
            pa.did(a.activation(U1[:, 1, 0:NV], U1[:, 1, 0:NV], ACT.Exp))
            a.wait_ge(s["pro_dve"], PRO_ABS)
            e_ = T1[:, 8:10, :]
            pa.did(a.activation(e_, e_, ACT.Exp, scale=-1.0))
            pa.wait()
            pa.did(a.activation(e_, e_, ACT.Ln, bias=1.0))
            a.wait_ge(s["pro_filled"], 8)
            a.wait_ge(s["pro_dve"], PRO_G + 2)
            pa.did(a.activation(scal[:, S_EG], scal[:, S_G], ACT.Exp))
            pa.did(a.activation(T1[:, 10:14, :], T1[:, 10:14, :], ACT.Exp))
            assert pa.k == PRO_ACT
            a.wait_ge(s["pro_dve"], PRO_DVE)


            def tap(h, j):
                if j == 0:
                    a.wait_ge(s["taps_qk_ready"], h + 1)
                if j == 4:
                    a.wait_ge(s["taps_v_ready"], h + 1)
                filled_a(a, h, QKJ if j < 4 else VJ, j % 4)
                a.activation(y[:, j], ring_a[j % 4][:], ACT.Copy, scale=tap_of(TAPS - 1, j)
                             ).then_inc(s["tap_done"], 1)

            def half_tanh(h, j):
                drained_from_a(a, h, QKJ if j < 4 else VJ, j % 4)
                a.wait_ge(s["act_done"], h * 8 + (j - 1 if j > 1 else 0) + 1)
                a.activation(th[:, j % 2], y[:, j], ACT.Tanh, scale=0.5).then_inc(s["tanh_done"], 1)

            def z_tanh(h, g, more):
                filled_a(a, h, ZJ, g)
                if g >= 2:
                    drained_from_a(a, h, ZJ, g - 2)
                else:
                    a.wait_ge(s["act_done"], (h + (1 if more else 0)) * 8 + 9)
                a.activation(th[:, g % 2], ring_a[g][:], ACT.Tanh, scale=0.5).then_inc(s["z_tanh"], 1)

            def squares(h):
                for i in range(4):
                    filled_a(a, h, TR_QK, i)
                    a.wait_ge(s["ss_done"], h * 4 + (i - 1 if i > 1 else 0) + 1)
                    a.activation(sq[:, i % 2], ring_a[i][:], ACT.Square).then_inc(s["sq_done"], 1)

            def kq_by_channel(h, parity):
                for g in range(4):
                    filled_a(a, h, BACK, g)
                    a.activation(kqT[parity][:, 2 * g:2 * g + 2].rearrange("p u x i -> p (u x i)"), ring_a[g][:], ACT.Copy
                                 ).then_inc(drained_a[g], 1)

            def v_by_token(h):
                for i in range(4):
                    r, b = i // 2, i % 2
                    filled_a(a, h, TR_V, i)
                    a.activation(v[:].rearrange("p (u r) d -> p u r d", r=R)[:, b * CH:(b + 1) * CH, r, :],
                                 ring_a[i][:].rearrange("p (u d) -> p u d", d=D), ACT.Copy, scale=0.5
                                 ).then_inc(drained_a[i], 1)

            def decays(h):
                a.wait_ge(s["masked"], h + 1)
                a.wait_ge(s["sc_a_ready"], h + 1)
                for m in range(M):
                    t = a.activation(dec[:, m], dec[:, m], ACT.Exp, bias=sc_a[:, S_G, m // R, m % R:m % R + 1])
                t.then_inc(s["exp_done"], 1)

            def merge(n, step):
                for g in range(4):
                    ms = slice(4 * g, 4 * g + 4)
                    filled_b(a, n, MERGE + 4 * step + g)
                    whole = ring_b[g][:].rearrange("p (m i) -> p m i", m=4)
                    left = ring_b[g][:, 0:256].rearrange("p (m i) -> p m i", m=4)
                    dst, src = {0: (Xm[:, ms], whole), 3: (Xm[:, ms], whole), 2: (T1[:, ms], whole),
                                5: (T1[0:64, ms, 0:64], whole[0:64, :, 0:64]),
                                6: (Xm[64:P, ms, 0:64], left[64:P]),
                                7: (U2[0:64, ms, 64:P], left[0:64])}[step]
                    a.activation(dst, src, ACT.Copy).then_inc(drained_b[g], 1)

            def recur(n, c):
                for b in range(B):
                    u = b * CH + c
                    if c:
                        j = RJ["state", u]
                        a.wait_ge(s["w_done"], n * (UNITS - B) + (c - 1) * B + b + 1)
                        if c > 1:
                            drained_from_b(a, n, RJ["local", u - 1])
                        for r in range(R):
                            t = a.activation(qs[:, b, r], ring_b[j % 4][:, 256 + r * D:256 + (r + 1) * D],
                                             ACT.Copy, scale=sc_b[:, S_EG, u, r:r + 1])
                        t.then_inc(drained_b[j % 4], 1)
                for b in range(B):
                    u = b * CH + c
                    j = RJ["solve", u]
                    if c == 0 and b == 0:
                        a.wait_ge(s["sc_b_ready"], n + 1)
                    if c < CH - 1:
                        a.wait_ge(s["vd_done"], n * (UNITS - B) + c * B + b + 1)
                    else:
                        filled_b(a, n, j)
                    if 0 < c < CH - 1:
                        filled_b(a, n, RJ["local", u - 1])
                    for r in range(R):
                        t = a.activation(vn[:, b, r], ring_b[j % 4][:, r * D:(r + 1) * D], ACT.Copy,
                                         scale=sc_b[:, S_BETA, u, r:r + 1])
                    t.then_inc(drained_b[j % 4], 1)

            def out_squares(n, k):
                g = GROUPS[k]
                a.wait_ge(s["x_gated"], n * 4 + k + 1)
                a.wait_ge(s["ss2_done"], n * 4 + (k - 1 if k > 1 else 0) + 1)
                a.activation(sq[:, k % 2],
                             core[:, 4 * g:4 * g + 4].rearrange("p m d -> p (m d)"), ACT.Square
                             ).then_inc(s["sq2_done"], 1)

            def out_by_channel(n, half):
                for k in (2 * half, 2 * half + 1):
                    g = GROUPS[k]
                    filled_b(a, n, XTJ[k])
                    a.activation(xT[:, 4 * g:4 * g + 4].rearrange("p m d -> p (m d)"), ring_b[XTJ[k] % 4][:],
                                 ACT.Copy, scale=normw[:, 0:1]).then_inc(drained_b[XTJ[k] % 4], 1)

            def body(n, parity, more, most):
                merge(n, 0)
                if more:
                    tap(n + 1, 4)
                    tap(n + 1, 5)
                    half_tanh(n + 1, 4)
                    half_tanh(n + 1, 5)
                    tap(n + 1, 6)
                merge(n, 2)
                if more:
                    tap(n + 1, 7)
                    half_tanh(n + 1, 6)
                    half_tanh(n + 1, 7)
                    squares(n + 1)
                merge(n, 3)
                merge(n, 5)
                if more:
                    kq_by_channel(n + 1, 1 - parity)
                merge(n, 6)
                merge(n, 7)
                recur(n, 0)
                z_tanh(n, 0, more)
                z_tanh(n, 1, more)
                recur(n, 1)
                z_tanh(n, 2, more)
                z_tanh(n, 3, more)
                recur(n, 2)
                if most:
                    tap(n + 2, 0)
                out_squares(n, 0)
                out_squares(n, 1)
                recur(n, 3)
                if most:
                    tap(n + 2, 1)
                    tap(n + 2, 2)
                    tap(n + 2, 3)
                out_squares(n, 2)
                out_squares(n, 3)
                out_by_channel(n, 0)
                if most:
                    half_tanh(n + 2, 0)
                    half_tanh(n + 2, 1)
                out_by_channel(n, 1)
                if most:
                    half_tanh(n + 2, 2)
                    half_tanh(n + 2, 3)
                if more:
                    v_by_token(n + 1)
                if most:
                    decays(n + 2)

            tap(0, 0)
            for j in range(1, 8):
                tap(0, j)
                half_tanh(0, j - 1)
            half_tanh(0, 7)
            decays(0)
            squares(0)
            kq_by_channel(0, 0)
            for j in (0, 2):
                tap(1, j)
                tap(1, j + 1)
                half_tanh(1, j)
                half_tanh(1, j + 1)
            v_by_token(0)
            decays(1)
            with a.Fori(0, (NK - 2) // 2) as pair:
                for parity in range(2):
                    body(pair * 2 + parity, parity, True, True)
            body(NK - 2, 0, True, False)
            body(NK - 1, 1, False, False)

            ea = Steps(a, s["ep_act"])
            a.wait_ge(s["ep_dve"], EP_EXP)
            ea.did(a.activation(probs, logits, ACT.Exp))
            with a.Fori(0, FT) as e:
                for b in range(B):
                    a.wait_ge(s["f_gu"], e * 2 + b + 1)
                    a.activation(thf[:, b], bank[2 * b][:], ACT.Tanh, scale=0.5).then_inc(s["f_tanh"], 1)

        @blk.vector
        def _(d):
            for name in ("act_done", "ss_done", "ss2_done"):
                d.sem_inc(s[name])
            d.sem_inc(s["f_h"], 2)
            d.sem_inc(s["f_y"], 4)
            for q in drained_a:
                d.sem_inc(q, 1 + job_a(0, QKJ, 0) // 4)
            for q in drained_b:
                d.sem_inc(q)
            pr = Steps(d, s["pro_dve"])
            flat8 = lin_x()

            def pool_first():
                d.wait_ge(s["pro_pool"], PRO_POOL + 2)
            d.wait_ge(s["x_loaded"], 16)
            norm(d, pr, X, flat8, pool_first)
            for q in range(4):
                d.wait_ge(s["pro_filled"], q + 1)
                pr.did(d.tensor_copy(xnT[:, q // 2, (q % 2) * 512:(q % 2 + 1) * 512], bank[q][:]))
            d.wait_ge(s["pro_filled"], 5)
            pr.did(d.tensor_copy(convT[:].rearrange("p a t -> p (a t)"), bank[5][:, 0:256]))
            d.wait_ge(s["pro_filled"], 6)
            d.wait_ge(s["pro_act"], 2)
            za = T1[:, 6:8, :]
            za4 = za.rearrange("p a b -> p (a b)").rearrange("p (u k r) -> p u k r", u=UNITS, r=R)
            ain = bank[4][:].rearrange("p (u k x) -> p u k x", u=UNITS, x=4)[:, :, :, 2:4]
            dtb = U1[:, 1, NV:2 * NV].rearrange("p (k r) -> p k r", r=R).unsqueeze(1).to_broadcast([P, UNITS, NK, R])
            pr.did(d.tensor_tensor(za4, ain, dtb, ALU.add))
            pr.wait()
            e_ = T1[:, 8:10, :]
            pr.did(d.scalar_tensor_tensor(e_, za, -1.0, za, ALU.mult, ALU.max))
            d.wait_ge(s["pro_act"], 4)
            pr.did(d.scalar_tensor_tensor(za, za, 0.0, e_, ALU.max, ALU.add))
            beta = scal[:, S_BETA]
            pr.did(d.tensor_scalar(beta, beta, 1.0, None, ALU.add))
            pr.wait()
            pr.did(d.reciprocal(beta, beta))
            g_ = U1[:, 2:4, :].rearrange("p a b -> p (a b)").rearrange("p (u h) -> p u h", u=UNITS)
            pr.did(d.scalar_tensor_tensor(g_, za.rearrange("p a b -> p (a b)").rearrange("p (u h) -> p u h", u=UNITS),
                                          -1.0, U1[:, 1, 0:NV].unsqueeze(1).to_broadcast([P, UNITS, NV]),
                                          ALU.mult, ALU.mult))
            assert pr.k == PRO_G
            d.wait_ge(s["pro_filled"], 8)
            G = scal[:, S_G].rearrange("p u h -> p (u h)")
            pr.did(d.tensor_copy(G, bank[6][:, 0:256]))
            pr.wait()
            gl = T1[:, 10:14, :].rearrange("p a b -> p (a b)")
            d.tensor_copy(gl[:, 0:256], bank[6][:, 256:512])
            pr.did(d.tensor_tensor(gl[:, 256:512], bank[6][:, 256:512], G, ALU.subtract))
            d.tensor_copy(Xm[0:NV, 0:4, :].rearrange("h u i -> h (u i)"), bank[0][0:NV, :])
            d.tensor_copy(Xm[0:NV, 4:8, :].rearrange("h u i -> h (u i)"), bank[1][0:NV, :]
                          ).then_inc(s["gates_ready"], 1)
            d.wait_ge(s["pro_act"], 6)
            pr.did(d.tensor_copy(scal[:, S_EGL].rearrange("p u h -> p (u h)"), gl[:, 0:256]))
            d.tensor_scalar(scal[:, S_NEG], scal[:, S_EG], -1.0, None, ALU.mult)
            d.tensor_scalar(scal[:, S_G], scal[:, S_G], -1.0, None, ALU.mult)
            pr.did(d.tensor_scalar(scal[:, S_NBETA], beta, -1.0, None, ALU.mult))
            pr.did(d.tensor_tensor(scal[:, S_BK].rearrange("p u h -> p (u h)"), gl[:, 256:512],
                                   scal[:, S_BETA].rearrange("p u h -> p (u h)"), ALU.mult))
            assert pr.k == PRO_DVE


            def conv(h, j):
                d.wait_ge(s["tap_done"], h * 8 + j + 1)
                ds = Steps(d, s["conv_step"], h * CONV_STEPS + 2 * j)
                for back in range(1, TAPS):
                    if back > 1:
                        ds.wait()
                    t = d.scalar_tensor_tensor(y[:, j, back:], ring_a[j % 4][:, 0:S - back],
                                               tap_of(TAPS - 1 - back, j), y[:, j, back:], ALU.mult, ALU.add)
                    if back < TAPS - 1:
                        ds.did(t)
                    else:
                        t.then_inc(drained_a[j % 4], 1)

            def silu(h, j):
                d.wait_ge(s["tanh_done"], h * 8 + j + 1)
                d.scalar_tensor_tensor(y[:, j], th[:, j % 2], 1.0, y[:, j], ALU.add, ALU.mult
                                       ).then_inc(s["act_done"], 1)

            def z_gate(h, g):
                d.wait_ge(s["z_tanh"], h * 4 + g + 1)
                d.scalar_tensor_tensor(gz[:, 4 * g:4 * g + 4].rearrange("p m d -> p (m d)"), th[:, g % 2], 1.0,
                                       ring_a[g][:], ALU.add, ALU.mult).then_inc(drained_a[g], 1)

            def square_sums(h):
                for i in range(4):
                    d.wait_ge(s["sq_done"], h * 4 + i + 1)
                    d.tensor_reduce(ss[:, 4 * i:4 * i + 4], sq[:, i % 2].rearrange("p (u d) -> p u d", d=D), AX.X,
                                    ALU.add).then_inc(s["ss_done"], 1)

            def normalise(h, parity):
                d.wait_ge(s["rr_done"], h + 1)
                for i in range(4):
                    dst = (qhat, khat[parity])[i // 2]
                    d.tensor_tensor(dst[:, (i % 2) * CH:(i % 2 + 1) * CH],
                                    ring_a[i][:].rearrange("p (u d) -> p u d", d=D),
                                    rr[:, 4 * i:4 * i + 4].unsqueeze(2).to_broadcast([P, 4, D]), ALU.mult
                                    ).then_inc(drained_a[i], 1)

            def n_of(h):
                d.wait_ge(s["decn_done"], h + 1)
                for g in range(4):
                    filled_a(d, h, GRAM, g)
                    times_decays(g, nmat, decn, 0).then_inc(s["nmat_done"], 1)

            def a_of(h, parity):
                for g in range(4):
                    times_decays(g, attn[parity], dec, 1).then_inc(drained_a[g], 1)

            def times_decays(g, dst, by, which):
                kk = ring_a[g][:].rearrange("p (u x i) -> p u x i", x=2, i=P)
                for i in range(2):
                    ms = slice(4 * g + 2 * i, 4 * g + 2 * i + 2)
                    t = d.tensor_tensor(dst[:, ms], kk[:, i, which, :].unsqueeze(1).to_broadcast([P, R, P]),
                                        by[:, ms], ALU.mult)
                return t

            def invert_blocks(h, lo=1, hi=BLK):
                ds = Steps(d, s["base_step"], h * BASE_STEPS + (2 * lo - 3 if lo > 1 else 0))
                if lo == 1:
                    d.wait_ge(s["raw_loaded"], (h + 1) * 16)
                else:
                    ds.wait()
                for i in range(lo, hi):
                    if i == 1:
                        ds.did(d.tensor_copy(ublk[:, 0:1, 1], nblk[:, 0:1, 1]))
                        ds.wait()
                        continue
                    pv = prod[:, 0:i * i].rearrange("p (c j) -> p c j", c=i)
                    ds.did(d.tensor_tensor(pv, ublk[:, 0:i, 0:i],
                                           nblk[:, 0:i, i].unsqueeze(1).to_broadcast([P, i, i]), ALU.mult))
                    ds.wait()
                    t = d.tensor_reduce(ublk[:, 0:i, i], pv, AX.X, ALU.add)
                    if i < BLK - 1:
                        ds.did(t)
                        if i < hi - 1:
                            ds.wait()
                    else:
                        t.then_inc(s["base_done"], 1)
                if hi == BLK:
                    assert 2 * lo - 3 + ds.k == BASE_STEPS or lo == 1, ds.k
                    d.wait_ge(s["base_done"], h * 2 + 1)
                    d.tensor_copy(tblk[:].rearrange("p i c -> p c i"), ublk[:]).then_inc(s["base_done"], 1)

            def merge(n, step):
                for g in range(4):
                    ms = slice(4 * g, 4 * g + 4)
                    filled_b(d, n, MERGE + 4 * step + g)
                    d.tensor_tensor(U1[:, ms], ring_b[g][:].rearrange("p (m i) -> p m i", m=4),
                                    (U0 if step == 1 else U1)[:, ms], ALU.add).then_inc(drained_b[g], 1)

            def recur(n, c, between):
                for b in range(B):
                    u = b * CH + c
                    if c:
                        j = RJ["state", u]
                        filled_b(d, n, j)
                        for r in range(R):
                            t = d.scalar_tensor_tensor(w_[:, b, r], ring_b[j % 4][:, r * D:(r + 1) * D],
                                                       sc_b[:, S_NEG, u, r:r + 1], v[:, u * R + r],
                                                       ALU.mult, ALU.add)
                        t.then_inc(s["w_done"], 1)
                if c < CH - 1:
                    for b in range(B):
                        u = b * CH + c
                        j = RJ["solve", u]
                        if c == 0 and b == 0:
                            d.wait_ge(s["sc_b_ready"], n + 1)
                        filled_b(d, n, j)
                        d.tensor_tensor(vd[:, b], ring_b[j % 4][:, 0:256].rearrange("p (r d) -> p r d", r=R),
                                        sc_b[:, S_BK, u].unsqueeze(2).to_broadcast([P, R, D]), ALU.mult
                                        ).then_inc(s["vd_done"], 1)
                for do in between:
                    do()
                for b in range(B):
                    u = b * CH + c
                    j = RJ["local", u]
                    filled_b(d, n, j)
                    cu = core[:, u * R:(u + 1) * R].rearrange("p r d -> p (r d)")
                    if c:
                        drained_from_b(d, n, RJ["state", u])
                        t = d.tensor_tensor(cu, ring_b[j % 4][:, 0:256], qs[:, b].rearrange("p r d -> p (r d)"),
                                            ALU.add)
                    else:
                        t = d.tensor_copy(cu, ring_b[j % 4][:, 0:256])
                    t.then_inc(drained_b[j % 4], 1)
                if c < CH - 1:
                    for b in range(B):
                        u = b * CH + c
                        j = RJ["update", u]
                        filled_b(d, n, j)
                        if c:
                            drained_from_b(d, n, RJ["update", u - 1])
                            for r in range(R):
                                t = d.scalar_tensor_tensor(st[:, b, r * D:(r + 1) * D],
                                                           st[:, b, r * D:(r + 1) * D],
                                                           sc_b[:, S_EGL, u, r:r + 1],
                                                           ring_b[j % 4][:, r * D:(r + 1) * D],
                                                           ALU.mult, ALU.add)
                        else:
                            t = d.tensor_copy(st[:, b], ring_b[j % 4][:, 0:256])
                        t.then_inc(drained_b[j % 4], 1)

            def out_sums(n, k):
                g = GROUPS[k]
                d.wait_ge(s["sq2_done"], n * 4 + k + 1)
                d.tensor_reduce(ss_out[:, 4 * g:4 * g + 4],
                                sq[:, k % 2].rearrange("p (m d) -> p m d", d=D), AX.X,
                                ALU.add).then_inc(s["ss2_done"], 1)

            def accumulate(n, half):
                for k in (2 * half, 2 * half + 1):
                    g = GROUPS[k]
                    filled_b(d, n, OUTJ[k])
                    au = acc[:, 2 * g:2 * g + 2].rearrange("p u h -> p (u h)")
                    d.tensor_tensor(au, au, ring_b[OUTJ[k] % 4][:], ALU.add).then_inc(drained_b[OUTJ[k] % 4], 1)

            def body(n, parity, more, most):
                if more:
                    conv(n + 1, 4)
                    conv(n + 1, 5)
                merge(n, 1)
                if more:
                    silu(n + 1, 4)
                    silu(n + 1, 5)
                    conv(n + 1, 6)
                    conv(n + 1, 7)
                    silu(n + 1, 6)
                    silu(n + 1, 7)
                    square_sums(n + 1)
                merge(n, 4)
                if more:
                    normalise(n + 1, 1 - parity)
                    n_of(n + 1)
                    a_of(n + 1, 1 - parity)
                invert = [lambda lo=lo, hi=hi: invert_blocks(n + 1, lo, hi)
                          for lo, hi in ((1, 6), (6, 9), (9, 11), (11, 13), (13, BLK))] if more else [lambda: None] * 5
                recur(n, 0, ())
                z_gate(n, 0)
                z_gate(n, 1)
                recur(n, 1, invert[0:1])
                z_gate(n, 2)
                z_gate(n, 3)
                recur(n, 2, invert[1:2])
                out_sums(n, 0)
                out_sums(n, 1)
                recur(n, 3, invert[2:4])
                invert[4]()
                if most:
                    conv(n + 2, 0)
                out_sums(n, 2)
                out_sums(n, 3)
                if most:
                    conv(n + 2, 1)
                accumulate(n, 0)
                if most:
                    silu(n + 2, 0)
                    silu(n + 2, 1)
                    conv(n + 2, 2)
                    conv(n + 2, 3)
                accumulate(n, 1)
                if most:
                    silu(n + 2, 2)
                    silu(n + 2, 3)

            for j in range(8):
                conv(0, j)
                if j:
                    silu(0, j - 1)
            silu(0, 7)
            square_sums(0)
            normalise(0, 0)
            n_of(0)
            a_of(0, 0)
            conv(1, 0)
            conv(1, 1)
            silu(1, 0)
            silu(1, 1)
            invert_blocks(0)
            conv(1, 2)
            conv(1, 3)
            silu(1, 2)
            silu(1, 3)
            with d.Fori(0, (NK - 2) // 2) as pair:
                for parity in range(2):
                    body(pair * 2 + parity, parity, True, True)
            body(NK - 2, 0, True, False)
            body(NK - 1, 1, False, False)

            ep = Steps(d, s["ep_dve"])
            for g in range(4):
                d.wait_ge(drained_b[g], NK * (JOBS_B // 4) + 1)
            t = d.tensor_copy(comb[:, :, E:FT], ones[:, 0:UNITS * 2].rearrange("p (u e) -> p u e", e=2))
            t.then_inc(s["ep_drained"], 1)
            d.wait_ge(s["ep_drained"], 1)

            def pool_turn(k):
                def wait():
                    d.wait_ge(s["ep_pool"], 2 * k)
                return wait
            norms = []
            norms.append(norm(d, ep, acc[:], acc[:], pool_turn(1)))
            ep.wait()
            d.wait_ge(s["x_loaded"], 32)
            ep.did(d.tensor_tensor(X, X, acc[:], ALU.add))
            ep.wait()
            d.memset(acc[:], 0.0).then_inc(s["acc_cleared"], 1)
            norms.append(norm(d, ep, X, lin_x(), pool_turn(2)))
            assert ep.k == EP_XN2, ep.k
            for q in range(4):
                d.wait_ge(s["ep_pe"], q + 1)
                ep.did(d.tensor_copy(xnT[:, q // 2, (q % 2) * 512:(q % 2 + 1) * 512], bank[q][:]))
            d.wait_ge(s["ep_pe"], 5)
            lg = bank[4][:, 0:UNITS * E].rearrange("p (u e) -> p u e", e=E)

            def row(i):
                return best[:, i].unsqueeze(2).to_broadcast([P, UNITS, E])
            ep.did(d.tensor_reduce(best[:, 0], lg, AX.X, ALU.max))
            ep.wait()
            ep.did(d.tensor_tensor(logits, lg, row(0), ALU.subtract))
            assert ep.k == EP_EXP, ep.k
            d.wait_ge(s["ep_act"], 1)
            ep.did(d.tensor_reduce(best[:, 1], probs, AX.X, ALU.add))
            ep.wait()
            ep.did(d.reciprocal(best[:, 1], best[:, 1]))
            ep.wait()
            ep.did(d.tensor_tensor(probs, probs, row(1), ALU.mult))
            ep.wait()
            src = probs
            for i, pick in enumerate((first, second)):
                ep.did(d.tensor_reduce(best[:, i], src, AX.X, ALU.max))
                ep.wait()
                ep.did(d.tensor_tensor(pick, src, row(i), ALU.is_equal))
                ep.wait()
                ep.did(d.tensor_tensor(pick, pick, rank_w[:].unsqueeze(1).to_broadcast([P, UNITS, E]), ALU.mult))
                ep.wait()
                ep.did(d.tensor_reduce(best[:, 2], pick, AX.X, ALU.max))
                ep.wait()
                ep.did(d.tensor_tensor(pick, pick, row(2), ALU.is_equal))
                ep.wait()
                if i == 0:
                    src = logits
                    ep.did(d.scalar_tensor_tensor(logits, first, -2.0, probs, ALU.mult, ALU.add))
                    ep.wait()
            ep.did(d.tensor_tensor(best[:, 3], best[:, 0], best[:, 1], ALU.add))
            ep.wait()
            ep.did(d.reciprocal(best[:, 3], best[:, 3]))
            ep.did(d.tensor_tensor(first, first, row(0), ALU.mult))
            ep.did(d.tensor_tensor(second, second, row(1), ALU.mult))
            ep.wait()
            ep.did(d.tensor_tensor(first, first, second, ALU.add))
            ep.wait()
            ep.did(d.tensor_tensor(comb[:, :, 0:E], first, row(3), ALU.mult))
            ep.wait()
            ep.did(d.tensor_scalar(comb, comb, 0.5, None, ALU.mult))
            ep.wait()
            assert ep.k == EP_COMB, ep.k
            d.wait_ge(s["acc_cleared"], 1)

            def hidden(e, i):
                for b in range(B):
                    h_ = hT[i % 2][:, b * S:(b + 1) * S]
                    d.wait_ge(s["f_tanh"], e * 2 + b + 1)
                    d.scalar_tensor_tensor(h_, thf[:, b], 1.0, bank[2 * b][:], ALU.add, ALU.mult
                                           ).then_inc(s["f_gated"], 1)
                    d.wait_ge(s["f_gated"], e * 2 + b + 1)
                    d.tensor_tensor(h_, h_, bank[2 * b + 1][:], ALU.mult).then_inc(s["f_h"], 1)

            def weigh(e):
                d.wait_ge(s["f_y"], e * 4 + 4)
                d.tensor_copy(comb_e[:], comb[:, :, bass.ds(e, 1)].rearrange("p u a -> p (u a)")
                              ).then_inc(s["comb_ready"], 1)
                for g in range(4):
                    if g == 0:
                        d.wait_ge(s["comb_ready"], e + 1)
                    d.wait_ge(s["f_down"], e * 4 + g + 1)
                    for x_ in range(2):
                        u = 2 * g + x_
                        t = d.scalar_tensor_tensor(acc[:, u], bank[4 + g][:, x_ * H:(x_ + 1) * H],
                                                   comb_e[:, u:u + 1], acc[:, u], ALU.mult, ALU.add)
                    t.then_inc(s["f_y"], 1)

            hidden(0, 0)
            with d.Fori(0, (FT - 2) // 2) as pair:
                hidden(pair * 2 + 1, 1)
                weigh(pair * 2)
                hidden(pair * 2 + 2, 0)
                weigh(pair * 2 + 1)
            hidden(FT - 1, 1)
            weigh(FT - 2)
            weigh(FT - 1)
            d.wait_ge(s["f_y"], 4 * FT + 4)
            norms.append(norm(d, ep, acc[:], acc[:], pool_turn(3)))
            ep.wait()
            d.tensor_tensor(X, X, acc[:], ALU.add).then_inc(s["layer_done"], 1)
            assert tuple(norms) == EP_NORMS, norms


_INS = ["L0_attn_hidden_states", "L0_attn_W_qkvz", "L0_attn_W_ba", "L0_attn_conv_weight", "L0_attn_A_log",
        "L0_attn_dt_bias", "L0_attn_norm_weight", "L0_attn_W_out", "L0_ffn_router_w", "L0_ffn_w_gate",
        "L0_ffn_w_up", "L0_ffn_w_down", "L0_ffn_sw_gate", "L0_ffn_sw_up", "L0_ffn_sw_down"]


def kernel(**inputs):
    import numpy as np
    import concourse.bacc as bacc
    from concourse.bass_utils import run_bass_kernel_spmd

    nc = bacc.Bacc("TRN2", target_bir_lowering=False, num_devices=1)
    arrays, args = {}, []
    for name in _INS:
        a = np.ascontiguousarray(inputs[name])
        arrays[name + "_dram"] = a
        args.append(nc.dram_tensor(name + "_dram", a.shape, mybir.dt.from_np(a.dtype), kind="ExternalInput").ap())
    args.append(nc.dram_tensor("out_dram", (B, S, H), F32, kind="ExternalOutput").ap())
    args.append(nc.dram_tensor("decay_rows", (NV, UNITS * P), F32, kind="Internal").ap())
    args.append(nc.dram_tensor("raw_blocks", (NB, M, BLK, BLK), F32, kind="Internal").ap())
    args.append(nc.dram_tensor("inv_blocks", (2, NB, M, BLK, BLK), F32, kind="Internal").ap())
    build(nc, *args)
    r = run_bass_kernel_spmd(nc, [arrays], core_ids=[0])
    return r.results[0]["out_dram"]
```
